# Optimizing a Trainium2 kernel written in Bass

```python
import numpy as np
import jax
import jax.numpy as jnp

def _softmax(x, axis=-1):
    return jax.nn.softmax(x, axis=axis)

def _gelu(x):
    return jax.nn.gelu(x, approximate=True)

def _silu(x):
    return jax.nn.silu(x)

def _sigmoid(x):
    return jax.nn.sigmoid(x)

def _layernorm(x, axis=-1, eps=1e-05):
    m = jnp.mean(x, axis=axis, keepdims=True)
    v = jnp.var(x, axis=axis, keepdims=True)
    return (x - m) / jnp.sqrt(v + eps)

def _scatter_add(tgt, idx, src, axis=0):
    return tgt.at[idx].add(src)

def _segment_sum(src, seg, n):
    return jax.ops.segment_sum(src, seg, n)
kernel_name = 'mk_flamingo_gated_d1_seqx_r2_e673a0'

def setup_inputs(seed: int=0):
    np.random.seed(seed)
    _w = jnp.asarray

    def _rec_inputs():
        import jax
        import jax.numpy as jnp
        _rk = jax.random.key(seed)
        x = -0.0002928 + 1 * jax.random.normal(jax.random.fold_in(_rk, 1), (2, 2048, 512), jnp.float32)
        _lenS = 2048 - jax.random.randint(jax.random.fold_in(_rk, 7), (2,), 0, max(1, 2048 // 4) + 1, jnp.int32)
        _lenS2 = 128 - jax.random.randint(jax.random.fold_in(_rk, 8), (2,), 0, max(1, 128 // 4) + 1, jnp.int32)
        _ctx_1024P = jax.random.normal(jax.random.fold_in(_rk, 11), (2, 16, 512), jnp.float32)
        _ctx_1024c = jax.random.dirichlet(jax.random.fold_in(_rk, 511), 0.3 * jnp.ones((16,), jnp.float32), (2, 128))
        _ctx_1024t = jnp.einsum('bsk,bkd->bsd', _ctx_1024c, _ctx_1024P)
        _ctx_1024t = _ctx_1024t * jax.lax.rsqrt(jnp.mean(jnp.square(_ctx_1024t)) + 1e-12) * 0.953939
        ctx_1024 = 2.81802e-05 + 1.00001 * (_ctx_1024t + 0.3 * jax.random.normal(jax.random.fold_in(_rk, 611), (2, 128, 512), jnp.float32))
        _validS = jnp.arange(2048)[None, :] < _lenS[:, None]
        _validS2 = jnp.arange(128)[None, :] < _lenS2[:, None]
        _causal = jnp.tril(jnp.ones((2048, 2048), dtype=bool))
        mask_BxS2_bk0 = jnp.logical_not(jnp.broadcast_to(_validS2[:, :], (2, 128)))
        _g = jax.random.normal(jax.random.fold_in(_rk, 9001), (2, 1), jnp.float32)
        _g = jnp.sign(_g) * jnp.maximum(jnp.abs(_g), 1.0) + (_g == 0) * 1.0
        g_xattn = _g[0]
        g_ffn = _g[1]
        return (x, ctx_1024, mask_BxS2_bk0, g_xattn, g_ffn)
    x, ctx_1024, mask_BxS2_bk0, g_xattn, g_ffn = _rec_inputs()

    def _L0_xattn_setup():
        import jax, jax.numpy as jnp
        import numpy as np
        NUM_HEADS, NUM_KV, HEAD_DIM, WIDTH = (4, 1, 128, 512)
        MASK_FILL = -2.3819763e+38

        def _apply_rope(x, positions, max_wavelength=10000.0):
            d = x.shape[-1]
            freq_exp = 2.0 / d * jnp.arange(d // 2, dtype=jnp.float32)
            timescale = max_wavelength ** freq_exp
            radians = positions[..., None].astype(jnp.float32) / timescale
            radians = radians[..., None, :]
            sin, cos = (jnp.sin(radians), jnp.cos(radians))
            x1, x2 = jnp.split(x, 2, axis=-1)
            out = jnp.concatenate([x1 * cos - x2 * sin, x2 * cos + x1 * sin], axis=-1)
            return out.astype(x.dtype)

        def _rmsnorm(x, scale):
            var = jnp.mean(jnp.square(x.astype(jnp.float32)), axis=-1, keepdims=True)
            normed = x * jax.lax.rsqrt(var + 1e-06)
            return (normed * (1 + scale)).astype(x.dtype)
        key = jax.random.key(seed)
        ks = jax.random.split(key, 7)
        B, T, S = (8, 256, 1024)
        return {'x': jax.random.normal(ks[0], (B, T, WIDTH), jnp.float32), 'mem_seq': jax.random.normal(ks[1], (B, S, WIDTH), jnp.float32), 'mem_mask': jax.random.randint(ks[2], (B, S), 0, 2).astype(bool), 'rms_scale': jax.random.normal(ks[3], (WIDTH,), jnp.float32) * 0.02, 'q_w': jax.random.normal(ks[4], (NUM_HEADS, WIDTH, HEAD_DIM), jnp.float32) / np.sqrt(WIDTH), 'kv_w': jax.random.normal(ks[5], (2, NUM_KV, WIDTH, HEAD_DIM), jnp.float32) / np.sqrt(WIDTH), 'out_w': jax.random.normal(ks[6], (NUM_HEADS, HEAD_DIM, WIDTH), jnp.float32) / np.sqrt(NUM_HEADS * HEAD_DIM)}
    _L0_xattn_all = _L0_xattn_setup()
    _L0_xattn_in = {k: v for k, v in _L0_xattn_all.items() if k in ('rms_scale', 'q_w', 'kv_w', 'out_w')}
    del _L0_xattn_all

    def _L0_ffn_setup():
        import jax, jax.numpy as jnp
        import numpy as np
        BLOCK = 32
        W_BITS = 4
        ACT_BITS = 16

        def act_qdq(x):
            qmax = 2.0 ** (ACT_BITS - 1) - 1.0
            scale = jnp.maximum(jnp.max(jnp.abs(x)) / qmax, 1e-12)
            return jnp.clip(jnp.round(x / scale), -qmax - 1.0, qmax) * scale

        def fixed_qdq_u16(x):
            scale = 1.0 / 65536.0
            return jnp.clip(jnp.round(x / scale), 0.0, 65535.0) * scale

        def lpbq_dequant(w):
            O, I = w.shape
            qmax = 2.0 ** (W_BITS - 1) - 1.0
            wb = w.reshape(O, I // BLOCK, BLOCK)
            s = jnp.maximum(jnp.max(jnp.abs(wb), axis=-1, keepdims=True) / qmax, 1e-12)
            wq = jnp.clip(jnp.round(wb / s), -qmax - 1.0, qmax) * s
            return wq.reshape(O, I)
        key = jax.random.key(seed)
        k1, k2, k3, k4 = jax.random.split(key, 4)
        B, S, H, I = (2, 2048, 512, 1536)
        x = jax.random.normal(k1, (B, S, H), jnp.float32)
        w_gate = jax.random.normal(k2, (I, H), jnp.float32) * 0.02
        w_up = jax.random.normal(k3, (I, H), jnp.float32) * 0.02
        w_down = jax.random.normal(k4, (H, I), jnp.float32) * 0.02
        return {'x': x, 'w_gate': w_gate, 'w_up': w_up, 'w_down': w_down}
    _L0_ffn_all = _L0_ffn_setup()
    _L0_ffn_in = {k: v for k, v in _L0_ffn_all.items() if k in ('w_gate', 'w_up', 'w_down')}
    del _L0_ffn_all
    return {'x': x, 'ctx_1024': ctx_1024, 'mask_BxS2_bk0': mask_BxS2_bk0, 'g_xattn': g_xattn, 'g_ffn': g_ffn, 'L0_xattn_rms_scale': _L0_xattn_in['rms_scale'], 'L0_xattn_q_w': _L0_xattn_in['q_w'], 'L0_xattn_kv_w': _L0_xattn_in['kv_w'], 'L0_xattn_out_w': _L0_xattn_in['out_w'], 'L0_ffn_w_gate': _L0_ffn_in['w_gate'], 'L0_ffn_w_up': _L0_ffn_in['w_up'], 'L0_ffn_w_down': _L0_ffn_in['w_down']}

def reference(x, ctx_1024, mask_BxS2_bk0, g_xattn, g_ffn, L0_xattn_rms_scale, L0_xattn_q_w, L0_xattn_kv_w, L0_xattn_out_w, L0_ffn_w_gate, L0_ffn_w_up, L0_ffn_w_down):
    import jax
    import jax.numpy as jnp

    def _L0_xattn_ref(x, mem_seq, mem_mask, rms_scale, q_w, kv_w, out_w):
        import jax, jax.numpy as jnp
        import numpy as np
        NUM_HEADS, NUM_KV, HEAD_DIM, WIDTH = (4, 1, 128, 512)
        MASK_FILL = -2.3819763e+38

        def _apply_rope(x, positions, max_wavelength=10000.0):
            d = x.shape[-1]
            freq_exp = 2.0 / d * jnp.arange(d // 2, dtype=jnp.float32)
            timescale = max_wavelength ** freq_exp
            radians = positions[..., None].astype(jnp.float32) / timescale
            radians = radians[..., None, :]
            sin, cos = (jnp.sin(radians), jnp.cos(radians))
            x1, x2 = jnp.split(x, 2, axis=-1)
            out = jnp.concatenate([x1 * cos - x2 * sin, x2 * cos + x1 * sin], axis=-1)
            return out.astype(x.dtype)

        def _rmsnorm(x, scale):
            var = jnp.mean(jnp.square(x.astype(jnp.float32)), axis=-1, keepdims=True)
            normed = x * jax.lax.rsqrt(var + 1e-06)
            return (normed * (1 + scale)).astype(x.dtype)
        B, S, _ = mem_seq.shape
        T = x.shape[1]
        G = NUM_HEADS // NUM_KV
        xn = _rmsnorm(x, rms_scale)
        mn = _rmsnorm(mem_seq, rms_scale)
        q = jnp.einsum('BTD,NDH->BTNH', xn, q_w)
        kv = jnp.einsum('BSD,cKDH->cBSKH', mn, kv_w)
        k, v = (kv[0], kv[1])
        q_pos = jnp.broadcast_to(jnp.arange(S, T + S), (B, T))
        k_pos = jnp.broadcast_to(jnp.arange(S), (B, S))
        q = _apply_rope(q, q_pos) * HEAD_DIM ** (-0.5)
        k = _apply_rope(k, k_pos)
        q = q.reshape(B, T, NUM_KV, G, HEAD_DIM)
        logits = jnp.einsum('BTKGH,BSKH->BKGTS', q, k, preferred_element_type=jnp.float32)
        masked = jnp.where(mem_mask[:, None, None, None, :], logits, MASK_FILL)
        probs = jax.nn.softmax(masked, axis=-1).astype(x.dtype)
        enc = jnp.einsum('BKGTS,BSKH->BTKGH', probs, v).reshape(B, T, NUM_HEADS, HEAD_DIM)
        return jnp.einsum('BTNH,NHD->BTD', enc, out_w)

    def _L0_ffn_ref(x, w_gate, w_up, w_down):
        import jax, jax.numpy as jnp
        import numpy as np
        BLOCK = 32
        W_BITS = 4
        ACT_BITS = 16

        def act_qdq(x):
            qmax = 2.0 ** (ACT_BITS - 1) - 1.0
            scale = jnp.maximum(jnp.max(jnp.abs(x)) / qmax, 1e-12)
            return jnp.clip(jnp.round(x / scale), -qmax - 1.0, qmax) * scale

        def fixed_qdq_u16(x):
            scale = 1.0 / 65536.0
            return jnp.clip(jnp.round(x / scale), 0.0, 65535.0) * scale

        def lpbq_dequant(w):
            O, I = w.shape
            qmax = 2.0 ** (W_BITS - 1) - 1.0
            wb = w.reshape(O, I // BLOCK, BLOCK)
            s = jnp.maximum(jnp.max(jnp.abs(wb), axis=-1, keepdims=True) / qmax, 1e-12)
            wq = jnp.clip(jnp.round(wb / s), -qmax - 1.0, qmax) * s
            return wq.reshape(O, I)
        x = act_qdq(x)
        up = act_qdq(x @ lpbq_dequant(w_up).T)
        gate = act_qdq(x @ lpbq_dequant(w_gate).T)
        sig = fixed_qdq_u16(jax.nn.sigmoid(gate))
        gate = act_qdq(gate * sig)
        o = act_qdq(gate * up)
        return o @ lpbq_dequant(w_down).T
    x = x + jnp.tanh(g_xattn[0]) * _L0_xattn_ref(_layernorm(x, axis=-1), ctx_1024, mask_BxS2_bk0, L0_xattn_rms_scale, L0_xattn_q_w, L0_xattn_kv_w, L0_xattn_out_w)
    x = x + jnp.tanh(g_ffn[0]) * _L0_ffn_ref(_layernorm(x, axis=-1), L0_ffn_w_gate, L0_ffn_w_up, L0_ffn_w_down)
    return x

_drawn_inputs = setup_inputs


def setup_inputs(seed=0):
    import zlib

    import numpy as np

    out = dict(_drawn_inputs(seed))
    spreads = {}
    factors = {'L0_xattn_rms_scale': 6.301}
    for name, (base, spread) in spreads.items():
        noise = np.random.default_rng([zlib.crc32(name.encode()), seed]).standard_normal(out[name].shape)
        drawn = base * np.exp(spread * noise) if base else spread * noise
        out[name] = jnp.asarray(drawn.astype(out[name].dtype))
    for name, factor in factors.items():
        out[name] = (out[name] * factor).astype(out[name].dtype)
    return out
```

```python
import concourse.bass as bass
from concourse import mybir
from contextlib import ExitStack

P = 128
BATCH, SEQ, D = 2, 2048, 512
CTX, NH, HD = 128, 4, 128
FF = 1536
BLOCK = 32
KD = D // P
OT = FF // P
TILES = BATCH * SEQ // P
CHUNK = 512
TPC = CHUNK // P
CHUNKS = TILES // TPC
PAIR = 2 * CHUNK
UPC = OT // 2
UNITS = CHUNKS * UPC
QMAX = 32767.0
QMAX4 = 7.0
TINY = 1e-12
MASK_FILL = -2.3819763e38
LEAD = 8
KB = 1024


def at(n):
    return n + 1 + LEAD


def flamingo_kernel(nc, x, ctx_in, mask, g_xattn, g_ffn, rms_scale, q_w, kv_w, out_w, w_gate, w_up, w_down,
                    rope_q, rope_k, out):
    F32, F16, I16, U16, I32, U8 = (mybir.dt.float32, mybir.dt.float16, mybir.dt.int16, mybir.dt.uint16,
                                   mybir.dt.int32, mybir.dt.uint8)
    ALU, ACT, AX = mybir.AluOpType, mybir.ActivationFunctionType, mybir.AxisListType
    SIZE = {F32: 4, F16: 2, I16: 2, U16: 2, I32: 4, U8: 1}

    h_dram = nc.dram_tensor("h_scratch", (CHUNKS, P, TPC, D), F32, kind="Internal").ap()
    g_dram = nc.dram_tensor("gate_scratch", (UNITS, P, PAIR), F32, kind="Internal").ap()
    u_dram = nc.dram_tensor("up_scratch", (UNITS, P, PAIR), F32, kind="Internal").ap()
    wg_dram = nc.dram_tensor("w_gate_parts", (OT, P, 2, KD, P), F16, kind="Internal").ap()
    wu_dram = nc.dram_tensor("w_up_parts", (OT, P, 2, KD, P), F16, kind="Internal").ap()
    wd_dram = nc.dram_tensor("w_down_parts", (OT, P, 2, D), F16, kind="Internal").ap()

    es = ExitStack()
    with es:
        arena = es.enter_context(nc.sbuf_tensor("arena", [P, 207 * KB // 4], F32))
        banks = [es.enter_context(nc.psum_tensor(f"bank{i}", [P, 512], F32)) for i in range(8)]

        def sem(name):
            return es.enter_context(nc.semaphore(name))

        def view(at_byte, shape, dt):
            n = SIZE[dt]
            for s in shape:
                n *= s
            assert at_byte % 4 == 0 and n % 4 == 0 and at_byte + n <= 207 * KB, (at_byte, shape)
            v = arena[:, at_byte // 4:(at_byte + n) // 4]
            if dt != F32:
                v = v.bitcast(dt)
            if len(shape) > 1:
                names = "abcde"[:len(shape)]
                v = v.rearrange(f"p ({' '.join(names)}) -> p {' '.join(names)}",
                                **{c: s for c, s in zip(names[1:], shape[1:])})
            return v

        H = view(0, [TILES, D], F32)
        class Small:
            top = 204 * KB
            end = 207 * KB

        def small(shape, dt=F32):
            n = SIZE[dt]
            for s in shape:
                n *= s
            if n % 4:
                v = view(Small.top, [2], dt)[:, 0:1]
                n = 4
            else:
                v = view(Small.top, shape, dt)
            Small.top += n
            assert Small.top <= Small.end
            return v

        ident = small([P])
        ident16 = small([P], F16)
        gates = small([2])
        w_row, w_all = small([3]), small([3])
        w_pow, w_scale, w_undo = small([3]), small([3]), small([3])
        x_row, x_all = small([1]), small([1])
        g_row, g_all = small([2]), small([2])
        gg_row, gg_all = small([1]), small([1])
        u_row, u_all = small([1]), small([1])
        p_row, p_all = small([1]), small([1])
        s_x, s_g, s_gg, s_u, s_p = (small([1]) for _ in range(5))
        i_x, i_g, i_gg, i_u, i_p = (small([1]) for _ in range(5))
        d_g, d_u = small([1]), small([1])
        c_g, c_u, c_gg, c_p, c_out = (small([1]) for _ in range(5))
        tmp1 = small([4])
        g_peak, u_peak, g_top = (small([UNITS]) for _ in range(3))
        top_i, top_sq = small([1], I16), small([1], U16)
        top_sig, top_g = small([1]), small([1])
        gg_acc, gg_run = small([2 * UPC]), small([2 * UPC])
        p_acc, p_peak = small([2]), small([UNITS])
        WRAW = view(72 * KB, [3, OT, D], F32)
        W_Q = view(160 * KB, [3, D], I16)
        W_F = view(163 * KB, [3, D], F32)
        W_HI = view(169 * KB, [3, D], F16)
        W_LO = view(172 * KB, [3, D], F16)
        W_T = view(175 * KB, [3, 2, KD, P], F16)
        W_BMAX = view(186 * KB, [3 * OT, D // BLOCK], F32)
        W_RECIP = view(186 * KB + 2304, [3 * OT, D // BLOCK], F32)
        W_BSCALE = view(186 * KB + 4608, [3 * OT, D // BLOCK], F32)
        STATS = 64 * KB
        BN_X = view(STATS, [TILES, 6], F32)
        BN_H = view(STATS + 768, [TILES, 6], F32)
        st = [view(STATS + 1536 + 128 * i, [TILES], F32) for i in range(20)]
        mean_x, var_x, r_x, ra, rb, rc, rd, hmax, hmin, mean_h, var_h, r_h, c_h, re_, rf = st[:15]
        bn_c = view(STATS + 1536 + 2560, [BATCH, 6], F32)
        QC = view(72 * KB, [2, NH, CHUNK], F32)
        QS = view(88 * KB, [2, NH, CHUNK], F32)
        XTC = view(104 * KB, [KD, CHUNK], F32)
        XN = view(112 * KB, [TPC, D], F32)
        VW = view(120 * KB, [BATCH, NH, D], F32)
        SC = view(160 * KB, [2, NH, CTX], F32)
        EX = view(164 * KB, [2, NH, CTX], F32)
        PT = view(168 * KB, [2, NH, P], F32)
        QW = view(172 * KB, [KD, NH, HD], F32)
        KT1 = view(180 * KB, [BATCH, CTX], F32)
        KT2 = view(181 * KB, [BATCH, CTX], F32)
        KVW = view(182 * KB, [2, KD, HD], F32)
        OW = view(186 * KB, [NH, D], F32)
        TAB = view(186 * KB, [2, 2, CHUNK], F32)
        CX = view(194 * KB, [BATCH, D], F32)
        CXT = view(198 * KB, [KD, CTX], F32)
        VT = view(200 * KB, [CTX], F32)
        KN = view(200 * KB + 512, [CTX], F32)
        KR = view(201 * KB, [CTX], F32)
        KR2 = view(201 * KB + 512, [CTX], F32)
        KM = view(202 * KB, [2, HD // 2], F32)
        RK = view(202 * KB + 512, [2, HD // 2], F32)
        MB = view(203 * KB, [BATCH, CTX], F32)
        a0 = STATS + 1536 + 2560 + 64
        MU8 = view(a0, [BATCH, CTX], U8)
        RMS = view(a0 + 256, [KD], F32)
        st_c = [view(a0 + 288 + 8 * i, [BATCH], F32) for i in range(6)]
        NMX = view(a0 + 352, [2, NH], F32)
        RSUM = view(a0 + 384, [2, NH], F32)
        RINV = view(a0 + 416, [2, NH], F32)
        XT = view(72 * KB, [CHUNKS, 2, KD, CHUNK], F16)
        G = view(0, [UNITS, PAIR], I16)
        W = view(136 * KB, [OT, 2, KD, P], F16)
        STG = view(160 * KB, [3, 2, CHUNK], F32)
        XI = view(172 * KB, [TPC, D], I16)
        XH = view(176 * KB, [TPC, D], F16)
        XL = view(180 * KB, [TPC, D], F16)
        GB = view(172 * KB, [6, PAIR], F32)
        SQ = view(196 * KB, [2, PAIR], U16)
        GQ = view(200 * KB, [2, PAIR], I16)
        LU = view(96 * KB, [UPC, PAIR], F32)
        UR = view(172 * KB, [6, PAIR], F32)
        UA = view(196 * KB, [3, PAIR], I16)
        AB = view(128 * KB, [3, PAIR], I16)
        OH = view(96 * KB, [2, OT, CHUNK], F16)
        OL = view(120 * KB, [2, OT, CHUNK], F16)
        WD = view(144 * KB, [OT, 2, D], F16)
        UB = view(168 * KB, [3, PAIR], F32)
        HB = view(180 * KB, [2, TPC, D], F32)
        UI = view(196 * KB, [2, PAIR], I16)
        OI = view(200 * KB, [2, PAIR], I16)

        def col(v, n):
            return v[:, bass.ds(n, 1)]

        bank16 = [b[:, :].bitcast(F16).rearrange("p (a k c) -> p a k c", a=2, k=KD) for b in banks]
        bank4 = [b[:, :].rearrange("p (a c) -> p a c", a=4) for b in banks]
        TB, QB, LB, PB, OB = (0, 1), (2, 3), (4, 5), 6, 7
        XB = (6, 7)
        MM = 6

        ld_w, ld_small, ld_attn, ld_wd, ld_wg = (sem(n) for n in
                                                 ("ld_w", "ld_small", "ld_attn", "ld_wd", "ld_wg"))
        ld_x = [sem(f"ld_x{c}") for c in range(CHUNKS)]
        ld_tab = [sem(f"ld_tab{i}") for i in range(2)]
        ld_wu = [sem(f"ld_wu{i}") for i in range(3)]
        ld_gb = [sem(f"ld_gb{i}") for i in range(6)]
        ld_ur = [sem(f"ld_ur{i}") for i in range(6)]
        ld_ub = [sem(f"ld_ub{i}") for i in range(3)]
        ld_hb = [sem(f"ld_hb{i}") for i in range(2)]
        st_wt = [sem(f"st_wt{i}") for i in range(3)]
        st_h, st_lu = sem("st_h"), sem("st_lu")
        st_stg = [sem(f"st_stg{i}") for i in range(3)]
        st_out = [sem(f"st_out{i}") for i in range(2)]
        idents = sem("idents")
        steps = sem("vector_steps")
        asteps = sem("scalar_steps")
        psteps = sem("tensor_steps")
        peaks = sem("peaks_over_partitions")
        counted = {}

        def event(name):
            counted[name] = sem(name)
            return counted[name]

        wq_ready, ws_ready, whi_ready, wlo_ready, wtrans, wt_ready = (event(n) for n in (
            "wq_ready", "ws_ready", "whi_ready", "wlo_ready", "w_transposed", "wt_ready"))
        xn_ready, xn_trans, xtc_ready, q_ready, roped = (event(n) for n in (
            "xn_ready", "xn_transposed", "xtc_ready", "q_ready", "roped"))
        scores_ready, masked, max_ready, exp_ready, inv_ready, probs_ready = (event(n) for n in (
            "scores_ready", "masked", "max_ready", "exp_ready", "inv_ready", "probs_ready"))
        probs_trans, pt_ready, attn_ready, h_ready, h_stats = (event(n) for n in (
            "probs_transposed", "pt_ready", "attn_ready", "h_ready", "h_stats"))
        xi_ready, xh_ready, xl_ready, x_trans, xt_ready = (event(n) for n in (
            "xi_ready", "xh_ready", "xl_ready", "x_transposed", "xt_ready"))
        mm_ready, stg_ready, stg_peaked = (event(n) for n in ("mm_ready", "stg_ready", "stg_peaked"))
        gi_ready, sig_ready, sq_ready, g_kept, gg_peaked, gg_folded = (event(n) for n in (
            "gi_ready", "sig_ready", "sq_ready", "g_kept", "gg_peaked", "gg_folded"))
        sig2_ready, sq2_ready, gg_ready = (event(n) for n in ("sig2_ready", "sq2_ready", "gg_ready"))
        ua_ready, pab_ready, pab2_ready, p_peaked, p_folded = (event(n) for n in (
            "ua_ready", "pab_ready", "pab2_ready", "p_peaked", "p_folded"))
        ui_ready, oi_ready, oh_ready, ol_ready, down_ready, y_ready = (event(n) for n in (
            "ui_ready", "oi_ready", "oh_ready", "ol_ready", "down_ready", "y_ready"))

        block = es.enter_context(nc.Block())
        marks = {}

        w_src = [w_gate.rearrange("(t p) d -> p t d", p=P), w_up.rearrange("(t p) d -> p t d", p=P),
                 w_down.rearrange("(r p) (s d) -> p r s d", p=P, d=D)]
        x_src = x.rearrange("b (c t p) d -> (b c) p t d", p=P, t=TPC)
        out_dst = out.rearrange("b (c t p) d -> (b c) p t d", p=P, t=TPC)

        @block.vector
        def _(dve):
            for name, s in counted.items():
                if name in DVE_EVENTS:
                    dve.sem_inc(s, LEAD)
            n_steps = [0]

            def step(ins, mark=None):
                n_steps[0] += 1
                ins.then_inc(steps, 1)
                dve.wait_ge(steps, n_steps[0])
                if mark:
                    marks[mark] = n_steps[0]

            def rsqrt(y, a, root, t, mark, act_step):
                marks[mark] = n_steps[0]
                dve.wait_ge(asteps, act_step)
                step(nc.vector.reciprocal(y, root))
                step(nc.vector.tensor_tensor(t, y, y, ALU.mult))
                step(nc.vector.tensor_tensor(t, t, a, ALU.mult))
                step(nc.vector.tensor_scalar(t, t, -0.5, 1.5, ALU.mult, ALU.add))
                step(nc.vector.tensor_tensor(y, y, t, ALU.mult))

            def moments(bn, mean, var, a, b):
                step(nc.vector.tensor_tensor(a, bn[:, :, 1], bn[:, :, 4], ALU.add))
                step(nc.vector.tensor_scalar(mean, a, 0.5, None, ALU.mult))
                step(nc.vector.tensor_tensor(a, bn[:, :, 1], bn[:, :, 4], ALU.subtract))
                step(nc.vector.tensor_tensor(a, a, a, ALU.mult))
                step(nc.vector.tensor_tensor(b, bn[:, :, 2], bn[:, :, 5], ALU.add))
                step(nc.vector.tensor_scalar(b, b, 1.0 / D, None, ALU.mult))
                step(nc.vector.scalar_tensor_tensor(var, a, 0.25, b, ALU.mult, ALU.add))

            def scale_of(s, inv, peak, qmax):
                step(nc.vector.tensor_scalar(s, peak, 1.0 / qmax, TINY, ALU.mult, ALU.max))
                step(nc.vector.reciprocal(inv, s))

            for m in range(3):
                dve.wait_ge(ld_w, 48)
                step(nc.vector.tensor_reduce(
                    W_BMAX[:, m * OT:(m + 1) * OT, :].rearrange("p t b -> p (t b)"),
                    WRAW[:, m].rearrange("p t (b e) -> p (t b) e", e=BLOCK), axis=AX.X, op=ALU.max,
                    apply_absolute_value=True))
                step(nc.vector.tensor_reduce(w_row[:, m:m + 1], W_BMAX[:, m * OT:(m + 1) * OT, :],
                                             axis=AX.XY, op=ALU.max))
            marks["w_row"] = n_steps[0]
            step(nc.vector.tensor_scalar(W_BSCALE, W_BMAX, 1.0 / QMAX4, TINY, ALU.mult, ALU.max))
            step(nc.vector.reciprocal(W_RECIP, W_BSCALE))
            dve.wait_ge(peaks, 1)
            step(nc.vector.tensor_scalar(w_pow, w_all, 1e-30, None, ALU.max))
            step(nc.vector.tensor_scalar(w_pow.bitcast(I32), w_pow.bitcast(I32), 0x7F800000, None,
                                         ALU.bitwise_and))
            step(nc.vector.reciprocal(w_scale, w_pow))
            step(nc.vector.tensor_scalar(w_scale, w_scale, 16384.0, None, ALU.mult))
            step(nc.vector.tensor_scalar(w_undo, w_pow, 1.0 / 16384.0, None, ALU.mult))
            for m in range(3):
                step(nc.vector.tensor_scalar(W_BSCALE[:, m * OT:(m + 1) * OT, :], W_BSCALE[:, m * OT:(m + 1) * OT, :],
                                             w_scale[:, m:m + 1], None, ALU.mult))

            def by_block(v):
                return v.rearrange("p (b e) -> p b e", e=BLOCK)

            for m in range(3):
                with dve.Fori(0, OT // 3) as j:
                    for s in range(3):
                        t = j * 3 + s
                        n = t + m * OT
                        recip = W_RECIP[:, n, :].unsqueeze(2).broadcast_to([P, D // BLOCK, BLOCK])
                        scale = W_BSCALE[:, n, :].unsqueeze(2).broadcast_to([P, D // BLOCK, BLOCK])
                        nc.vector.tensor_tensor(by_block(W_Q[:, s]), by_block(WRAW[:, m, t, :]), recip,
                                                ALU.mult).then_inc(wq_ready, 1)
                        dve.wait_ge(wq_ready, at(n))
                        nc.vector.tensor_tensor(by_block(W_F[:, s]), by_block(W_Q[:, s]), scale,
                                                ALU.mult).then_inc(ws_ready, 1)
                    for s in range(3):
                        n = j * 3 + s + m * OT
                        dve.wait_ge(ws_ready, at(n))
                        dve.wait_ge(whi_ready, at(n))
                        dve.wait_ge(wtrans, at(n - 3))
                        nc.vector.tensor_tensor(W_LO[:, s], W_F[:, s], W_HI[:, s],
                                                ALU.subtract).then_inc(wlo_ready, 1)

            for c in range(CHUNKS):
                dve.wait_ge(ld_x[c], 16)
                for tt in range(TPC):
                    n_steps[0] += 1
                    nc.vector.bn_stats(BN_X[:, c * TPC + tt, :], H[:, c * TPC + tt, :]).then_inc(steps, 1)
            dve.wait_ge(steps, n_steps[0])
            moments(BN_X, mean_x, var_x, ra, rb)
            step(nc.vector.tensor_scalar(ra, var_x, 1e-5, None, ALU.add))
            rsqrt(rc, ra, rb, rd, "var_x", 2)
            step(nc.vector.tensor_tensor(ra, rc, rc, ALU.mult))
            step(nc.vector.tensor_tensor(ra, ra, var_x, ALU.mult))
            step(nc.vector.tensor_scalar(ra, ra, 1e-6, None, ALU.add))
            rsqrt(r_x, ra, rb, rd, "ms_x", 3)
            step(nc.vector.tensor_tensor(r_x, r_x, rc, ALU.mult))
            dve.wait_ge(ld_attn, 16 * N_ATTN)
            for b in range(BATCH):
                step(nc.vector.bn_stats(bn_c[:, b, :], CX[:, b, :]))
            mc, vc, cc, ca, cb, cd = st_c
            moments(bn_c, mc, vc, ca, cb)
            step(nc.vector.tensor_tensor(ca, mc, mc, ALU.mult))
            step(nc.vector.tensor_tensor(ca, ca, vc, ALU.add))
            step(nc.vector.tensor_scalar(ca, ca, 1e-6, None, ALU.add))
            rsqrt(cc, ca, cb, cd, "ms_c", 4)
            for b in range(BATCH):
                step(nc.vector.tensor_scalar(CX[:, b, :], CX[:, b, :], cc[:, b:b + 1], None, ALU.mult))
            marks["cx"] = n_steps[0]
            step(nc.vector.tensor_scalar(RMS, RMS, 1.0, None, ALU.add))
            for k in range(KD):
                step(nc.vector.tensor_scalar(QW[:, k], QW[:, k], RMS[:, k:k + 1], None, ALU.mult))
                step(nc.vector.tensor_scalar(KVW[:, :, k], KVW[:, :, k], RMS[:, k:k + 1], None, ALU.mult))
            marks["weights"] = n_steps[0]
            step(nc.vector.tensor_copy(MB, MU8))
            step(nc.vector.tensor_scalar(MB, MB, 1.0, -MASK_FILL, ALU.subtract, ALU.mult))
            HH = HD // 2
            for b in range(BATCH):
                dve.wait_ge(psteps, PS_CXT[b])
                step(nc.vector.tensor_copy(CXT, bank4[0]), f"cxt{b}")
                dve.wait_ge(psteps, PS_KV[b])
                step(nc.vector.tensor_copy(KN, banks[2][:, 0:CTX]))
                step(nc.vector.tensor_copy(VT, banks[3][:, 0:CTX]), f"vt{b}")
                kcos, ksin = RK[:, 0], RK[:, 1]
                step(nc.vector.tensor_tensor(KR[:, 0:HH], KN[:, 0:HH], kcos, ALU.mult))
                step(nc.vector.tensor_tensor(KM[:, 0], KN[:, HH:], ksin, ALU.mult))
                step(nc.vector.tensor_tensor(KR[:, 0:HH], KR[:, 0:HH], KM[:, 0], ALU.subtract))
                step(nc.vector.tensor_tensor(KR[:, HH:], KN[:, HH:], kcos, ALU.mult))
                step(nc.vector.tensor_tensor(KM[:, 1], KN[:, 0:HH], ksin, ALU.mult))
                step(nc.vector.tensor_tensor(KR[:, HH:], KR[:, HH:], KM[:, 1], ALU.add))
                step(nc.vector.tensor_copy(KR2[:, 0:HH], KR[:, HH:]))
                step(nc.vector.tensor_scalar(KR2[:, HH:], KR[:, 0:HH], -1.0, None, ALU.mult), f"kr{b}")
                dve.wait_ge(psteps, PS_KT[b])
                step(nc.vector.tensor_copy(KT1[:, b], bank4[4][:, 0, :]))
                step(nc.vector.tensor_copy(KT2[:, b], bank4[4][:, 1, :]), f"kt{b}")
                for n in range(NH):
                    dve.wait_ge(psteps, PS_VW[b][n])
                    step(nc.vector.tensor_copy(VW[:, b, n, :], banks[6 + n % 2][:, :]), f"vw{b}{n}")

            def norm_tile(c, tt):
                n = c * TPC + tt
                dve.wait_ge(xn_trans, at(n - TPC))
                nc.vector.tensor_scalar(XN[:, tt, :], H[:, n, :], col(mean_x, n), col(r_x, n),
                                        ALU.subtract, ALU.mult).then_inc(xn_ready, 1)

            def mask_and_max(c, tt, b):
                m, s = c * TPC + tt, tt % 2
                dve.wait_ge(scores_ready, at(m))
                dve.wait_ge(exp_ready, at(m - 2))
                nc.vector.tensor_tensor(SC[:, s], bank4[LB[s]],
                                        MB[:, b, :].unsqueeze(1).broadcast_to([P, NH, CTX]),
                                        ALU.add).then_inc(masked, 1)
                dve.wait_ge(masked, at(m))
                nc.vector.tensor_reduce(NMX[:, s, :], SC[:, s], axis=AX.X, op=ALU.max,
                                        negate=True).then_inc(max_ready, 1)

            def normalise(c, tt):
                m, s = c * TPC + tt, tt % 2
                dve.wait_ge(exp_ready, at(m))
                nc.vector.reciprocal(RINV[:, s, :], RSUM[:, s, :]).then_inc(inv_ready, 1)
                dve.wait_ge(inv_ready, at(m))
                nc.vector.tensor_tensor(EX[:, s], EX[:, s], RINV[:, s, :].unsqueeze(2).broadcast_to([P, NH, CTX]),
                                        ALU.mult).then_inc(probs_ready, 1)

            def rope(c, par, n, turn):
                q = c * NH + n
                dve.wait_ge(q_ready, at(q))
                if n == 0:
                    dve.wait_ge(ld_tab[par], (turn + 1) * 16)
                    dve.wait_ge(scores_ready, at(c * TPC - TPC - 1))
                for buf, k in ((QC, 0), (QS, 1)):
                    last = nc.vector.tensor_tensor(buf[:, par, n, :], banks[QB[n % 2]][:, :], TAB[:, par, k, :],
                                                   ALU.mult)
                last.then_inc(roped, 1)

            def residual(c, tt):
                m = c * TPC + tt
                dve.wait_ge(attn_ready, at(m))
                nc.vector.scalar_tensor_tensor(H[:, m, :], banks[OB][:, :], gates[:, 0:1], H[:, m, :],
                                               ALU.mult, ALU.add).then_inc(h_ready, 1)
                dve.wait_ge(h_ready, at(m))
                nc.vector.bn_stats(BN_H[:, m, :], H[:, m, :])
                nc.vector.tensor_reduce(col(hmax, m), H[:, m, :], axis=AX.X, op=ALU.max)
                nc.vector.tensor_reduce(col(hmin, m), H[:, m, :], axis=AX.X, op=ALU.min).then_inc(h_stats, 1)

            def attend(c, par, turn, b, last=False, norm=True):
                mask_and_max(c, 0, b)
                mask_and_max(c, 1, b)
                for tt in range(TPC):
                    if tt >= 1:
                        if tt + 1 < TPC:
                            mask_and_max(c, tt + 1, b)
                    if not last and tt < 3:
                        normalise(c, tt)
                        rope(c + 1, 1 - par, tt, turn)
                    elif not last:
                        rope(c + 1, 1 - par, 3, turn)
                        normalise(c, 3)
                    else:
                        normalise(c, tt)
                    residual(c, tt)
                if norm:
                    for tt in range(TPC):
                        norm_tile(c + 2, tt)

            dve.wait_ge(asteps, 1)
            for tt in range(TPC):
                norm_tile(0, tt)
            for n in range(NH):
                rope(0, 0, n, 0)
            for tt in range(TPC):
                norm_tile(1, tt)

            def attend_pair(j, last):
                attend(j * 2, 0, j, j // 2, norm=not last)
                attend(j * 2 + 1, 1, j + 1, j // 2, last=last, norm=not last)

            with dve.Fori(0, CHUNKS // 2 - 1) as j:
                attend_pair(j, False)
            attend_pair(CHUNKS // 2 - 1, True)

            dve.wait_ge(h_stats, at(TILES - 1))
            moments(BN_H, mean_h, var_h, ra, rb)
            step(nc.vector.tensor_scalar(ra, var_h, 1e-5, None, ALU.add))
            rsqrt(r_h, ra, rb, rd, "var_h", 5)
            step(nc.vector.tensor_tensor(ra, hmax, mean_h, ALU.subtract))
            step(nc.vector.tensor_tensor(rb, mean_h, hmin, ALU.subtract))
            step(nc.vector.tensor_tensor(ra, ra, rb, ALU.max))
            step(nc.vector.tensor_tensor(ra, ra, r_h, ALU.mult))
            step(nc.vector.tensor_reduce(x_row, ra, axis=AX.X, op=ALU.max), "x_row")
            dve.wait_ge(peaks, 2)
            scale_of(s_x, i_x, x_all, QMAX)
            step(nc.vector.tensor_scalar(c_h, r_h, i_x, None, ALU.mult))
            step(nc.vector.tensor_scalar(d_g, w_undo[:, 0:1], s_x, None, ALU.mult))
            step(nc.vector.tensor_scalar(d_u, w_undo[:, 1:2], s_x, None, ALU.mult))
            step(nc.vector.memset(gg_run, 0.0))
            step(nc.vector.memset(p_acc, 0.0))

            def quantise_row(n, s):
                dve.wait_ge(x_trans, at(n - TPC))
                nc.vector.tensor_scalar(XI[:, s, :], H[:, n, :], col(mean_h, n), col(c_h, n),
                                        ALU.subtract, ALU.mult).then_inc(xi_ready, 1)
                dve.wait_ge(xi_ready, at(n))
                nc.vector.tensor_copy(XH[:, s, :], XI[:, s, :]).then_inc(xh_ready, 1)
                dve.wait_ge(xh_ready, at(n))
                nc.vector.tensor_tensor(XL[:, s, :], XI[:, s, :], XH[:, s, :], ALU.subtract).then_inc(xl_ready, 1)

            def peak_of(r, k, table, top=None, late=False):
                dve.wait_ge(stg_ready, at(r * 2 + 1))
                unit = LU[:, k] if late else STG[:, k % 3].rearrange("p a b -> p (a b)")
                if top is not None:
                    nc.vector.tensor_reduce(top, unit, axis=AX.X, op=ALU.max)
                nc.vector.tensor_reduce(table, unit, axis=AX.X, op=ALU.max,
                                        apply_absolute_value=True).then_inc(stg_peaked, 1)

            for tt in range(TPC):
                quantise_row(tt, tt)
            for tt in range(TPC):
                quantise_row(TPC + tt, tt)

            def gate_chunk(c, rows):
                for k in range(UPC):
                    r = c * UPC + k
                    peak_of(r, k, col(g_peak, r), col(g_top, r))
                    if rows and k >= 2:
                        quantise_row((c + 2) * TPC + k - 2, k - 2)

            with dve.Fori(0, CHUNKS - 2) as c:
                gate_chunk(c, True)
            for c in (CHUNKS - 2, CHUNKS - 1):
                gate_chunk(c, False)
            dve.wait_ge(stg_peaked, at(UNITS - 1))
            step(nc.vector.tensor_reduce(g_row[:, 0:1], g_peak, axis=AX.X, op=ALU.max))
            step(nc.vector.tensor_reduce(g_row[:, 1:2], g_top, axis=AX.X, op=ALU.max), "g_row")
            dve.wait_ge(peaks, 3)
            step(nc.vector.tensor_scalar(tmp1[:, 0:1], g_all[:, 0:1], d_g, None, ALU.mult))
            scale_of(s_g, i_g, tmp1[:, 0:1], QMAX)
            step(nc.vector.tensor_scalar(c_g, i_g, d_g, None, ALU.mult), "c_g")
            dve.wait_ge(asteps, 7)
            step(nc.vector.tensor_scalar(top_sq, top_sig, 65536.0, 65535.0, ALU.mult, ALU.min))
            step(nc.vector.tensor_tensor(top_g, top_i, top_sq, ALU.mult))

            with dve.Fori(0, CHUNKS // 2) as c:
                for k in range(2 * UPC):
                    q = c * (2 * UPC) + k
                    dve.wait_ge(sig_ready, at(q))
                    nc.vector.tensor_scalar(SQ[:, k % 2, :], GB[:, k % 6, :], 65536.0, 65535.0, ALU.mult,
                                            ALU.min).then_inc(sq_ready, 1)
                    if k == 0:
                        dve.wait_ge(gg_folded, at(c - 1))
                    dve.wait_ge(sq_ready, at(q))
                    nc.vector.tensor_copy(G[:, q, :], GQ[:, k % 2, :]).then_inc(g_kept, 1)
                    nc.vector.tensor_tensor_reduce(GB[:, k % 6, :], GQ[:, k % 2, :], SQ[:, k % 2, :], -1.0, 0.0,
                                                   op0=ALU.mult, op1=ALU.max,
                                                   accum_out=gg_acc[:, k:k + 1]).then_inc(gg_peaked, 1)
                    if k % 2:
                        r = c * UPC + k // 2
                        peak_of(r + UNITS, k // 2, col(u_peak, r))
                dve.wait_ge(gg_peaked, at(c * (2 * UPC) + 2 * UPC - 1))
                nc.vector.tensor_tensor(gg_run, gg_run, gg_acc, ALU.max).then_inc(gg_folded, 1)
            dve.wait_ge(gg_folded, at(CHUNKS // 2 - 1))
            step(nc.vector.tensor_reduce(gg_row, gg_run, axis=AX.X, op=ALU.max))
            step(nc.vector.tensor_tensor(gg_row, gg_row, top_g, ALU.max), "gg_row")
            dve.wait_ge(peaks, 4)
            step(nc.vector.tensor_scalar(tmp1[:, 1:2], s_g, 1.0 / 65536.0, None, ALU.mult))
            step(nc.vector.tensor_scalar(tmp1[:, 2:3], gg_all, tmp1[:, 1:2], None, ALU.mult))
            scale_of(s_gg, i_gg, tmp1[:, 2:3], QMAX)
            step(nc.vector.tensor_scalar(c_gg, i_gg, tmp1[:, 1:2], None, ALU.mult))

            def second_half(c, late=False):
                for k in range(2 * UPC):
                    q = c * (2 * UPC) + k
                    dve.wait_ge(sig2_ready, at(q))
                    nc.vector.tensor_scalar(SQ[:, k % 2, :], GB[:, k % 3, :], 65536.0, 65535.0, ALU.mult,
                                            ALU.min).then_inc(sq2_ready, 1)
                    dve.wait_ge(sq2_ready, at(q))
                    nc.vector.scalar_tensor_tensor(G[:, q, :], SQ[:, k % 2, :], c_gg, G[:, q, :], ALU.mult,
                                                   ALU.mult).then_inc(gg_ready, 1)
                    if k % 2:
                        r = c * UPC + k // 2 + UNITS // 2
                        peak_of(r + UNITS, k // 2, col(u_peak, r), late=late)

            with dve.Fori(0, CHUNKS // 2 - 1) as c:
                second_half(c)
            second_half(CHUNKS // 2 - 1, late=True)
            dve.wait_ge(stg_peaked, at(2 * UNITS - 1))
            step(nc.vector.tensor_reduce(u_row, u_peak, axis=AX.X, op=ALU.max), "u_row")
            dve.wait_ge(peaks, 5)
            step(nc.vector.tensor_scalar(tmp1[:, 0:1], u_all, d_u, None, ALU.mult))
            scale_of(s_u, i_u, tmp1[:, 0:1], QMAX)
            step(nc.vector.tensor_scalar(c_u, i_u, d_u, None, ALU.mult), "c_u")

            dve.wait_ge(gg_ready, at(UNITS - 1))
            def product_peaks(i):
                for k in range(UPC):
                    n = i * UPC + k
                    q = UNITS - UPC + k if late_group(i) else (i - 1) * UPC + k
                    up = (LU if late_group(i) else UR)[:, k]
                    s = k % 3
                    dve.wait_ge(p_peaked, at(n - 1))
                    if k in DVE_ABS:
                        nc.vector.scalar_tensor_tensor(AB[:, s, :], G[:, q, :], -1.0, G[:, q, :], ALU.mult,
                                                       ALU.max).then_inc(pab2_ready, 1)
                        dve.wait_ge(pab2_ready, at(i * len(DVE_ABS) + DVE_ABS.index(k)))
                    else:
                        dve.wait_ge(pab_ready, at(i * len(ACT_ABS) + ACT_ABS.index(k)))
                    dve.wait_ge(ua_ready, at(n))
                    nc.vector.tensor_copy(col(p_peak, n), p_acc[:, 1 - k % 2:2 - k % 2]).then_inc(p_folded, 1)
                    nc.vector.tensor_tensor_reduce(up, AB[:, s, :], UA[:, s, :], 1.0, 0.0, op0=ALU.mult,
                                                   op1=ALU.max, accum_out=p_acc[:, k % 2:k % 2 + 1]) \
                        .then_inc(p_peaked, 1)

            product_peaks(0)
            with dve.Fori(1, CHUNKS) as i:
                product_peaks(i)
            dve.wait_ge(p_peaked, at(UNITS - 1))
            dve.wait_ge(p_folded, at(UNITS - 1))
            step(nc.vector.tensor_reduce(p_row, p_peak, axis=AX.X, op=ALU.max))
            step(nc.vector.tensor_tensor(p_row, p_row, p_acc[:, 1:2], ALU.max), "p_row")
            dve.wait_ge(peaks, 6)
            step(nc.vector.tensor_tensor(tmp1[:, 0:1], s_gg, s_u, ALU.mult))
            step(nc.vector.tensor_scalar(tmp1[:, 1:2], p_all, tmp1[:, 0:1], None, ALU.mult))
            scale_of(s_p, i_p, tmp1[:, 1:2], QMAX)
            step(nc.vector.tensor_scalar(c_p, tmp1[:, 0:1], i_p, None, ALU.mult))
            step(nc.vector.tensor_scalar(c_out, s_p, w_undo[:, 2:3], None, ALU.mult))
            step(nc.vector.tensor_scalar(c_out, c_out, gates[:, 1:2], None, ALU.mult))

            def product_units(c, par):
                for k in range(UPC):
                    q, s = c * UPC + k, k % 2
                    dve.wait_ge(ui_ready, at(q))
                    nc.vector.scalar_tensor_tensor(OI[:, s, :], G[:, q, :], c_p, UI[:, s, :], ALU.mult,
                                                   ALU.mult).then_inc(oi_ready, 1)
                    oi = OI[:, s, :]
                    hi = OH[:, par, 2 * k:2 * k + 2, :].rearrange("p a b -> p (a b)")
                    lo = OL[:, par, 2 * k:2 * k + 2, :].rearrange("p a b -> p (a b)")
                    dve.wait_ge(oi_ready, at(q))
                    dve.wait_ge(down_ready, at(c * TPC - TPC - 1))
                    nc.vector.tensor_copy(hi, oi).then_inc(oh_ready, 1)
                    dve.wait_ge(oh_ready, at(q))
                    nc.vector.tensor_tensor(lo, oi, hi, ALU.subtract).then_inc(ol_ready, 1)

            def output_tiles(j, par):
                for tt in range(TPC):
                    m = (j * 2 + par) * TPC + tt
                    if tt == 0:
                        dve.wait_ge(ld_hb[par], (j + 1) * 16)
                    dve.wait_ge(down_ready, at(m))
                    nc.vector.scalar_tensor_tensor(HB[:, par, tt, :], banks[par * TPC + tt][:, :], c_out,
                                                   HB[:, par, tt, :], ALU.mult, ALU.add).then_inc(y_ready, 1)

            product_units(0, 0)
            with dve.Fori(0, CHUNKS // 2 - 1) as j:
                product_units(j * 2 + 1, 1)
                output_tiles(j, 0)
                product_units(j * 2 + 2, 0)
                output_tiles(j, 1)
            product_units(CHUNKS - 1, 1)
            output_tiles(CHUNKS // 2 - 1, 0)
            output_tiles(CHUNKS // 2 - 1, 1)

        @block.scalar
        def _(act):
            for name, s in counted.items():
                if name in ACT_EVENTS:
                    act.sem_inc(s, LEAD)
            act.wait_ge(ld_small, 16 * N_SMALL)
            nc.scalar.activation(gates, gates, ACT.Tanh).then_inc(asteps, 1)
            for m in range(3):
                with act.Fori(0, OT // 3) as j:
                    for s in range(3):
                        n = j * 3 + s + m * OT
                        act.wait_ge(ws_ready, at(n))
                        act.wait_ge(wtrans, at(n - 3))
                        nc.scalar.activation(W_HI[:, s], W_F[:, s], ACT.Copy).then_inc(whi_ready, 1)
                    for s in range(3):
                        n = j * 3 + s + m * OT
                        act.wait_ge(wtrans, at(n))
                        act.wait_ge(st_wt[s], (j + m * (OT // 3) + 1) * 16 if m < 2 else (j * 2 + 2 * (OT // 3) + 1) * 16)
                        nc.scalar.activation(W_T[:, s], bank16[s], ACT.Copy).then_inc(wt_ready, 1)
            act.wait_ge(steps, marks["var_x"])
            nc.scalar.activation(rb, ra, ACT.Sqrt).then_inc(asteps, 1)
            act.wait_ge(steps, marks["ms_x"])
            nc.scalar.activation(rb, ra, ACT.Sqrt).then_inc(asteps, 1)
            act.wait_ge(steps, marks["ms_c"])
            nc.scalar.activation(st_c[4], st_c[3], ACT.Sqrt).then_inc(asteps, 1)

            def take_xt(c, tt):
                n = c * TPC + tt
                act.wait_ge(xn_trans, at(n))
                act.wait_ge(q_ready, at(c * NH - 1))
                nc.scalar.activation(XTC[:, :, tt * P:(tt + 1) * P], bank4[TB[tt % 2]],
                                     ACT.Copy).then_inc(xtc_ready, 1)

            def exps(c, tt):
                m, s = c * TPC + tt, tt % 2
                act.wait_ge(max_ready, at(m))
                act.wait_ge(probs_trans, at(m - 2))
                for n in range(NH):
                    last = nc.scalar.activation(EX[:, s, n, :], SC[:, s, n, :], ACT.Exp, bias=NMX[:, s, n:n + 1],
                                                accum_out=RSUM[:, s, n:n + 1])
                last.then_inc(exp_ready, 1)

            def take_pt(c, tt):
                m, s = c * TPC + tt, tt % 2
                act.wait_ge(probs_trans, at(m))
                act.wait_ge(attn_ready, at(m - 2))
                nc.scalar.activation(PT[:, s], bank4[PB], ACT.Copy).then_inc(pt_ready, 1)

            for tt in range(TPC):
                take_xt(0, tt)

            def attend(c, last):
                exps(c, 0)
                if not last:
                    for tt in range(TPC):
                        take_xt(c + 1, tt)
                for tt in range(TPC):
                    if tt + 1 < TPC:
                        exps(c, tt + 1)
                    take_pt(c, tt)

            with act.Fori(0, CHUNKS - 1) as c:
                attend(c, False)
            attend(CHUNKS - 1, True)
            act.wait_ge(steps, marks["var_h"])
            nc.scalar.activation(rb, ra, ACT.Sqrt).then_inc(asteps, 1)

            def take_x(n, c, tt):
                act.wait_ge(x_trans, at(n))
                nc.scalar.activation(XT[:, c, :, :, tt * P:(tt + 1) * P], bank16[XB[tt % 2]],
                                     ACT.Copy).then_inc(xt_ready, 1)

            def take_mm(c, o, late=False):
                n, k = c * OT + o, o // 2
                act.wait_ge(mm_ready, at(n))
                if late:
                    nc.scalar.activation(LU[:, k, bass.ts(o % 2, CHUNK)], banks[o % MM][:, :],
                                         ACT.Copy).then_inc(stg_ready, 1)
                    return
                if o % 2 == 0:
                    act.wait_ge(stg_peaked, at(c * UPC + k - 3))
                    act.wait_ge(st_stg[k % 3], (c * (UPC // 3) + k // 3 + 1) * 16)
                nc.scalar.activation(STG[:, k % 3, o % 2, :], banks[o % MM][:, :], ACT.Copy).then_inc(stg_ready, 1)

            for tt in range(TPC):
                take_x(tt, 0, tt)
            with act.Fori(0, CHUNKS - 1) as c:
                for o in range(OT):
                    take_mm(c, o)
                    if o % 3 == 2:
                        take_x((c + 1) * TPC + o // 3, c + 1, o // 3)
            for o in range(OT):
                take_mm(CHUNKS - 1, o)

            act.wait_ge(steps, marks["c_g"])
            nc.scalar.activation(top_i, g_all[:, 1:2], ACT.Copy, scale=c_g).then_inc(asteps, 1)
            act.wait_ge(asteps, 6)
            nc.scalar.activation(top_sig, top_i, ACT.Sigmoid, scale=s_g).then_inc(asteps, 1)
            with act.Fori(0, CHUNKS // 2) as c:
                for k in range(2 * UPC):
                    q = c * (2 * UPC) + k
                    act.wait_ge(ld_gb[k % 6], (c * 2 + k // 6 + 1) * 16)
                    act.wait_ge(gg_peaked, at(q - 2))
                    nc.scalar.activation(GQ[:, k % 2, :], GB[:, k % 6, :], ACT.Copy, scale=c_g).then_inc(gi_ready, 1)
                    take_mm(c + CHUNKS, k)
                    act.wait_ge(gi_ready, at(q))
                    nc.scalar.activation(GB[:, k % 6, :], GQ[:, k % 2, :], ACT.Sigmoid, scale=s_g).then_inc(sig_ready, 1)
            act.wait_ge(g_kept, at(UNITS - 1))
            def second_half(c, late=False):
                for k in range(2 * UPC):
                    q = c * (2 * UPC) + k
                    if k < 3:
                        act.wait_ge(gg_peaked, at(UNITS - 1))
                    act.wait_ge(sq2_ready, at(q - 3))
                    nc.scalar.activation(GB[:, k % 3, :], G[:, q, :], ACT.Sigmoid, scale=s_g).then_inc(sig2_ready, 1)
                    take_mm(c + CHUNKS + CHUNKS // 2, k, late=late)

            with act.Fori(0, CHUNKS // 2 - 1) as c:
                second_half(c)
            second_half(CHUNKS // 2 - 1, late=True)

            act.wait_ge(steps, marks["c_u"])
            def absolutes(i):
                for k in range(UPC):
                    n = i * UPC + k
                    q = UNITS - UPC + k if late_group(i) else (i - 1) * UPC + k
                    act.wait_ge(p_peaked, at(n - 3))
                    if k in ACT_ABS:
                        nc.scalar.activation(AB[:, k % 3, :], G[:, q, :], ACT.Abs).then_inc(pab_ready, 1)
                    if not late_group(i):
                        act.wait_ge(ld_ur[k], i * 16)
                    nc.scalar.activation(UA[:, k % 3, :], (LU if late_group(i) else UR)[:, k], ACT.Abs,
                                         scale=c_u).then_inc(ua_ready, 1)

            act.wait_ge(gg_ready, at(UNITS - 1))
            act.wait_ge(st_lu, 16 * UPC)
            absolutes(0)
            with act.Fori(1, CHUNKS) as i:
                absolutes(i)

            act.wait_ge(p_peaked, at(UNITS - 1))
            with act.Fori(0, CHUNKS) as c:
                for k in range(UPC):
                    q = c * UPC + k
                    act.wait_ge(ld_ub[k % 3], (c * 2 + k // 3 + 1) * 16)
                    act.wait_ge(oi_ready, at(q - 2))
                    nc.scalar.activation(UI[:, k % 2, :], UB[:, k % 3, :], ACT.Copy, scale=c_u).then_inc(ui_ready, 1)

        @block.tensor
        def _(pe):
            for name, s in counted.items():
                if name in PE_EVENTS:
                    pe.sem_inc(s, LEAD)
            pe.wait_ge(idents, 4)
            for m in range(3):
                with pe.Fori(0, OT // 3) as j:
                    for s in range(3):
                        n = j * 3 + s + m * OT
                        pe.wait_ge(wlo_ready, at(n))
                        pe.wait_ge(wt_ready, at(n - 3))
                        for a, part in enumerate((W_HI, W_LO)):
                            for k in range(KD):
                                last = nc.tensor.transpose(bank16[s][:, a, k, :], part[:, s, k * P:(k + 1) * P],
                                                           ident16)
                        last.then_inc(wtrans, 1)
            n_steps = [0]

            def step(ins, want):
                n_steps[0] += 1
                assert n_steps[0] == want, (n_steps, want)
                ins.then_inc(psteps, 1)

            pe.wait_ge(wt_ready, at(3 * OT - 1))
            for b in range(BATCH):
                pe.wait_ge(steps, marks["cx"] if b == 0 else marks[f"vw{b - 1}3"])
                for k in range(KD):
                    last = nc.tensor.transpose(bank4[0][:, k, :], CX[:, b, k * P:(k + 1) * P], ident)
                step(last, PS_CXT[b])
                pe.wait_ge(steps, max(marks[f"cxt{b}"], marks["weights"]))
                for k in range(KD):
                    nc.tensor.matmul(banks[2][:, 0:CTX], CXT[:, k, :], KVW[:, 0, k, :], start=k == 0, stop=k == KD - 1)
                for k in range(KD):
                    last = nc.tensor.matmul(banks[3][:, 0:CTX], KVW[:, 1, k, :], CXT[:, k, :], start=k == 0,
                                            stop=k == KD - 1)
                step(last, PS_KV[b])
                pe.wait_ge(steps, marks[f"kr{b}"])
                nc.tensor.transpose(bank4[4][:, 0, :], KR, ident)
                step(nc.tensor.transpose(bank4[4][:, 1, :], KR2, ident), PS_KT[b])
                for n in range(NH):
                    if n >= 2:
                        pe.wait_ge(steps, marks[f"vw{b}{n - 2}"])
                    step(nc.tensor.matmul(banks[6 + n % 2][:, :], VT, OW[:, n, :], start=True, stop=True), PS_VW[b][n])
            pe.wait_ge(steps, marks["vw13"])

            def transposes(c, tt):
                n = c * TPC + tt
                pe.wait_ge(xn_ready, at(n))
                pe.wait_ge(xtc_ready, at(n - 2))
                for k in range(KD):
                    last = nc.tensor.transpose(bank4[TB[tt % 2]][:, k, :], XN[:, tt, k * P:(k + 1) * P], ident)
                last.then_inc(xn_trans, 1)

            def query(c, n):
                pe.wait_ge(xtc_ready, at(c * TPC + TPC - 1))
                pe.wait_ge(roped, at(c * NH + n - 2))
                for k in range(KD):
                    last = nc.tensor.matmul(banks[QB[n % 2]][:, :], QW[:, k, n, :], XTC[:, k, :], start=k == 0,
                                            stop=k == KD - 1)
                last.then_inc(q_ready, 1)

            def scores(c, par, tt, b):
                m, s = c * TPC + tt, tt % 2
                pe.wait_ge(roped, at(c * NH + NH - 1))
                pe.wait_ge(masked, at(m - 2))
                for n in range(NH):
                    nc.tensor.matmul(bank4[LB[s]][:, n, :], QC[:, par, n, tt * P:(tt + 1) * P], KT1[:, b, :],
                                     start=True, stop=False)
                    last = nc.tensor.matmul(bank4[LB[s]][:, n, :], QS[:, par, n, tt * P:(tt + 1) * P], KT2[:, b, :],
                                            start=False, stop=True)
                last.then_inc(scores_ready, 1)

            def probs(c, tt):
                m, s = c * TPC + tt, tt % 2
                pe.wait_ge(probs_ready, at(m))
                pe.wait_ge(pt_ready, at(m - 1))
                for n in range(NH):
                    last = nc.tensor.transpose(bank4[PB][:, n, :], EX[:, s, n, :], ident)
                last.then_inc(probs_trans, 1)

            def output(c, tt, b):
                m, s = c * TPC + tt, tt % 2
                pe.wait_ge(pt_ready, at(m))
                pe.wait_ge(h_ready, at(m - 1))
                for n in range(NH):
                    last = nc.tensor.matmul(banks[OB][:, :], PT[:, s, n, :], VW[:, b, n, :], start=n == 0,
                                            stop=n == NH - 1)
                last.then_inc(attn_ready, 1)

            def attend(c, par, b, b_next, last=False):
                scores(c, par, 1, b)
                if not last:
                    for tt in range(TPC):
                        transposes(c + 1, tt)
                for tt in range(TPC):
                    if not last:
                        query(c + 1, tt)
                    probs(c, tt)
                    output(c, tt, b)
                    if tt + 2 < TPC:
                        scores(c, par, tt + 2, b)
                if not last:
                    scores(c + 1, 1 - par, 0, b_next)

            for tt in range(TPC):
                transposes(0, tt)
            for n in range(NH):
                query(0, n)
            scores(0, 0, 0, 0)
            with pe.Fori(0, CHUNKS // 2 - 1) as j:
                attend(j * 2, 0, j // 2, j // 2)
                attend(j * 2 + 1, 1, j // 2, (j + 1) // 2)
            attend(CHUNKS - 2, 0, 1, 1)
            attend(CHUNKS - 1, 1, 1, 1, last=True)

            def transpose_x(n, tt):
                pe.wait_ge(xl_ready, at(n))
                pe.wait_ge(xt_ready, at(n - 2))
                for a, part in enumerate((XH, XL)):
                    for k in range(KD):
                        last = nc.tensor.transpose(bank16[XB[tt % 2]][:, a, k, :], part[:, tt, k * P:(k + 1) * P],
                                                   ident16)
                last.then_inc(x_trans, 1)

            def product(c, cx, o):
                n = c * OT + o
                pe.wait_ge(stg_ready, at(n - MM))
                i = 0
                for a, x_part in ((0, 0), (0, 1), (1, 0)):
                    for k in range(KD):
                        last = nc.tensor.matmul(banks[o % MM][:, :], W[:, o, a, k, :], XT[:, cx, x_part, k, :],
                                                start=i == 0, stop=i == 3 * KD - 1)
                        i += 1
                last.then_inc(mm_ready, 1)

            for tt in range(TPC):
                transpose_x(tt, tt)
            pe.wait_ge(ld_wg, 16)
            with pe.Fori(0, CHUNKS - 1) as c:
                pe.wait_ge(xt_ready, at(c * TPC + TPC - 1))
                for o in range(OT):
                    product(c, c, o)
                    if o % 3 == 2:
                        transpose_x((c + 1) * TPC + o // 3, o // 3)
            pe.wait_ge(xt_ready, at(TILES - 1))
            for o in range(OT):
                product(CHUNKS - 1, CHUNKS - 1, o)
            with pe.Fori(0, CHUNKS) as c:
                for o in range(OT):
                    if o % 4 == 0:
                        pe.wait_ge(ld_wu[o // 4], 16)
                    product(c + CHUNKS, c, o)

            def down(c, par):
                for tt in range(TPC):
                    m = c * TPC + tt
                    pe.wait_ge(y_ready, at(m - 2 * TPC))
                    i = 0
                    for o in range(OT):
                        if tt == 0 and o % 2 == 0:
                            pe.wait_ge(ol_ready, at(c * UPC + o // 2))
                        for part, a in ((OH, 0), (OH, 1), (OL, 0)):
                            last = nc.tensor.matmul(banks[par * TPC + tt][:, :],
                                                    part[:, par, o, tt * P:(tt + 1) * P], WD[:, o, a, :],
                                                    start=i == 0, stop=i == 3 * OT - 1)
                            i += 1
                    last.then_inc(down_ready, 1)

            pe.wait_ge(ld_wd, 16)
            pe.wait_ge(stg_ready, at(2 * CHUNKS * OT - 1))
            down(0, 0)
            down(1, 1)
            with pe.Fori(1, CHUNKS // 2) as j:
                down(j * 2, 0)
                down(j * 2 + 1, 1)

        @block.gpsimd
        def _(pool):
            pool.memset(ident, 0.0).then_inc(idents, 1)
            pool.memset(ident16, 0.0).then_inc(idents, 1)
            pool.wait_ge(idents, 2)
            for m in (ident, ident16):
                pool.affine_select(out=m, in_=m, compare_op=ALU.not_equal, fill=1.0, base=0,
                                   pattern=[[-1, P]], channel_multiplier=1).then_inc(idents, 1)
            RMAX = bass.bass_isa.ReduceOp.max
            for mark, row, all_ in (("w_row", w_row, w_all), ("x_row", x_row, x_all), ("g_row", g_row, g_all),
                                    ("gg_row", gg_row, gg_all), ("u_row", u_row, u_all), ("p_row", p_row, p_all)):
                pool.wait_ge(steps, marks[mark])
                pool.partition_all_reduce(all_, row, P, RMAX).then_inc(peaks, 1)

        @block.sync
        def _(sp):
            for s in st_wt + st_stg + st_out:
                sp.sem_inc(s, 16)
            for m in range(3):
                dst = WRAW[:, m] if m < 2 else WRAW[:, m].rearrange("p (r s) d -> p r s d", s=3)
                sp.dma_start(dst, w_src[m]).then_inc(ld_w, 16)
            sp.dma_start(gates[:, 0:1], g_xattn.partition_broadcast(P)).then_inc(ld_small, 16)
            sp.dma_start(gates[:, 1:2], g_ffn.partition_broadcast(P)).then_inc(ld_small, 16)
            for c in range(CHUNKS):
                sp.dma_start(H[:, c * TPC:(c + 1) * TPC, :], x_src[c]).then_inc(ld_x[c], 16)
            for m, dst in enumerate((wg_dram, wu_dram, wd_dram)):
                with sp.Fori(0, OT // 3) as j:
                    for s in range(3):
                        sp.wait_ge(wt_ready, at(j * 3 + s + m * OT))
                        if m < 2:
                            sp.dma_start(dst[j * 3 + s], W_T[:, s]).then_inc(st_wt[s], 16)
                        else:
                            for a in range(2):
                                sp.dma_start(dst[s * KD:(s + 1) * KD, :, a, bass.ts(j, P)]
                                             .rearrange("k p c -> p k c"), W_T[:, s, a]).then_inc(st_wt[s], 16)
            for s in range(3):
                sp.wait_ge(st_wt[s], (4 * (OT // 3) + 1) * 16)
            sp.dma_start(W, wg_dram.rearrange("o p a k c -> p o a k c")).then_inc(ld_wg, 16)
            sp.dma_start(RMS, rms_scale.rearrange("(k p) -> p k", p=P),
                         allow_slow_non_contiguous=True).then_inc(ld_attn, 16)
            for n in range(NH):
                sp.dma_start(QW[:, :, n, :], q_w[n].rearrange("(k p) h -> p k h", p=P)).then_inc(ld_attn, 16)
            for dst, src in (
                             (KVW[:, 0], kv_w[0, 0].rearrange("(k p) h -> p k h", p=P)),
                             (KVW[:, 1], kv_w[1, 0].rearrange("(k p) h -> p k h", p=P)),
                             (OW, out_w.rearrange("n h d -> h n d")),
                             (CX, ctx_in.rearrange("b s d -> s b d")),
                             (MU8, mask.partition_broadcast(P)),
                             (RK, rope_k)):
                sp.dma_start(dst, src).then_inc(ld_attn, 16)
            sp.wait_ge(psteps, PS_VW[1][NH - 1])
            for par in range(2):
                sp.dma_start(TAB[:, par], rope_q[par]).then_inc(ld_tab[par], 16)
            with sp.Fori(0, CHUNKS // 2 - 1) as j:
                for par in range(2):
                    c = j * 2 + par
                    sp.wait_ge(h_ready, at(c * TPC + TPC - 1))
                    sp.dma_start(h_dram[c], H[:, bass.ds(c * TPC, TPC), :]).then_inc(st_h, 16)
                    sp.dma_start(TAB[:, par], rope_q[c + 2]).then_inc(ld_tab[par], 16)
            for c in (CHUNKS - 2, CHUNKS - 1):
                sp.wait_ge(h_ready, at(c * TPC + TPC - 1))
                sp.dma_start(h_dram[c], H[:, c * TPC:(c + 1) * TPC, :]).then_inc(st_h, 16)

            def store(c, k, dst, q):
                sp.wait_ge(stg_ready, at(c * OT + 2 * k + 1))
                sp.dma_start(dst[q], STG[:, k % 3].rearrange("p a b -> p (a b)")).then_inc(st_stg[k % 3], 16)

            with sp.Fori(0, CHUNKS - 1) as c:
                for k in range(UPC):
                    store(c, k, g_dram, c * UPC + k)
            sp.wait_ge(x_trans, at(TILES - 1))
            for s in range(3):
                sp.wait_ge(st_stg[s], 3 * 16)
            for k in range(6):
                sp.dma_start(GB[:, k, :], g_dram[k]).then_inc(ld_gb[k], 16)
            for k in range(UPC):
                store(CHUNKS - 1, k, g_dram, (CHUNKS - 1) * UPC + k)
            for i in range(3):
                sp.wait_ge(mm_ready, at((CHUNKS - 1) * OT + 4 * i + 3))
                sp.dma_start(W[:, 4 * i:4 * i + 4], wu_dram[4 * i:4 * i + 4].rearrange("o p a k c -> p o a k c")) \
                    .then_inc(ld_wu[i], 16)
            for s in range(3):
                sp.wait_ge(st_stg[s], (UNITS // 3 + 1) * 16)
            def first_half(c, units):
                for k in range(2 * UPC):
                    if k in units:
                        q = c * (2 * UPC) + k + 6
                        sp.wait_ge(gg_peaked, at(q - 6))
                        sp.dma_start(GB[:, k % 6, :], g_dram[q]).then_inc(ld_gb[k % 6], 16)
                    if k % 2:
                        store(c + CHUNKS, k // 2, u_dram, c * UPC + k // 2)

            with sp.Fori(0, CHUNKS // 2 - 1) as c:
                first_half(c, range(12))
            first_half(CHUNKS // 2 - 1, range(6))
            with sp.Fori(CHUNKS // 2, CHUNKS - 1) as c:
                for k in range(UPC):
                    store(c + CHUNKS, k, u_dram, c * UPC + k)
            for s in range(3):
                sp.wait_ge(st_stg[s], (UNITS // 3 + 5) * 16)

            def load_up(q, k):
                sp.dma_start(UR[:, k, :], u_dram[q]).then_inc(ld_ur[k], 16)

            for k in (3, 4, 5):
                load_up(k, k)
            for k in range(UPC):
                sp.wait_ge(stg_ready, at((2 * CHUNKS - 1) * OT + 2 * k + 1))
                sp.dma_start(u_dram[UNITS - UPC + k], LU[:, k, :]).then_inc(st_lu, 16)
            sp.wait_ge(sq2_ready, at(UNITS - 1))
            for k in range(3):
                load_up(k, k)
            sp.wait_ge(mm_ready, at(2 * CHUNKS * OT - 1))
            sp.wait_ge(stg_peaked, at(2 * UNITS - 1))
            for s in range(3):
                sp.wait_ge(st_stg[s], (4 * CHUNKS - 1) * 16)
            sp.dma_start(WD, wd_dram.rearrange("o p a d -> p o a d")).then_inc(ld_wd, 16)
            with sp.Fori(1, CHUNKS - 1) as i:
                for k in range(UPC):
                    sp.wait_ge(p_peaked, at(i * UPC + k))
                    load_up(i * UPC + k, k)
            sp.wait_ge(st_lu, 16 * UPC)
            sp.wait_ge(st_h, 16 * CHUNKS)
            sp.wait_ge(p_peaked, at(UNITS - 1))
            sp.wait_ge(sq2_ready, at(UNITS - 1))
            for par in range(2):
                sp.dma_start(HB[:, par], h_dram[par]).then_inc(ld_hb[par], 16)

            def up_units(c):
                for k in range(UPC):
                    sp.wait_ge(ui_ready, at(c * UPC + k - 3))
                    sp.dma_start(UB[:, k % 3, :], u_dram[c * UPC + k]).then_inc(ld_ub[k % 3], 16)

            def out_chunk(j, par, more):
                sp.wait_ge(y_ready, at((j * 2 + par) * TPC + TPC - 1))
                sp.dma_start(out_dst[j * 2 + par], HB[:, par]).then_inc(st_out[par], 16)
                if more:
                    sp.wait_ge(st_out[par], (j + 2) * 16)
                    sp.dma_start(HB[:, par], h_dram[j * 2 + par + 2]).then_inc(ld_hb[par], 16)

            up_units(0)
            with sp.Fori(0, CHUNKS // 2 - 1) as j:
                up_units(j * 2 + 1)
                out_chunk(j, 0, True)
                up_units(j * 2 + 2)
                out_chunk(j, 1, True)
            up_units(CHUNKS - 1)
            for par in range(2):
                out_chunk(CHUNKS // 2 - 1, par, False)
            for par in range(2):
                sp.wait_ge(st_out[par], (CHUNKS // 2 + 1) * 16)


PS_CXT = [1, 8]
PS_KV = [2, 9]
PS_KT = [3, 10]
PS_VW = [[4, 5, 6, 7], [11, 12, 13, 14]]
N_ATTN = 7 + NH
N_SMALL = 2
DVE_ABS, ACT_ABS = (2, 5), (0, 1, 3, 4)


def late_group(i):
    return isinstance(i, int) and i == 0


ACT_EVENTS = {"whi_ready", "wt_ready", "xtc_ready", "exp_ready", "pt_ready", "xt_ready", "stg_ready", "gi_ready",
              "sig_ready", "sig2_ready", "ua_ready", "pab_ready", "ui_ready"}
PE_EVENTS = {"w_transposed", "xn_transposed", "q_ready", "scores_ready", "probs_transposed", "attn_ready",
             "x_transposed", "mm_ready", "down_ready"}
DVE_EVENTS = {"wq_ready", "ws_ready", "wlo_ready", "xn_ready", "roped", "masked", "max_ready", "inv_ready",
              "probs_ready", "h_ready", "h_stats", "xi_ready", "xh_ready", "xl_ready", "stg_peaked",
              "sq_ready", "g_kept", "gg_peaked", "gg_folded", "sq2_ready", "gg_ready", "pab2_ready", "p_peaked", "p_folded",
              "oi_ready", "oh_ready", "ol_ready", "y_ready"}

_INS = ["x", "ctx_1024", "mask_BxS2_bk0", "g_xattn", "g_ffn", "L0_xattn_rms_scale", "L0_xattn_q_w", "L0_xattn_kv_w",
        "L0_xattn_out_w", "L0_ffn_w_gate", "L0_ffn_w_up", "L0_ffn_w_down"]


def _rope_tables():
    import numpy as np
    half = HD // 2
    exponent = np.float32(2.0 / HD) * np.arange(half, dtype=np.float32)
    timescale = np.power(np.float32(10000.0), exponent).astype(np.float32)

    def table(first, count):
        radians = np.arange(first, first + count, dtype=np.float32)[:, None] / timescale
        r = radians.astype(np.float64)
        return np.cos(r), np.sin(r)

    c, s = table(CTX, SEQ)
    q = np.stack([np.concatenate([c, c], 1), np.concatenate([s, s], 1)], 0) * HD ** -0.5
    q = q.reshape(2, SEQ // CHUNK, CHUNK, HD).transpose(1, 3, 0, 2)
    q = np.concatenate([q] * BATCH, 0)
    c, s = table(0, CTX)
    return np.ascontiguousarray(q, np.float32), np.ascontiguousarray(np.stack([c, s], 1), np.float32)


def kernel(**inputs):
    import numpy as np
    import concourse.bacc as bacc
    from concourse.bass_utils import run_bass_kernel_spmd

    nc = bacc.Bacc("TRN2", target_bir_lowering=False, num_devices=1)
    arrays, args = {}, []
    rope_q, rope_k = _rope_tables()
    given = [(n, np.ascontiguousarray(inputs[n])) for n in _INS] + [("rope_q", rope_q), ("rope_k", rope_k)]
    for name, a in given:
        arrays[f"in_{name}"] = a
        args.append(nc.dram_tensor(f"in_{name}", a.shape, mybir.dt.from_np(a.dtype), kind="ExternalInput").ap())
    args.append(nc.dram_tensor("out_0", (BATCH, SEQ, D), mybir.dt.float32, kind="ExternalOutput").ap())
    flamingo_kernel(nc, *args)
    r = run_bass_kernel_spmd(nc, [arrays], core_ids=[0])
    return r.results[0]["out_0"]
```

```python
import concourse.bass as bass
from concourse import mybir
from contextlib import ExitStack

P = 128
BATCH, SEQ, D = 2, 2048, 512
CTX, NH, HD = 128, 4, 128
FF = 1536
BLOCK = 32
KD = D // P
OT = FF // P
TILES = BATCH * SEQ // P
CHUNK = 512
TPC = CHUNK // P
CHUNKS = TILES // TPC
PAIR = 2 * CHUNK
UPC = OT // 2
UNITS = CHUNKS * UPC
QMAX = 32767.0
QMAX4 = 7.0
TINY = 1e-12
MASK_FILL = -2.3819763e38
LEAD = 8
KB = 1024


def at(n):
    return n + 1 + LEAD


def flamingo_kernel(nc, x, ctx_in, mask, g_xattn, g_ffn, rms_scale, q_w, kv_w, out_w, w_gate, w_up, w_down,
                    rope_q, rope_k, out):
    F32, F16, I16, U16, I32, U8 = (mybir.dt.float32, mybir.dt.float16, mybir.dt.int16, mybir.dt.uint16,
                                   mybir.dt.int32, mybir.dt.uint8)
    ALU, ACT, AX = mybir.AluOpType, mybir.ActivationFunctionType, mybir.AxisListType
    SIZE = {F32: 4, F16: 2, I16: 2, U16: 2, I32: 4, U8: 1}

    h_dram = nc.dram_tensor("h_scratch", (CHUNKS, P, TPC, D), F32, kind="Internal").ap()
    g_dram = nc.dram_tensor("gate_scratch", (UNITS, P, PAIR), F32, kind="Internal").ap()
    u_dram = nc.dram_tensor("up_scratch", (UNITS, P, PAIR), F32, kind="Internal").ap()
    wg_dram = nc.dram_tensor("w_gate_parts", (OT, P, 2, KD, P), F16, kind="Internal").ap()
    wu_dram = nc.dram_tensor("w_up_parts", (OT, P, 2, KD, P), F16, kind="Internal").ap()
    wd_dram = nc.dram_tensor("w_down_parts", (OT, P, 2, D), F16, kind="Internal").ap()

    es = ExitStack()
    with es:
        arena = es.enter_context(nc.sbuf_tensor("arena", [P, 207 * KB // 4], F32))
        banks = [es.enter_context(nc.psum_tensor(f"bank{i}", [P, 512], F32)) for i in range(8)]

        def sem(name):
            return es.enter_context(nc.semaphore(name))

        def view(at_byte, shape, dt):
            n = SIZE[dt]
            for s in shape:
                n *= s
            assert at_byte % 4 == 0 and n % 4 == 0 and at_byte + n <= 207 * KB, (at_byte, shape)
            v = arena[:, at_byte // 4:(at_byte + n) // 4]
            if dt != F32:
                v = v.bitcast(dt)
            if len(shape) > 1:
                names = "abcde"[:len(shape)]
                v = v.rearrange(f"p ({' '.join(names)}) -> p {' '.join(names)}",
                                **{c: s for c, s in zip(names[1:], shape[1:])})
            return v

        H = view(0, [TILES, D], F32)
        class Small:
            top = 204 * KB
            end = 207 * KB

        def small(shape, dt=F32):
            n = SIZE[dt]
            for s in shape:
                n *= s
            if n % 4:
                v = view(Small.top, [2], dt)[:, 0:1]
                n = 4
            else:
                v = view(Small.top, shape, dt)
            Small.top += n
            assert Small.top <= Small.end
            return v

        ident = small([P])
        ident16 = small([P], F16)
        gates = small([2])
        w_row, w_all = small([3]), small([3])
        w_pow, w_scale, w_undo = small([3]), small([3]), small([3])
        x_row, x_all = small([1]), small([1])
        g_row, g_all = small([2]), small([2])
        gg_row, gg_all = small([1]), small([1])
        u_row, u_all = small([1]), small([1])
        p_row, p_all = small([1]), small([1])
        s_x, s_g, s_gg, s_u, s_p = (small([1]) for _ in range(5))
        i_x, i_g, i_gg, i_u, i_p = (small([1]) for _ in range(5))
        d_g, d_u = small([1]), small([1])
        c_g, c_u, c_gg, c_p, c_out = (small([1]) for _ in range(5))
        tmp1 = small([4])
        g_peak, u_peak, g_top = (small([UNITS]) for _ in range(3))
        top_i, top_sq = small([1], I16), small([1], U16)
        top_sig, top_g = small([1]), small([1])
        gg_acc, gg_run = small([2 * UPC]), small([2 * UPC])
        p_acc, p_peak = small([2]), small([UNITS])
        WRAW = view(72 * KB, [3, OT, D], F32)
        W_Q = view(160 * KB, [3, D], I16)
        W_F = view(163 * KB, [3, D], F32)
        W_HI = view(169 * KB, [3, D], F16)
        W_LO = view(172 * KB, [3, D], F16)
        W_T = view(175 * KB, [3, 2, KD, P], F16)
        W_BMAX = view(186 * KB, [3 * OT, D // BLOCK], F32)
        W_RECIP = view(186 * KB + 2304, [3 * OT, D // BLOCK], F32)
        W_BSCALE = view(186 * KB + 4608, [3 * OT, D // BLOCK], F32)
        STATS = 64 * KB
        BN_X = view(STATS, [TILES, 6], F32)
        BN_H = view(STATS + 768, [TILES, 6], F32)
        st = [view(STATS + 1536 + 128 * i, [TILES], F32) for i in range(20)]
        mean_x, var_x, r_x, ra, rb, rc, rd, hmax, hmin, mean_h, var_h, r_h, c_h, nmr_x = st[:14]
        bn_c = view(STATS + 1536 + 2560, [BATCH, 6], F32)
        QC = view(72 * KB, [2, NH, CHUNK], F32)
        QS = view(88 * KB, [2, NH, CHUNK], F32)
        XN = view(104 * KB, [TPC, D], F32)
        VWP = view(112 * KB, [BATCH, 2, NH, D], F16)
        QWP = view(128 * KB, [2, KD, NH, HD], F16)
        XTC = view(136 * KB, [2, 2, KD, CHUNK], F16)
        VW = view(72 * KB, [BATCH, NH, D], F32)
        SC = view(160 * KB, [2, NH, CTX], F32)
        EX = view(164 * KB, [2, NH, CTX], F32)
        PT = view(168 * KB, [2, 2, NH, P], F16)
        QW = view(172 * KB, [KD, NH, HD], F32)
        KT1 = view(180 * KB, [BATCH, CTX], F32)
        KT2 = view(181 * KB, [BATCH, CTX], F32)
        KVW = view(182 * KB, [2, KD, HD], F32)
        OW = view(186 * KB, [NH, D], F32)
        TAB = view(186 * KB, [2, 2, CHUNK], F32)
        CX = view(194 * KB, [BATCH, D], F32)
        CXT = view(198 * KB, [KD, CTX], F32)
        VT = view(200 * KB, [CTX], F32)
        KN = view(200 * KB + 512, [CTX], F32)
        KR = view(201 * KB, [CTX], F32)
        KR2 = view(201 * KB + 512, [CTX], F32)
        KM = view(202 * KB, [2, HD // 2], F32)
        RK = view(202 * KB + 512, [2, HD // 2], F32)
        MB = view(203 * KB, [BATCH, CTX], F32)
        a0 = STATS + 1536 + 2560 + 64
        MU8 = view(a0, [BATCH, CTX], U8)
        RMS = view(a0 + 256, [KD], F32)
        st_c = [view(a0 + 288 + 8 * i, [BATCH], F32) for i in range(6)]
        NMX = view(a0 + 352, [2, NH], F32)
        RSUM = view(a0 + 384, [2, NH], F32)
        RINV = view(a0 + 416, [2, NH], F32)
        v_row, v_all = view(a0 + 448, [2], F32), view(a0 + 456, [2], F32)
        v_pow, v_scale, v_undo = (view(a0 + 464 + 8 * i, [2], F32) for i in range(3))
        q_undo, o_gate = view(a0 + 488, [1], F32), view(a0 + 492, [1], F32)
        XT = view(72 * KB, [CHUNKS, 2, KD, CHUNK], F16)
        G = view(0, [UNITS, PAIR], I16)
        W = view(136 * KB, [OT, 2, KD, P], F16)
        STG = view(160 * KB, [3, 2, CHUNK], F32)
        XI = view(172 * KB, [TPC, D], I16)
        XH = view(176 * KB, [TPC, D], F16)
        XL = view(180 * KB, [TPC, D], F16)
        GB = view(172 * KB, [6, PAIR], F32)
        SQ = view(196 * KB, [2, PAIR], U16)
        GQ = view(200 * KB, [2, PAIR], I16)
        LU = view(96 * KB, [UPC, PAIR], F32)
        UR = view(172 * KB, [6, PAIR], F32)
        UA = view(196 * KB, [3, PAIR], I16)
        AB = view(128 * KB, [3, PAIR], I16)
        OH = view(96 * KB, [2, OT, CHUNK], F16)
        OL = view(120 * KB, [2, OT, CHUNK], F16)
        WD = view(144 * KB, [OT, 2, D], F16)
        UB = view(168 * KB, [3, PAIR], F32)
        HB = view(180 * KB, [2, TPC, D], F32)
        UI = view(196 * KB, [2, PAIR], I16)
        OI = view(200 * KB, [2, PAIR], I16)

        def col(v, n):
            return v[:, bass.ds(n, 1)]

        bank16 = [b[:, :].bitcast(F16).rearrange("p (a k c) -> p a k c", a=2, k=KD) for b in banks]
        bank4 = [b[:, :].rearrange("p (a c) -> p a c", a=4) for b in banks]
        TB, QB, LB, PB, OB = (0, 1), (2, 3), (4, 5), 6, 7
        XB = (6, 7)
        MM = 6

        ld_w, ld_small, ld_attn, ld_wd, ld_wg = (sem(n) for n in
                                                 ("ld_w", "ld_small", "ld_attn", "ld_wd", "ld_wg"))
        ld_x = [sem(f"ld_x{c}") for c in range(CHUNKS)]
        ld_tab = [sem(f"ld_tab{i}") for i in range(2)]
        ld_wu = [sem(f"ld_wu{i}") for i in range(3)]
        ld_gb = [sem(f"ld_gb{i}") for i in range(6)]
        ld_ur = [sem(f"ld_ur{i}") for i in range(6)]
        ld_ub = [sem(f"ld_ub{i}") for i in range(3)]
        ld_hb = [sem(f"ld_hb{i}") for i in range(2)]
        st_wt = [sem(f"st_wt{i}") for i in range(3)]
        st_h, st_lu = sem("st_h"), sem("st_lu")
        st_stg = [sem(f"st_stg{i}") for i in range(3)]
        st_out = [sem(f"st_out{i}") for i in range(2)]
        idents = sem("idents")
        steps = sem("vector_steps")
        asteps = sem("scalar_steps")
        psteps = sem("tensor_steps")
        peaks = sem("peaks_over_partitions")
        counted = {}

        def event(name):
            counted[name] = sem(name)
            return counted[name]

        wq_ready, ws_ready, whi_ready, wlo_ready, wtrans, wt_ready = (event(n) for n in (
            "wq_ready", "ws_ready", "whi_ready", "wlo_ready", "w_transposed", "wt_ready"))
        xn_ready, xn_trans, xtc_hi, xtc_lo, q_ready, roped = (event(n) for n in (
            "xn_ready", "xn_transposed", "xtc_hi", "xtc_lo", "q_ready", "roped"))
        scores_ready, masked, max_ready, exp_ready, inv_ready, probs_ready = (event(n) for n in (
            "scores_ready", "masked", "max_ready", "exp_ready", "inv_ready", "probs_ready"))
        probs_trans, pt_hi, pt_lo, attn_ready, h_ready, h_stats = (event(n) for n in (
            "probs_transposed", "pt_hi", "pt_lo", "attn_ready", "h_ready", "h_stats"))
        xi_ready, xh_ready, xl_ready, x_trans, xt_ready = (event(n) for n in (
            "xi_ready", "xh_ready", "xl_ready", "x_transposed", "xt_ready"))
        mm_ready, stg_ready, stg_peaked = (event(n) for n in ("mm_ready", "stg_ready", "stg_peaked"))
        gi_ready, sig_ready, sq_ready, g_kept, gg_peaked, gg_folded = (event(n) for n in (
            "gi_ready", "sig_ready", "sq_ready", "g_kept", "gg_peaked", "gg_folded"))
        sig2_ready, sq2_ready, gg_ready = (event(n) for n in ("sig2_ready", "sq2_ready", "gg_ready"))
        ua_ready, pab_ready, pab2_ready, p_peaked, p_folded = (event(n) for n in (
            "ua_ready", "pab_ready", "pab2_ready", "p_peaked", "p_folded"))
        ui_ready, oi_ready, oh_ready, ol_ready, down_ready, y_ready = (event(n) for n in (
            "ui_ready", "oi_ready", "oh_ready", "ol_ready", "down_ready", "y_ready"))

        block = es.enter_context(nc.Block())
        marks = {}

        w_src = [w_gate.rearrange("(t p) d -> p t d", p=P), w_up.rearrange("(t p) d -> p t d", p=P),
                 w_down.rearrange("(r p) (s d) -> p r s d", p=P, d=D)]
        x_src = x.rearrange("b (c t p) d -> (b c) p t d", p=P, t=TPC)
        out_dst = out.rearrange("b (c t p) d -> (b c) p t d", p=P, t=TPC)

        def ahead(j, i, d):
            if isinstance(j, int) and 8 * j + i + d >= TILES:
                return None
            e, tt = divmod(i + d, TPC)
            return j * 2 + e, e % 2, tt, (j + e // 2) // 2

        @block.vector
        def _(dve):
            for name, s in counted.items():
                if name in DVE_EVENTS:
                    dve.sem_inc(s, LEAD)
            n_steps = [0]

            def step(ins, mark=None):
                n_steps[0] += 1
                ins.then_inc(steps, 1)
                dve.wait_ge(steps, n_steps[0])
                if mark:
                    marks[mark] = n_steps[0]

            def rsqrt(y, a, root, t, mark, act_step):
                marks[mark] = n_steps[0]
                dve.wait_ge(asteps, act_step)
                step(nc.vector.reciprocal(y, root))
                step(nc.vector.tensor_tensor(t, y, y, ALU.mult))
                step(nc.vector.tensor_tensor(t, t, a, ALU.mult))
                step(nc.vector.tensor_scalar(t, t, -0.5, 1.5, ALU.mult, ALU.add))
                step(nc.vector.tensor_tensor(y, y, t, ALU.mult))

            def moments(bn, mean, var, a, b):
                step(nc.vector.tensor_tensor(a, bn[:, :, 1], bn[:, :, 4], ALU.add))
                step(nc.vector.tensor_scalar(mean, a, 0.5, None, ALU.mult))
                step(nc.vector.tensor_tensor(a, bn[:, :, 1], bn[:, :, 4], ALU.subtract))
                step(nc.vector.tensor_tensor(a, a, a, ALU.mult))
                step(nc.vector.tensor_tensor(b, bn[:, :, 2], bn[:, :, 5], ALU.add))
                step(nc.vector.tensor_scalar(b, b, 1.0 / D, None, ALU.mult))
                step(nc.vector.scalar_tensor_tensor(var, a, 0.25, b, ALU.mult, ALU.add))

            def scale_of(s, inv, peak, qmax):
                step(nc.vector.tensor_scalar(s, peak, 1.0 / qmax, TINY, ALU.mult, ALU.max))
                step(nc.vector.reciprocal(inv, s))

            def power_scale(peak, power, scale, undo):
                step(nc.vector.tensor_scalar(power, peak, 1e-30, None, ALU.max))
                step(nc.vector.tensor_scalar(power.bitcast(I32), power.bitcast(I32), 0x7F800000, None,
                                             ALU.bitwise_and))
                step(nc.vector.reciprocal(scale, power))
                step(nc.vector.tensor_scalar(scale, scale, 16384.0, None, ALU.mult))
                step(nc.vector.tensor_scalar(undo, power, 1.0 / 16384.0, None, ALU.mult))

            for m in range(3):
                dve.wait_ge(ld_w, 48)
                step(nc.vector.tensor_reduce(
                    W_BMAX[:, m * OT:(m + 1) * OT, :].rearrange("p t b -> p (t b)"),
                    WRAW[:, m].rearrange("p t (b e) -> p (t b) e", e=BLOCK), axis=AX.X, op=ALU.max,
                    apply_absolute_value=True))
                step(nc.vector.tensor_reduce(w_row[:, m:m + 1], W_BMAX[:, m * OT:(m + 1) * OT, :],
                                             axis=AX.XY, op=ALU.max))
            marks["w_row"] = n_steps[0]
            step(nc.vector.tensor_scalar(W_BSCALE, W_BMAX, 1.0 / QMAX4, TINY, ALU.mult, ALU.max))
            step(nc.vector.reciprocal(W_RECIP, W_BSCALE))
            dve.wait_ge(peaks, 1)
            power_scale(w_all, w_pow, w_scale, w_undo)
            for m in range(3):
                step(nc.vector.tensor_scalar(W_BSCALE[:, m * OT:(m + 1) * OT, :], W_BSCALE[:, m * OT:(m + 1) * OT, :],
                                             w_scale[:, m:m + 1], None, ALU.mult))

            def by_block(v):
                return v.rearrange("p (b e) -> p b e", e=BLOCK)

            for m in range(3):
                with dve.Fori(0, OT // 3) as j:
                    for s in range(3):
                        t = j * 3 + s
                        n = t + m * OT
                        recip = W_RECIP[:, n, :].unsqueeze(2).broadcast_to([P, D // BLOCK, BLOCK])
                        scale = W_BSCALE[:, n, :].unsqueeze(2).broadcast_to([P, D // BLOCK, BLOCK])
                        nc.vector.tensor_tensor(by_block(W_Q[:, s]), by_block(WRAW[:, m, t, :]), recip,
                                                ALU.mult).then_inc(wq_ready, 1)
                        dve.wait_ge(wq_ready, at(n))
                        nc.vector.tensor_tensor(by_block(W_F[:, s]), by_block(W_Q[:, s]), scale,
                                                ALU.mult).then_inc(ws_ready, 1)
                    for s in range(3):
                        n = j * 3 + s + m * OT
                        dve.wait_ge(ws_ready, at(n))
                        dve.wait_ge(whi_ready, at(n))
                        dve.wait_ge(wtrans, at(n - 3))
                        nc.vector.tensor_tensor(W_LO[:, s], W_F[:, s], W_HI[:, s],
                                                ALU.subtract).then_inc(wlo_ready, 1)

            for c in range(CHUNKS):
                dve.wait_ge(ld_x[c], 16)
                for tt in range(TPC):
                    n_steps[0] += 1
                    nc.vector.bn_stats(BN_X[:, c * TPC + tt, :], H[:, c * TPC + tt, :]).then_inc(steps, 1)
            dve.wait_ge(steps, n_steps[0])
            moments(BN_X, mean_x, var_x, ra, rb)
            step(nc.vector.tensor_scalar(ra, var_x, 1e-5, None, ALU.add))
            rsqrt(rc, ra, rb, rd, "var_x", 2)
            step(nc.vector.tensor_tensor(ra, rc, rc, ALU.mult))
            step(nc.vector.tensor_tensor(ra, ra, var_x, ALU.mult))
            step(nc.vector.tensor_scalar(ra, ra, 1e-6, None, ALU.add))
            rsqrt(r_x, ra, rb, rd, "ms_x", 3)
            step(nc.vector.tensor_tensor(r_x, r_x, rc, ALU.mult))
            step(nc.vector.scalar_tensor_tensor(nmr_x, mean_x, -1.0, r_x, ALU.mult, ALU.mult), "r_x")
            dve.wait_ge(ld_attn, 16 * N_ATTN)
            for b in range(BATCH):
                step(nc.vector.bn_stats(bn_c[:, b, :], CX[:, b, :]))
            mc, vc, cc, ca, cb, cd = st_c
            moments(bn_c, mc, vc, ca, cb)
            step(nc.vector.tensor_tensor(ca, mc, mc, ALU.mult))
            step(nc.vector.tensor_tensor(ca, ca, vc, ALU.add))
            step(nc.vector.tensor_scalar(ca, ca, 1e-6, None, ALU.add))
            rsqrt(cc, ca, cb, cd, "ms_c", 4)
            for b in range(BATCH):
                step(nc.vector.tensor_scalar(CX[:, b, :], CX[:, b, :], cc[:, b:b + 1], None, ALU.mult))
            marks["cx"] = n_steps[0]
            step(nc.vector.tensor_scalar(RMS, RMS, 1.0, None, ALU.add))
            for k in range(KD):
                step(nc.vector.tensor_scalar(QW[:, k], QW[:, k], RMS[:, k:k + 1], None, ALU.mult))
                step(nc.vector.tensor_scalar(KVW[:, :, k], KVW[:, :, k], RMS[:, k:k + 1], None, ALU.mult))
            marks["weights"] = n_steps[0]
            step(nc.vector.tensor_reduce(v_row[:, 0:1], QW, axis=AX.XYZ, op=ALU.max, apply_absolute_value=True),
                 "qw_row")
            dve.wait_ge(peaks, 2)
            power_scale(v_all[:, 0:1], v_pow[:, 0:1], v_scale[:, 0:1], v_undo[:, 0:1])
            marks["qw_scale"] = n_steps[0]
            step(nc.vector.tensor_scalar(q_undo, v_undo[:, 0:1], 1.0 / XN_SCALE, None, ALU.mult))
            dve.wait_ge(asteps, AS_QWH)
            step(nc.vector.scalar_tensor_tensor(QWP[:, 1], QW, v_scale[:, 0:1], QWP[:, 0], ALU.mult,
                                                ALU.subtract), "qwl")
            step(nc.vector.tensor_copy(MB, MU8))
            step(nc.vector.tensor_scalar(MB, MB, 1.0, -MASK_FILL, ALU.subtract, ALU.mult))
            HH = HD // 2
            for b in range(BATCH):
                dve.wait_ge(psteps, PS_CXT[b])
                step(nc.vector.tensor_copy(CXT, bank4[0]), f"cxt{b}")
                dve.wait_ge(psteps, PS_KV[b])
                step(nc.vector.tensor_copy(KN, banks[2][:, 0:CTX]))
                step(nc.vector.tensor_copy(VT, banks[3][:, 0:CTX]), f"vt{b}")
                kcos, ksin = RK[:, 0], RK[:, 1]
                step(nc.vector.tensor_tensor(KR[:, 0:HH], KN[:, 0:HH], kcos, ALU.mult))
                step(nc.vector.tensor_tensor(KM[:, 0], KN[:, HH:], ksin, ALU.mult))
                step(nc.vector.tensor_tensor(KR[:, 0:HH], KR[:, 0:HH], KM[:, 0], ALU.subtract))
                step(nc.vector.tensor_tensor(KR[:, HH:], KN[:, HH:], kcos, ALU.mult))
                step(nc.vector.tensor_tensor(KM[:, 1], KN[:, 0:HH], ksin, ALU.mult))
                step(nc.vector.tensor_tensor(KR[:, HH:], KR[:, HH:], KM[:, 1], ALU.add))
                step(nc.vector.tensor_copy(KR2[:, 0:HH], KR[:, HH:]))
                step(nc.vector.tensor_scalar(KR2[:, HH:], KR[:, 0:HH], -1.0, None, ALU.mult), f"kr{b}")
                dve.wait_ge(psteps, PS_KT[b])
                step(nc.vector.tensor_copy(KT1[:, b], bank4[4][:, 0, :]))
                step(nc.vector.tensor_copy(KT2[:, b], bank4[4][:, 1, :]), f"kt{b}")
                for n in range(NH):
                    dve.wait_ge(psteps, PS_VW[b][n])
                    step(nc.vector.tensor_copy(VW[:, b, n, :], banks[6 + n % 2][:, :]), f"vw{b}{n}")

            def xt_low(c, par, tt):
                n = c * TPC + tt
                dve.wait_ge(xtc_hi, at(n))
                part = XTC[:, par, :, :, tt * P:(tt + 1) * P]
                nc.vector.scalar_tensor_tensor(part[:, 1], bank4[TB[tt % 2]], XN_SCALE, part[:, 0], ALU.mult,
                                               ALU.subtract).then_inc(xtc_lo, 1)

            def mask_and_max(c, tt, b):
                m, s = c * TPC + tt, tt % 2
                dve.wait_ge(scores_ready, at(m))
                dve.wait_ge(exp_ready, at(m - 2))
                nc.vector.tensor_tensor(SC[:, s], bank4[LB[s]],
                                        MB[:, b, :].unsqueeze(1).broadcast_to([P, NH, CTX]),
                                        ALU.add).then_inc(masked, 1)
                dve.wait_ge(masked, at(m))
                nc.vector.tensor_reduce(NMX[:, s, :], SC[:, s], axis=AX.X, op=ALU.max,
                                        negate=True).then_inc(max_ready, 1)

            def normalise(c, tt):
                m, s = c * TPC + tt, tt % 2
                dve.wait_ge(exp_ready, at(m))
                nc.vector.reciprocal(RINV[:, s, :], RSUM[:, s, :]).then_inc(inv_ready, 1)
                dve.wait_ge(inv_ready, at(m))
                nc.vector.tensor_tensor(EX[:, s], EX[:, s], RINV[:, s, :].unsqueeze(2).broadcast_to([P, NH, CTX]),
                                        ALU.mult).then_inc(probs_ready, 1)

            def probs_low(c, tt):
                m, s = c * TPC + tt, tt % 2
                dve.wait_ge(pt_hi, at(m))
                nc.vector.scalar_tensor_tensor(PT[:, s, 1], bank4[PB], PROB_SCALE, PT[:, s, 0], ALU.mult,
                                               ALU.subtract).then_inc(pt_lo, 1)

            def rope(c, par, n, turn):
                q = c * NH + n
                dve.wait_ge(q_ready, at(q))
                if n == 0:
                    dve.wait_ge(ld_tab[par], (turn + 1) * 16)
                    dve.wait_ge(scores_ready, at(c * TPC - TPC - 1))
                for buf, k in ((QC, 0), (QS, 1)):
                    last = nc.vector.scalar_tensor_tensor(buf[:, par, n, :], banks[QB[n % 2]][:, :], q_undo,
                                                          TAB[:, par, k, :], ALU.mult, ALU.mult)
                last.then_inc(roped, 1)

            def residual(c, tt):
                m = c * TPC + tt
                dve.wait_ge(attn_ready, at(m))
                nc.vector.scalar_tensor_tensor(H[:, m, :], banks[OB][:, :], o_gate, H[:, m, :],
                                               ALU.mult, ALU.add).then_inc(h_ready, 1)

            def statistics(c, tt):
                m = c * TPC + tt
                dve.wait_ge(h_ready, at(m))
                nc.vector.bn_stats(BN_H[:, m, :], H[:, m, :])
                nc.vector.tensor_reduce(col(hmax, m), H[:, m, :], axis=AX.X, op=ALU.max)
                nc.vector.tensor_reduce(col(hmin, m), H[:, m, :], axis=AX.X, op=ALU.min).then_inc(h_stats, 1)

            def slot(j, i):
                c, par, tt, b = ahead(j, i, 0)
                nxt, row, head = ahead(j, i, 1), ahead(j, i, ROW_AHEAD), ahead(j, i, HEAD_AHEAD)
                if nxt:
                    mask_and_max(nxt[0], nxt[2], nxt[3])
                probs_low(c, tt)
                if row:
                    xt_low(*row[:3])
                if nxt:
                    normalise(nxt[0], nxt[2])
                if head:
                    rope(*head[:3], j + (i + HEAD_AHEAD) // (2 * NH))
                residual(c, tt)
                statistics(c, tt)

            for tt in range(TPC):
                xt_low(0, 0, tt)
            step(nc.vector.tensor_reduce(v_row[:, 1:2], VW, axis=AX.XYZ, op=ALU.max, apply_absolute_value=True),
                 "vw_row")
            dve.wait_ge(peaks, 3)
            power_scale(v_all[:, 1:2], v_pow[:, 1:2], v_scale[:, 1:2], v_undo[:, 1:2])
            marks["vw_scale"] = n_steps[0]
            dve.wait_ge(asteps, 1)
            step(nc.vector.tensor_scalar(o_gate, v_undo[:, 1:2], gates[:, 0:1], 1.0 / PROB_SCALE, ALU.mult,
                                         ALU.mult))
            for b in range(BATCH):
                dve.wait_ge(asteps, AS_VWH + b)
                step(nc.vector.scalar_tensor_tensor(VWP[:, b, 1], VW[:, b], v_scale[:, 1:2], VWP[:, b, 0],
                                                    ALU.mult, ALU.subtract))
            marks["vwl"] = n_steps[0]
            for n in range(NH):
                rope(0, 0, n, 0)
            for tt in range(TPC):
                xt_low(1, 1, tt)
            rope(1, 1, 0, 0)
            xt_low(2, 0, 0)
            mask_and_max(0, 0, 0)
            normalise(0, 0)
            with dve.Fori(0, CHUNKS // 2 - 2) as j:
                for i in range(2 * TPC):
                    slot(j, i)
            for j in (CHUNKS // 2 - 2, CHUNKS // 2 - 1):
                for i in range(2 * TPC):
                    slot(j, i)

            dve.wait_ge(h_stats, at(TILES - 1))
            moments(BN_H, mean_h, var_h, ra, rb)
            step(nc.vector.tensor_scalar(ra, var_h, 1e-5, None, ALU.add))
            rsqrt(r_h, ra, rb, rd, "var_h", AS_VARH)
            step(nc.vector.tensor_tensor(ra, hmax, mean_h, ALU.subtract))
            step(nc.vector.tensor_tensor(rb, mean_h, hmin, ALU.subtract))
            step(nc.vector.tensor_tensor(ra, ra, rb, ALU.max))
            step(nc.vector.tensor_tensor(ra, ra, r_h, ALU.mult))
            step(nc.vector.tensor_reduce(x_row, ra, axis=AX.X, op=ALU.max), "x_row")
            dve.wait_ge(peaks, 4)
            scale_of(s_x, i_x, x_all, QMAX)
            step(nc.vector.tensor_scalar(c_h, r_h, i_x, None, ALU.mult))
            step(nc.vector.tensor_scalar(d_g, w_undo[:, 0:1], s_x, None, ALU.mult))
            step(nc.vector.tensor_scalar(d_u, w_undo[:, 1:2], s_x, None, ALU.mult))
            step(nc.vector.memset(gg_run, 0.0))
            step(nc.vector.memset(p_acc, 0.0))

            def quantise_row(n, s):
                dve.wait_ge(x_trans, at(n - TPC))
                nc.vector.tensor_scalar(XI[:, s, :], H[:, n, :], col(mean_h, n), col(c_h, n),
                                        ALU.subtract, ALU.mult).then_inc(xi_ready, 1)
                dve.wait_ge(xi_ready, at(n))
                nc.vector.tensor_copy(XH[:, s, :], XI[:, s, :]).then_inc(xh_ready, 1)
                dve.wait_ge(xh_ready, at(n))
                nc.vector.tensor_tensor(XL[:, s, :], XI[:, s, :], XH[:, s, :], ALU.subtract).then_inc(xl_ready, 1)

            def peak_of(r, k, table, top=None, late=False):
                dve.wait_ge(stg_ready, at(r * 2 + 1))
                unit = LU[:, k] if late else STG[:, k % 3].rearrange("p a b -> p (a b)")
                if top is not None:
                    nc.vector.tensor_reduce(top, unit, axis=AX.X, op=ALU.max)
                nc.vector.tensor_reduce(table, unit, axis=AX.X, op=ALU.max,
                                        apply_absolute_value=True).then_inc(stg_peaked, 1)

            for tt in range(TPC):
                quantise_row(tt, tt)
            for tt in range(TPC):
                quantise_row(TPC + tt, tt)

            def gate_chunk(c, rows):
                for k in range(UPC):
                    r = c * UPC + k
                    peak_of(r, k, col(g_peak, r), col(g_top, r))
                    if rows and k >= 2:
                        quantise_row((c + 2) * TPC + k - 2, k - 2)

            with dve.Fori(0, CHUNKS - 2) as c:
                gate_chunk(c, True)
            for c in (CHUNKS - 2, CHUNKS - 1):
                gate_chunk(c, False)
            dve.wait_ge(stg_peaked, at(UNITS - 1))
            step(nc.vector.tensor_reduce(g_row[:, 0:1], g_peak, axis=AX.X, op=ALU.max))
            step(nc.vector.tensor_reduce(g_row[:, 1:2], g_top, axis=AX.X, op=ALU.max), "g_row")
            dve.wait_ge(peaks, 5)
            step(nc.vector.tensor_scalar(tmp1[:, 0:1], g_all[:, 0:1], d_g, None, ALU.mult))
            scale_of(s_g, i_g, tmp1[:, 0:1], QMAX)
            step(nc.vector.tensor_scalar(c_g, i_g, d_g, None, ALU.mult), "c_g")
            dve.wait_ge(asteps, AS_TOP + 1)
            step(nc.vector.tensor_scalar(top_sq, top_sig, 65536.0, 65535.0, ALU.mult, ALU.min))
            step(nc.vector.tensor_tensor(top_g, top_i, top_sq, ALU.mult))

            with dve.Fori(0, CHUNKS // 2) as c:
                for k in range(2 * UPC):
                    q = c * (2 * UPC) + k
                    dve.wait_ge(sig_ready, at(q))
                    nc.vector.tensor_scalar(SQ[:, k % 2, :], GB[:, k % 6, :], 65536.0, 65535.0, ALU.mult,
                                            ALU.min).then_inc(sq_ready, 1)
                    if k == 0:
                        dve.wait_ge(gg_folded, at(c - 1))
                    dve.wait_ge(sq_ready, at(q))
                    nc.vector.tensor_copy(G[:, q, :], GQ[:, k % 2, :]).then_inc(g_kept, 1)
                    nc.vector.tensor_tensor_reduce(GB[:, k % 6, :], GQ[:, k % 2, :], SQ[:, k % 2, :], -1.0, 0.0,
                                                   op0=ALU.mult, op1=ALU.max,
                                                   accum_out=gg_acc[:, k:k + 1]).then_inc(gg_peaked, 1)
                    if k % 2:
                        r = c * UPC + k // 2
                        peak_of(r + UNITS, k // 2, col(u_peak, r))
                dve.wait_ge(gg_peaked, at(c * (2 * UPC) + 2 * UPC - 1))
                nc.vector.tensor_tensor(gg_run, gg_run, gg_acc, ALU.max).then_inc(gg_folded, 1)
            dve.wait_ge(gg_folded, at(CHUNKS // 2 - 1))
            step(nc.vector.tensor_reduce(gg_row, gg_run, axis=AX.X, op=ALU.max))
            step(nc.vector.tensor_tensor(gg_row, gg_row, top_g, ALU.max), "gg_row")
            dve.wait_ge(peaks, 6)
            step(nc.vector.tensor_scalar(tmp1[:, 1:2], s_g, 1.0 / 65536.0, None, ALU.mult))
            step(nc.vector.tensor_scalar(tmp1[:, 2:3], gg_all, tmp1[:, 1:2], None, ALU.mult))
            scale_of(s_gg, i_gg, tmp1[:, 2:3], QMAX)
            step(nc.vector.tensor_scalar(c_gg, i_gg, tmp1[:, 1:2], None, ALU.mult))

            def second_half(c, late=False):
                for k in range(2 * UPC):
                    q = c * (2 * UPC) + k
                    dve.wait_ge(sig2_ready, at(q))
                    nc.vector.tensor_scalar(SQ[:, k % 2, :], GB[:, k % 3, :], 65536.0, 65535.0, ALU.mult,
                                            ALU.min).then_inc(sq2_ready, 1)
                    dve.wait_ge(sq2_ready, at(q))
                    nc.vector.scalar_tensor_tensor(G[:, q, :], SQ[:, k % 2, :], c_gg, G[:, q, :], ALU.mult,
                                                   ALU.mult).then_inc(gg_ready, 1)
                    if k % 2:
                        r = c * UPC + k // 2 + UNITS // 2
                        peak_of(r + UNITS, k // 2, col(u_peak, r), late=late)

            with dve.Fori(0, CHUNKS // 2 - 1) as c:
                second_half(c)
            second_half(CHUNKS // 2 - 1, late=True)
            dve.wait_ge(stg_peaked, at(2 * UNITS - 1))
            step(nc.vector.tensor_reduce(u_row, u_peak, axis=AX.X, op=ALU.max), "u_row")
            dve.wait_ge(peaks, 7)
            step(nc.vector.tensor_scalar(tmp1[:, 0:1], u_all, d_u, None, ALU.mult))
            scale_of(s_u, i_u, tmp1[:, 0:1], QMAX)
            step(nc.vector.tensor_scalar(c_u, i_u, d_u, None, ALU.mult), "c_u")

            dve.wait_ge(gg_ready, at(UNITS - 1))
            def product_peaks(i):
                for k in range(UPC):
                    n = i * UPC + k
                    q = UNITS - UPC + k if late_group(i) else (i - 1) * UPC + k
                    up = (LU if late_group(i) else UR)[:, k]
                    s = k % 3
                    dve.wait_ge(p_peaked, at(n - 1))
                    if k in DVE_ABS:
                        nc.vector.scalar_tensor_tensor(AB[:, s, :], G[:, q, :], -1.0, G[:, q, :], ALU.mult,
                                                       ALU.max).then_inc(pab2_ready, 1)
                        dve.wait_ge(pab2_ready, at(i * len(DVE_ABS) + DVE_ABS.index(k)))
                    else:
                        dve.wait_ge(pab_ready, at(i * len(ACT_ABS) + ACT_ABS.index(k)))
                    dve.wait_ge(ua_ready, at(n))
                    nc.vector.tensor_copy(col(p_peak, n), p_acc[:, 1 - k % 2:2 - k % 2]).then_inc(p_folded, 1)
                    nc.vector.tensor_tensor_reduce(up, AB[:, s, :], UA[:, s, :], 1.0, 0.0, op0=ALU.mult,
                                                   op1=ALU.max, accum_out=p_acc[:, k % 2:k % 2 + 1]) \
                        .then_inc(p_peaked, 1)

            product_peaks(0)
            with dve.Fori(1, CHUNKS) as i:
                product_peaks(i)
            dve.wait_ge(p_peaked, at(UNITS - 1))
            dve.wait_ge(p_folded, at(UNITS - 1))
            step(nc.vector.tensor_reduce(p_row, p_peak, axis=AX.X, op=ALU.max))
            step(nc.vector.tensor_tensor(p_row, p_row, p_acc[:, 1:2], ALU.max), "p_row")
            dve.wait_ge(peaks, 8)
            step(nc.vector.tensor_tensor(tmp1[:, 0:1], s_gg, s_u, ALU.mult))
            step(nc.vector.tensor_scalar(tmp1[:, 1:2], p_all, tmp1[:, 0:1], None, ALU.mult))
            scale_of(s_p, i_p, tmp1[:, 1:2], QMAX)
            step(nc.vector.tensor_scalar(c_p, tmp1[:, 0:1], i_p, None, ALU.mult))
            step(nc.vector.tensor_scalar(c_out, s_p, w_undo[:, 2:3], None, ALU.mult))
            step(nc.vector.tensor_scalar(c_out, c_out, gates[:, 1:2], None, ALU.mult))

            def product_units(c, par):
                for k in range(UPC):
                    q, s = c * UPC + k, k % 2
                    dve.wait_ge(ui_ready, at(q))
                    nc.vector.scalar_tensor_tensor(OI[:, s, :], G[:, q, :], c_p, UI[:, s, :], ALU.mult,
                                                   ALU.mult).then_inc(oi_ready, 1)
                    oi = OI[:, s, :]
                    hi = OH[:, par, 2 * k:2 * k + 2, :].rearrange("p a b -> p (a b)")
                    lo = OL[:, par, 2 * k:2 * k + 2, :].rearrange("p a b -> p (a b)")
                    dve.wait_ge(oi_ready, at(q))
                    dve.wait_ge(down_ready, at(c * TPC - TPC - 1))
                    nc.vector.tensor_copy(hi, oi).then_inc(oh_ready, 1)
                    dve.wait_ge(oh_ready, at(q))
                    nc.vector.tensor_tensor(lo, oi, hi, ALU.subtract).then_inc(ol_ready, 1)

            def output_tiles(j, par):
                for tt in range(TPC):
                    m = (j * 2 + par) * TPC + tt
                    if tt == 0:
                        dve.wait_ge(ld_hb[par], (j + 1) * 16)
                    dve.wait_ge(down_ready, at(m))
                    nc.vector.scalar_tensor_tensor(HB[:, par, tt, :], banks[par * TPC + tt][:, :], c_out,
                                                   HB[:, par, tt, :], ALU.mult, ALU.add).then_inc(y_ready, 1)

            product_units(0, 0)
            with dve.Fori(0, CHUNKS // 2 - 1) as j:
                product_units(j * 2 + 1, 1)
                output_tiles(j, 0)
                product_units(j * 2 + 2, 0)
                output_tiles(j, 1)
            product_units(CHUNKS - 1, 1)
            output_tiles(CHUNKS // 2 - 1, 0)
            output_tiles(CHUNKS // 2 - 1, 1)

        @block.scalar
        def _(act):
            for name, s in counted.items():
                if name in ACT_EVENTS:
                    act.sem_inc(s, LEAD)
            act.wait_ge(ld_small, 16 * N_SMALL)
            nc.scalar.activation(gates, gates, ACT.Tanh).then_inc(asteps, 1)
            for m in range(3):
                with act.Fori(0, OT // 3) as j:
                    for s in range(3):
                        n = j * 3 + s + m * OT
                        act.wait_ge(ws_ready, at(n))
                        act.wait_ge(wtrans, at(n - 3))
                        nc.scalar.activation(W_HI[:, s], W_F[:, s], ACT.Copy).then_inc(whi_ready, 1)
                    for s in range(3):
                        n = j * 3 + s + m * OT
                        act.wait_ge(wtrans, at(n))
                        act.wait_ge(st_wt[s], (j + m * (OT // 3) + 1) * 16 if m < 2 else (j * 2 + 2 * (OT // 3) + 1) * 16)
                        nc.scalar.activation(W_T[:, s], bank16[s], ACT.Copy).then_inc(wt_ready, 1)
            act.wait_ge(steps, marks["var_x"])
            nc.scalar.activation(rb, ra, ACT.Sqrt).then_inc(asteps, 1)
            act.wait_ge(steps, marks["ms_x"])
            nc.scalar.activation(rb, ra, ACT.Sqrt).then_inc(asteps, 1)
            act.wait_ge(steps, marks["ms_c"])
            nc.scalar.activation(st_c[4], st_c[3], ACT.Sqrt).then_inc(asteps, 1)

            act.wait_ge(steps, marks["qw_scale"])
            nc.scalar.activation(QWP[:, 0], QW, ACT.Copy, scale=v_scale[:, 0:1]).then_inc(asteps, 1)

            def norm_tile(c, tt):
                n = c * TPC + tt
                act.wait_ge(xn_trans, at(n - TPC))
                nc.scalar.activation(XN[:, tt, :], H[:, n, :], ACT.Identity, bias=col(nmr_x, n),
                                     scale=col(r_x, n)).then_inc(xn_ready, 1)

            def take_xt(c, par, tt):
                n = c * TPC + tt
                act.wait_ge(xn_trans, at(n))
                act.wait_ge(q_ready, at(c * NH - NH - 1))
                nc.scalar.activation(XTC[:, par, 0, :, tt * P:(tt + 1) * P], bank4[TB[tt % 2]], ACT.Copy,
                                     scale=XN_SCALE).then_inc(xtc_hi, 1)

            def exps(c, tt):
                m, s = c * TPC + tt, tt % 2
                act.wait_ge(max_ready, at(m))
                act.wait_ge(probs_trans, at(m - 2))
                for n in range(NH):
                    last = nc.scalar.activation(EX[:, s, n, :], SC[:, s, n, :], ACT.Exp, bias=NMX[:, s, n:n + 1],
                                                accum_out=RSUM[:, s, n:n + 1])
                last.then_inc(exp_ready, 1)

            def take_pt(c, tt):
                m, s = c * TPC + tt, tt % 2
                act.wait_ge(probs_trans, at(m))
                act.wait_ge(attn_ready, at(m - 2))
                nc.scalar.activation(PT[:, s, 0], bank4[PB], ACT.Copy, scale=PROB_SCALE).then_inc(pt_hi, 1)

            act.wait_ge(steps, marks["r_x"])
            for c in range(2):
                for tt in range(TPC):
                    norm_tile(c, tt)
                for tt in range(TPC):
                    take_xt(c, c, tt)
                if c == 0:
                    act.wait_ge(steps, marks["vw_scale"])
                    for b in range(BATCH):
                        nc.scalar.activation(VWP[:, b, 0], VW[:, b], ACT.Copy,
                                             scale=v_scale[:, 1:2]).then_inc(asteps, 1)
            norm_tile(2, 0)
            take_xt(2, 0, 0)
            norm_tile(2, 1)
            exps(0, 0)

            def slot(j, i):
                c, par, tt, b = ahead(j, i, 0)
                nxt, row, norm = ahead(j, i, 1), ahead(j, i, ROW_AHEAD), ahead(j, i, ROW_AHEAD + 1)
                take_pt(c, tt)
                if row:
                    take_xt(*row[:3])
                if nxt:
                    exps(nxt[0], nxt[2])
                if norm:
                    norm_tile(norm[0], norm[2])

            with act.Fori(0, CHUNKS // 2 - 2) as j:
                for i in range(2 * TPC):
                    slot(j, i)
            for j in (CHUNKS // 2 - 2, CHUNKS // 2 - 1):
                for i in range(2 * TPC):
                    slot(j, i)
            act.wait_ge(steps, marks["var_h"])
            nc.scalar.activation(rb, ra, ACT.Sqrt).then_inc(asteps, 1)

            def take_x(n, c, tt):
                act.wait_ge(x_trans, at(n))
                nc.scalar.activation(XT[:, c, :, :, tt * P:(tt + 1) * P], bank16[XB[tt % 2]],
                                     ACT.Copy).then_inc(xt_ready, 1)

            def take_mm(c, o, late=False):
                n, k = c * OT + o, o // 2
                act.wait_ge(mm_ready, at(n))
                if late:
                    nc.scalar.activation(LU[:, k, bass.ts(o % 2, CHUNK)], banks[o % MM][:, :],
                                         ACT.Copy).then_inc(stg_ready, 1)
                    return
                if o % 2 == 0:
                    act.wait_ge(stg_peaked, at(c * UPC + k - 3))
                    act.wait_ge(st_stg[k % 3], (c * (UPC // 3) + k // 3 + 1) * 16)
                nc.scalar.activation(STG[:, k % 3, o % 2, :], banks[o % MM][:, :], ACT.Copy).then_inc(stg_ready, 1)

            for tt in range(TPC):
                take_x(tt, 0, tt)
            with act.Fori(0, CHUNKS - 1) as c:
                for o in range(OT):
                    take_mm(c, o)
                    if o % 3 == 2:
                        take_x((c + 1) * TPC + o // 3, c + 1, o // 3)
            for o in range(OT):
                take_mm(CHUNKS - 1, o)

            act.wait_ge(steps, marks["c_g"])
            nc.scalar.activation(top_i, g_all[:, 1:2], ACT.Copy, scale=c_g).then_inc(asteps, 1)
            act.wait_ge(asteps, AS_TOP)
            nc.scalar.activation(top_sig, top_i, ACT.Sigmoid, scale=s_g).then_inc(asteps, 1)
            with act.Fori(0, CHUNKS // 2) as c:
                for k in range(2 * UPC):
                    q = c * (2 * UPC) + k
                    act.wait_ge(ld_gb[k % 6], (c * 2 + k // 6 + 1) * 16)
                    act.wait_ge(gg_peaked, at(q - 2))
                    nc.scalar.activation(GQ[:, k % 2, :], GB[:, k % 6, :], ACT.Copy, scale=c_g).then_inc(gi_ready, 1)
                    take_mm(c + CHUNKS, k)
                    act.wait_ge(gi_ready, at(q))
                    nc.scalar.activation(GB[:, k % 6, :], GQ[:, k % 2, :], ACT.Sigmoid, scale=s_g).then_inc(sig_ready, 1)
            act.wait_ge(g_kept, at(UNITS - 1))
            def second_half(c, late=False):
                for k in range(2 * UPC):
                    q = c * (2 * UPC) + k
                    if k < 3:
                        act.wait_ge(gg_peaked, at(UNITS - 1))
                    act.wait_ge(sq2_ready, at(q - 3))
                    nc.scalar.activation(GB[:, k % 3, :], G[:, q, :], ACT.Sigmoid, scale=s_g).then_inc(sig2_ready, 1)
                    take_mm(c + CHUNKS + CHUNKS // 2, k, late=late)

            with act.Fori(0, CHUNKS // 2 - 1) as c:
                second_half(c)
            second_half(CHUNKS // 2 - 1, late=True)

            act.wait_ge(steps, marks["c_u"])
            def absolutes(i):
                for k in range(UPC):
                    n = i * UPC + k
                    q = UNITS - UPC + k if late_group(i) else (i - 1) * UPC + k
                    act.wait_ge(p_peaked, at(n - 3))
                    if k in ACT_ABS:
                        nc.scalar.activation(AB[:, k % 3, :], G[:, q, :], ACT.Abs).then_inc(pab_ready, 1)
                    if not late_group(i):
                        act.wait_ge(ld_ur[k], i * 16)
                    nc.scalar.activation(UA[:, k % 3, :], (LU if late_group(i) else UR)[:, k], ACT.Abs,
                                         scale=c_u).then_inc(ua_ready, 1)

            act.wait_ge(gg_ready, at(UNITS - 1))
            act.wait_ge(st_lu, 16 * UPC)
            absolutes(0)
            with act.Fori(1, CHUNKS) as i:
                absolutes(i)

            act.wait_ge(p_peaked, at(UNITS - 1))
            with act.Fori(0, CHUNKS) as c:
                for k in range(UPC):
                    q = c * UPC + k
                    act.wait_ge(ld_ub[k % 3], (c * 2 + k // 3 + 1) * 16)
                    act.wait_ge(oi_ready, at(q - 2))
                    nc.scalar.activation(UI[:, k % 2, :], UB[:, k % 3, :], ACT.Copy, scale=c_u).then_inc(ui_ready, 1)

        @block.tensor
        def _(pe):
            for name, s in counted.items():
                if name in PE_EVENTS:
                    pe.sem_inc(s, LEAD)
            pe.wait_ge(idents, 4)
            for m in range(3):
                with pe.Fori(0, OT // 3) as j:
                    for s in range(3):
                        n = j * 3 + s + m * OT
                        pe.wait_ge(wlo_ready, at(n))
                        pe.wait_ge(wt_ready, at(n - 3))
                        for a, part in enumerate((W_HI, W_LO)):
                            for k in range(KD):
                                last = nc.tensor.transpose(bank16[s][:, a, k, :], part[:, s, k * P:(k + 1) * P],
                                                           ident16)
                        last.then_inc(wtrans, 1)
            n_steps = [0]

            def step(ins, want):
                n_steps[0] += 1
                assert n_steps[0] == want, (n_steps, want)
                ins.then_inc(psteps, 1)

            pe.wait_ge(wt_ready, at(3 * OT - 1))
            for b in range(BATCH):
                pe.wait_ge(steps, marks["cx"] if b == 0 else marks[f"vw{b - 1}3"])
                for k in range(KD):
                    last = nc.tensor.transpose(bank4[0][:, k, :], CX[:, b, k * P:(k + 1) * P], ident)
                step(last, PS_CXT[b])
                pe.wait_ge(steps, max(marks[f"cxt{b}"], marks["weights"]))
                for k in range(KD):
                    nc.tensor.matmul(banks[2][:, 0:CTX], CXT[:, k, :], KVW[:, 0, k, :], start=k == 0, stop=k == KD - 1)
                for k in range(KD):
                    last = nc.tensor.matmul(banks[3][:, 0:CTX], KVW[:, 1, k, :], CXT[:, k, :], start=k == 0,
                                            stop=k == KD - 1)
                step(last, PS_KV[b])
                pe.wait_ge(steps, marks[f"kr{b}"])
                nc.tensor.transpose(bank4[4][:, 0, :], KR, ident)
                step(nc.tensor.transpose(bank4[4][:, 1, :], KR2, ident), PS_KT[b])
                for n in range(NH):
                    if n >= 2:
                        pe.wait_ge(steps, marks[f"vw{b}{n - 2}"])
                    step(nc.tensor.matmul(banks[6 + n % 2][:, :], VT, OW[:, n, :], start=True, stop=True), PS_VW[b][n])

            def transposes(c, tt):
                n = c * TPC + tt
                pe.wait_ge(xn_ready, at(n))
                pe.wait_ge(xtc_lo, at(n - 2))
                for k in range(KD):
                    last = nc.tensor.transpose(bank4[TB[tt % 2]][:, k, :], XN[:, tt, k * P:(k + 1) * P], ident)
                last.then_inc(xn_trans, 1)

            def query(c, par, n):
                pe.wait_ge(xtc_lo, at(c * TPC + TPC - 1))
                pe.wait_ge(roped, at(c * NH + n - 2))
                i = 0
                for a, x_part in ((0, 0), (0, 1), (1, 0)):
                    for k in range(KD):
                        last = nc.tensor.matmul(banks[QB[n % 2]][:, :], QWP[:, a, k, n, :], XTC[:, par, x_part, k, :],
                                                start=i == 0, stop=i == 3 * KD - 1)
                        i += 1
                last.then_inc(q_ready, 1)

            def scores(c, par, tt, b):
                m, s = c * TPC + tt, tt % 2
                pe.wait_ge(roped, at(c * NH + NH - 1))
                pe.wait_ge(masked, at(m - 2))
                for n in range(NH):
                    nc.tensor.matmul(bank4[LB[s]][:, n, :], QC[:, par, n, tt * P:(tt + 1) * P], KT1[:, b, :],
                                     start=True, stop=False)
                    last = nc.tensor.matmul(bank4[LB[s]][:, n, :], QS[:, par, n, tt * P:(tt + 1) * P], KT2[:, b, :],
                                            start=False, stop=True)
                last.then_inc(scores_ready, 1)

            def probs(c, tt):
                m, s = c * TPC + tt, tt % 2
                pe.wait_ge(probs_ready, at(m))
                pe.wait_ge(pt_lo, at(m - 1))
                for n in range(NH):
                    last = nc.tensor.transpose(bank4[PB][:, n, :], EX[:, s, n, :], ident)
                last.then_inc(probs_trans, 1)

            def output(c, tt, b):
                m, s = c * TPC + tt, tt % 2
                pe.wait_ge(pt_lo, at(m))
                pe.wait_ge(h_ready, at(m - 1))
                i = 0
                for a, v_part in ((0, 0), (0, 1), (1, 0)):
                    for n in range(NH):
                        last = nc.tensor.matmul(banks[OB][:, :], PT[:, s, a, n, :], VWP[:, b, v_part, n, :],
                                                start=i == 0, stop=i == 3 * NH - 1)
                        i += 1
                last.then_inc(attn_ready, 1)

            def slot(j, i):
                c, par, tt, b = ahead(j, i, 0)
                row, head, score = ahead(j, i, ROW_AHEAD), ahead(j, i, HEAD_AHEAD), ahead(j, i, 2)
                probs(c, tt)
                if row:
                    transposes(row[0], row[2])
                if head:
                    query(*head[:3])
                output(c, tt, b)
                if score:
                    scores(*score)

            for tt in range(TPC):
                transposes(0, tt)
            pe.wait_ge(steps, marks["qwl"])
            for n in range(NH):
                query(0, 0, n)
            for tt in range(TPC):
                transposes(1, tt)
            scores(0, 0, 0, 0)
            transposes(2, 0)
            query(1, 1, 0)
            scores(0, 0, 1, 0)
            pe.wait_ge(steps, marks["vwl"])
            with pe.Fori(0, CHUNKS // 2 - 2) as j:
                for i in range(2 * TPC):
                    slot(j, i)
            for j in (CHUNKS // 2 - 2, CHUNKS // 2 - 1):
                for i in range(2 * TPC):
                    slot(j, i)

            def transpose_x(n, tt):
                pe.wait_ge(xl_ready, at(n))
                pe.wait_ge(xt_ready, at(n - 2))
                for a, part in enumerate((XH, XL)):
                    for k in range(KD):
                        last = nc.tensor.transpose(bank16[XB[tt % 2]][:, a, k, :], part[:, tt, k * P:(k + 1) * P],
                                                   ident16)
                last.then_inc(x_trans, 1)

            def product(c, cx, o):
                n = c * OT + o
                pe.wait_ge(stg_ready, at(n - MM))
                i = 0
                for a, x_part in ((0, 0), (0, 1), (1, 0)):
                    for k in range(KD):
                        last = nc.tensor.matmul(banks[o % MM][:, :], W[:, o, a, k, :], XT[:, cx, x_part, k, :],
                                                start=i == 0, stop=i == 3 * KD - 1)
                        i += 1
                last.then_inc(mm_ready, 1)

            for tt in range(TPC):
                transpose_x(tt, tt)
            pe.wait_ge(ld_wg, 16)
            with pe.Fori(0, CHUNKS - 1) as c:
                pe.wait_ge(xt_ready, at(c * TPC + TPC - 1))
                for o in range(OT):
                    product(c, c, o)
                    if o % 3 == 2:
                        transpose_x((c + 1) * TPC + o // 3, o // 3)
            pe.wait_ge(xt_ready, at(TILES - 1))
            for o in range(OT):
                product(CHUNKS - 1, CHUNKS - 1, o)
            with pe.Fori(0, CHUNKS) as c:
                for o in range(OT):
                    if o % 4 == 0:
                        pe.wait_ge(ld_wu[o // 4], 16)
                    product(c + CHUNKS, c, o)

            def down(c, par):
                for tt in range(TPC):
                    m = c * TPC + tt
                    pe.wait_ge(y_ready, at(m - 2 * TPC))
                    i = 0
                    for o in range(OT):
                        if tt == 0 and o % 2 == 0:
                            pe.wait_ge(ol_ready, at(c * UPC + o // 2))
                        for part, a in ((OH, 0), (OH, 1), (OL, 0)):
                            last = nc.tensor.matmul(banks[par * TPC + tt][:, :],
                                                    part[:, par, o, tt * P:(tt + 1) * P], WD[:, o, a, :],
                                                    start=i == 0, stop=i == 3 * OT - 1)
                            i += 1
                    last.then_inc(down_ready, 1)

            pe.wait_ge(ld_wd, 16)
            pe.wait_ge(stg_ready, at(2 * CHUNKS * OT - 1))
            down(0, 0)
            down(1, 1)
            with pe.Fori(1, CHUNKS // 2) as j:
                down(j * 2, 0)
                down(j * 2 + 1, 1)

        @block.gpsimd
        def _(pool):
            pool.memset(ident, 0.0).then_inc(idents, 1)
            pool.memset(ident16, 0.0).then_inc(idents, 1)
            pool.wait_ge(idents, 2)
            for m in (ident, ident16):
                pool.affine_select(out=m, in_=m, compare_op=ALU.not_equal, fill=1.0, base=0,
                                   pattern=[[-1, P]], channel_multiplier=1).then_inc(idents, 1)
            RMAX = bass.bass_isa.ReduceOp.max
            for mark, row, all_ in (("w_row", w_row, w_all), ("qw_row", v_row[:, 0:1], v_all[:, 0:1]),
                                    ("vw_row", v_row[:, 1:2], v_all[:, 1:2]), ("x_row", x_row, x_all), ("g_row", g_row, g_all),
                                    ("gg_row", gg_row, gg_all), ("u_row", u_row, u_all), ("p_row", p_row, p_all)):
                pool.wait_ge(steps, marks[mark])
                pool.partition_all_reduce(all_, row, P, RMAX).then_inc(peaks, 1)

        @block.sync
        def _(sp):
            for s in st_wt + st_stg + st_out:
                sp.sem_inc(s, 16)
            for m in range(3):
                dst = WRAW[:, m] if m < 2 else WRAW[:, m].rearrange("p (r s) d -> p r s d", s=3)
                sp.dma_start(dst, w_src[m]).then_inc(ld_w, 16)
            sp.dma_start(gates[:, 0:1], g_xattn.partition_broadcast(P)).then_inc(ld_small, 16)
            sp.dma_start(gates[:, 1:2], g_ffn.partition_broadcast(P)).then_inc(ld_small, 16)
            for c in range(CHUNKS):
                sp.dma_start(H[:, c * TPC:(c + 1) * TPC, :], x_src[c]).then_inc(ld_x[c], 16)
            for m, dst in enumerate((wg_dram, wu_dram, wd_dram)):
                with sp.Fori(0, OT // 3) as j:
                    for s in range(3):
                        sp.wait_ge(wt_ready, at(j * 3 + s + m * OT))
                        if m < 2:
                            sp.dma_start(dst[j * 3 + s], W_T[:, s]).then_inc(st_wt[s], 16)
                        else:
                            for a in range(2):
                                sp.dma_start(dst[s * KD:(s + 1) * KD, :, a, bass.ts(j, P)]
                                             .rearrange("k p c -> p k c"), W_T[:, s, a]).then_inc(st_wt[s], 16)
            for s in range(3):
                sp.wait_ge(st_wt[s], (4 * (OT // 3) + 1) * 16)
            sp.dma_start(RMS, rms_scale.rearrange("(k p) -> p k", p=P),
                         allow_slow_non_contiguous=True).then_inc(ld_attn, 16)
            for n in range(NH):
                sp.dma_start(QW[:, :, n, :], q_w[n].rearrange("(k p) h -> p k h", p=P)).then_inc(ld_attn, 16)
            for dst, src in (
                             (KVW[:, 0], kv_w[0, 0].rearrange("(k p) h -> p k h", p=P)),
                             (KVW[:, 1], kv_w[1, 0].rearrange("(k p) h -> p k h", p=P)),
                             (OW, out_w.rearrange("n h d -> h n d")),
                             (CX, ctx_in.rearrange("b s d -> s b d")),
                             (MU8, mask.partition_broadcast(P)),
                             (RK, rope_k)):
                sp.dma_start(dst, src).then_inc(ld_attn, 16)
            sp.wait_ge(psteps, PS_VW[1][NH - 1])
            for par in range(2):
                sp.dma_start(TAB[:, par], rope_q[par]).then_inc(ld_tab[par], 16)
            with sp.Fori(0, CHUNKS // 2 - 1) as j:
                for par in range(2):
                    c = j * 2 + par
                    sp.wait_ge(roped, at(c * NH + NH - 1))
                    sp.dma_start(TAB[:, par], rope_q[c + 2]).then_inc(ld_tab[par], 16)
                    sp.wait_ge(h_ready, at(c * TPC + TPC - 1))
                    sp.dma_start(h_dram[c], H[:, bass.ds(c * TPC, TPC), :]).then_inc(st_h, 16)
            sp.wait_ge(q_ready, at(CHUNKS * NH - 1))
            sp.dma_start(W, wg_dram.rearrange("o p a k c -> p o a k c")).then_inc(ld_wg, 16)
            for c in (CHUNKS - 2, CHUNKS - 1):
                sp.wait_ge(h_ready, at(c * TPC + TPC - 1))
                sp.dma_start(h_dram[c], H[:, c * TPC:(c + 1) * TPC, :]).then_inc(st_h, 16)

            def store(c, k, dst, q):
                sp.wait_ge(stg_ready, at(c * OT + 2 * k + 1))
                sp.dma_start(dst[q], STG[:, k % 3].rearrange("p a b -> p (a b)")).then_inc(st_stg[k % 3], 16)

            with sp.Fori(0, CHUNKS - 1) as c:
                for k in range(UPC):
                    store(c, k, g_dram, c * UPC + k)
            sp.wait_ge(x_trans, at(TILES - 1))
            for s in range(3):
                sp.wait_ge(st_stg[s], 3 * 16)
            for k in range(6):
                sp.dma_start(GB[:, k, :], g_dram[k]).then_inc(ld_gb[k], 16)
            for k in range(UPC):
                store(CHUNKS - 1, k, g_dram, (CHUNKS - 1) * UPC + k)
            for i in range(3):
                sp.wait_ge(mm_ready, at((CHUNKS - 1) * OT + 4 * i + 3))
                sp.dma_start(W[:, 4 * i:4 * i + 4], wu_dram[4 * i:4 * i + 4].rearrange("o p a k c -> p o a k c")) \
                    .then_inc(ld_wu[i], 16)
            for s in range(3):
                sp.wait_ge(st_stg[s], (UNITS // 3 + 1) * 16)
            def first_half(c, units):
                for k in range(2 * UPC):
                    if k in units:
                        q = c * (2 * UPC) + k + 6
                        sp.wait_ge(gg_peaked, at(q - 6))
                        sp.dma_start(GB[:, k % 6, :], g_dram[q]).then_inc(ld_gb[k % 6], 16)
                    if k % 2:
                        store(c + CHUNKS, k // 2, u_dram, c * UPC + k // 2)

            with sp.Fori(0, CHUNKS // 2 - 1) as c:
                first_half(c, range(12))
            first_half(CHUNKS // 2 - 1, range(6))
            with sp.Fori(CHUNKS // 2, CHUNKS - 1) as c:
                for k in range(UPC):
                    store(c + CHUNKS, k, u_dram, c * UPC + k)
            for s in range(3):
                sp.wait_ge(st_stg[s], (UNITS // 3 + 5) * 16)

            def load_up(q, k):
                sp.dma_start(UR[:, k, :], u_dram[q]).then_inc(ld_ur[k], 16)

            for k in (3, 4, 5):
                load_up(k, k)
            for k in range(UPC):
                sp.wait_ge(stg_ready, at((2 * CHUNKS - 1) * OT + 2 * k + 1))
                sp.dma_start(u_dram[UNITS - UPC + k], LU[:, k, :]).then_inc(st_lu, 16)
            sp.wait_ge(sq2_ready, at(UNITS - 1))
            for k in range(3):
                load_up(k, k)
            sp.wait_ge(mm_ready, at(2 * CHUNKS * OT - 1))
            sp.wait_ge(stg_peaked, at(2 * UNITS - 1))
            for s in range(3):
                sp.wait_ge(st_stg[s], (4 * CHUNKS - 1) * 16)
            sp.dma_start(WD, wd_dram.rearrange("o p a d -> p o a d")).then_inc(ld_wd, 16)
            with sp.Fori(1, CHUNKS - 1) as i:
                for k in range(UPC):
                    sp.wait_ge(p_peaked, at(i * UPC + k))
                    load_up(i * UPC + k, k)
            sp.wait_ge(st_lu, 16 * UPC)
            sp.wait_ge(st_h, 16 * CHUNKS)
            sp.wait_ge(p_peaked, at(UNITS - 1))
            sp.wait_ge(sq2_ready, at(UNITS - 1))
            for par in range(2):
                sp.dma_start(HB[:, par], h_dram[par]).then_inc(ld_hb[par], 16)

            def up_units(c):
                for k in range(UPC):
                    sp.wait_ge(ui_ready, at(c * UPC + k - 3))
                    sp.dma_start(UB[:, k % 3, :], u_dram[c * UPC + k]).then_inc(ld_ub[k % 3], 16)

            def out_chunk(j, par, more):
                sp.wait_ge(y_ready, at((j * 2 + par) * TPC + TPC - 1))
                sp.dma_start(out_dst[j * 2 + par], HB[:, par]).then_inc(st_out[par], 16)
                if more:
                    sp.wait_ge(st_out[par], (j + 2) * 16)
                    sp.dma_start(HB[:, par], h_dram[j * 2 + par + 2]).then_inc(ld_hb[par], 16)

            up_units(0)
            with sp.Fori(0, CHUNKS // 2 - 1) as j:
                up_units(j * 2 + 1)
                out_chunk(j, 0, True)
                up_units(j * 2 + 2)
                out_chunk(j, 1, True)
            up_units(CHUNKS - 1)
            for par in range(2):
                out_chunk(CHUNKS // 2 - 1, par, False)
            for par in range(2):
                sp.wait_ge(st_out[par], (CHUNKS // 2 + 1) * 16)


PS_CXT = [1, 8]
PS_KV = [2, 9]
PS_KT = [3, 10]
PS_VW = [[4, 5, 6, 7], [11, 12, 13, 14]]
N_ATTN = 7 + NH
N_SMALL = 2
AS_QWH, AS_VWH, AS_VARH, AS_TOP = 5, 6, 8, 9
ROW_AHEAD, HEAD_AHEAD = 9, 5
XN_SCALE = 1024.0
PROB_SCALE = 4096.0
DVE_ABS, ACT_ABS = (2, 5), (0, 1, 3, 4)


def late_group(i):
    return isinstance(i, int) and i == 0


ACT_EVENTS = {"whi_ready", "wt_ready", "xn_ready", "xtc_hi", "exp_ready", "pt_hi", "xt_ready", "stg_ready", "gi_ready",
              "sig_ready", "sig2_ready", "ua_ready", "pab_ready", "ui_ready"}
PE_EVENTS = {"w_transposed", "xn_transposed", "q_ready", "scores_ready", "probs_transposed", "attn_ready",
             "x_transposed", "mm_ready", "down_ready"}
DVE_EVENTS = {"wq_ready", "ws_ready", "wlo_ready", "xtc_lo", "pt_lo", "roped", "masked", "max_ready", "inv_ready",
              "probs_ready", "h_ready", "h_stats", "xi_ready", "xh_ready", "xl_ready", "stg_peaked",
              "sq_ready", "g_kept", "gg_peaked", "gg_folded", "sq2_ready", "gg_ready", "pab2_ready", "p_peaked", "p_folded",
              "oi_ready", "oh_ready", "ol_ready", "y_ready"}

_INS = ["x", "ctx_1024", "mask_BxS2_bk0", "g_xattn", "g_ffn", "L0_xattn_rms_scale", "L0_xattn_q_w", "L0_xattn_kv_w",
        "L0_xattn_out_w", "L0_ffn_w_gate", "L0_ffn_w_up", "L0_ffn_w_down"]


def _rope_tables():
    import numpy as np
    half = HD // 2
    exponent = np.float32(2.0 / HD) * np.arange(half, dtype=np.float32)
    timescale = np.power(np.float32(10000.0), exponent).astype(np.float32)

    def table(first, count):
        radians = np.arange(first, first + count, dtype=np.float32)[:, None] / timescale
        r = radians.astype(np.float64)
        return np.cos(r), np.sin(r)

    c, s = table(CTX, SEQ)
    q = np.stack([np.concatenate([c, c], 1), np.concatenate([s, s], 1)], 0) * HD ** -0.5
    q = q.reshape(2, SEQ // CHUNK, CHUNK, HD).transpose(1, 3, 0, 2)
    q = np.concatenate([q] * BATCH, 0)
    c, s = table(0, CTX)
    return np.ascontiguousarray(q, np.float32), np.ascontiguousarray(np.stack([c, s], 1), np.float32)


def kernel(**inputs):
    import numpy as np
    import concourse.bacc as bacc
    from concourse.bass_utils import run_bass_kernel_spmd

    nc = bacc.Bacc("TRN2", target_bir_lowering=False, num_devices=1)
    arrays, args = {}, []
    rope_q, rope_k = _rope_tables()
    given = [(n, np.ascontiguousarray(inputs[n])) for n in _INS] + [("rope_q", rope_q), ("rope_k", rope_k)]
    for name, a in given:
        arrays[f"in_{name}"] = a
        args.append(nc.dram_tensor(f"in_{name}", a.shape, mybir.dt.from_np(a.dtype), kind="ExternalInput").ap())
    args.append(nc.dram_tensor("out_0", (BATCH, SEQ, D), mybir.dt.float32, kind="ExternalOutput").ap())
    flamingo_kernel(nc, *args)
    r = run_bass_kernel_spmd(nc, [arrays], core_ids=[0])
    return r.results[0]["out_0"]
```

```python
import concourse.bass as bass
from concourse import mybir
from contextlib import ExitStack

P = 128
BATCH, SEQ, D = 2, 2048, 512
CTX, NH, HD = 128, 4, 128
FF = 1536
BLOCK = 32
KD = D // P
OT = FF // P
TILES = BATCH * SEQ // P
CHUNK = 512
TPC = CHUNK // P
CHUNKS = TILES // TPC
PAIR = 2 * CHUNK
UPC = OT // 2
UNITS = CHUNKS * UPC
QMAX = 32767.0
QMAX4 = 7.0
TINY = 1e-12
MASK_FILL = -2.3819763e38
LEAD = 8
KB = 1024


def at(n):
    return n + 1 + LEAD


def flamingo_kernel(nc, x, ctx_in, mask, g_xattn, g_ffn, rms_scale, q_w, kv_w, out_w, w_gate, w_up, w_down,
                    rope_q, rope_k, out):
    F32, F16, BF16, I16, U16, I32, U8 = (mybir.dt.float32, mybir.dt.float16, mybir.dt.bfloat16, mybir.dt.int16,
                                         mybir.dt.uint16, mybir.dt.int32, mybir.dt.uint8)
    ALU, ACT, AX = mybir.AluOpType, mybir.ActivationFunctionType, mybir.AxisListType
    SIZE = {F32: 4, F16: 2, BF16: 2, I16: 2, U16: 2, I32: 4, U8: 1}

    h_dram = nc.dram_tensor("h_scratch", (CHUNKS, P, TPC, D), F32, kind="Internal").ap()
    g_dram = nc.dram_tensor("gate_scratch", (UNITS, P, PAIR), F32, kind="Internal").ap()
    u_dram = nc.dram_tensor("up_scratch", (UNITS, P, PAIR), F32, kind="Internal").ap()
    wg_dram = nc.dram_tensor("w_gate_parts", (OT, P, 2, KD, P), F16, kind="Internal").ap()
    wu_dram = nc.dram_tensor("w_up_parts", (OT, P, 2, KD, P), F16, kind="Internal").ap()
    wd_dram = nc.dram_tensor("w_down_parts", (3, KD, P, 2, KD, P), F16, kind="Internal").ap()

    es = ExitStack()
    with es:
        arena = es.enter_context(nc.sbuf_tensor("arena", [P, 207 * KB // 4], F32))
        banks = [es.enter_context(nc.psum_tensor(f"bank{i}", [P, 512], F32)) for i in range(8)]

        def sem(name):
            return es.enter_context(nc.semaphore(name))

        def view(at_byte, shape, dt):
            n = SIZE[dt]
            for s in shape:
                n *= s
            assert at_byte % 4 == 0 and n % 4 == 0 and at_byte + n <= 207 * KB, (at_byte, shape)
            v = arena[:, at_byte // 4:(at_byte + n) // 4]
            if dt != F32:
                v = v.bitcast(dt)
            if len(shape) > 1:
                names = "abcde"[:len(shape)]
                v = v.rearrange(f"p ({' '.join(names)}) -> p {' '.join(names)}",
                                **{c: s for c, s in zip(names[1:], shape[1:])})
            return v

        H = view(0, [TILES, D], F32)

        class Small:
            top = 204 * KB
            end = 207 * KB

        def small(shape, dt=F32):
            n = SIZE[dt]
            for s in shape:
                n *= s
            if n % 4:
                v = view(Small.top, [2], dt)[:, 0:1]
                n = 4
            else:
                v = view(Small.top, shape, dt)
            Small.top += n
            assert Small.top <= Small.end
            return v

        ident = small([P])
        ident16 = small([P], F16)
        gates = small([2])
        w_row, w_all = small([3]), small([3])
        w_pow, w_scale, w_undo = small([3]), small([3]), small([3])
        x_row, x_all = small([1]), small([1])
        g_row, g_all = small([2]), small([2])
        gg_row, gg_all = small([1]), small([1])
        u_row, u_all = small([1]), small([1])
        p_row, p_all = small([1]), small([1])
        s_x, s_g, s_gg, s_u, s_p = (small([1]) for _ in range(5))
        i_x, i_g, i_gg, i_u, i_p = (small([1]) for _ in range(5))
        d_g, d_u = small([1]), small([1])
        c_g, c_u, c_gg, c_p, c_out = (small([1]) for _ in range(5))
        tmp = small([4])
        g_peak, g_top = small([UNITS]), small([UNITS])
        u_peak = small([2 * UNITS])
        top_i, top_sq = small([1], I16), small([1], U16)
        top_sig, top_g = small([1]), small([1])
        gg_acc, gg_run = small([2 * UPC]), small([2 * UPC])
        p_acc, p_run = small([UPC]), small([UPC])
        W_RAW = view(144 * KB, [OT, D], F32)
        W_HI = view(88 * KB, [4, 3, D], F16)
        W_QI = view(100 * KB, [4, 3, D], I16)
        W_LO = view(100 * KB, [4, 3, D], F16)
        W_T = view(136 * KB, [4, 2, KD, P], F16)
        V_RAW = view(184 * KB, [3, D], F32)
        V_QI = view(190 * KB, [3, D], I16)
        V_LO = view(190 * KB, [3, D], F16)
        V_HI = view(193 * KB, [3, D], F16)
        V_T = view(196 * KB, [3, 2, KD, P], F16)
        M_RAW = view(152 * KB, [2, 2, D], F32)
        M_SUM = view(194 * KB, [2, M_GROUPS * 2], F32)
        STATS = 64 * KB
        BN_X = view(STATS, [TILES, 6], F32)
        BN_H = view(STATS + 768, [TILES, 6], F32)
        st = [view(STATS + 1536 + 128 * i, [TILES], F32) for i in range(20)]
        mean_x, var_x, r_x, ra, rb, rc, rd, hmax, hmin, mean_h, var_h, r_h, c_h, nmr_x = st[:14]
        bn_c = view(STATS + 1536 + 2560, [BATCH, 6], F32)
        W_BMAX, W_RECIP, W_BSCALE = (view(STATS + 4672 + 768 * i, [OT, D // BLOCK], F32) for i in range(3))
        RK = view(STATS + 6976, [2, HD // 2], F32)
        QC = view(72 * KB, [2, NH, CHUNK], F32)
        QS = view(88 * KB, [2, NH, CHUNK], F32)
        XN = view(104 * KB, [TPC, D], F32)
        VWP = view(112 * KB, [BATCH, 2, NH, D], F16)
        QWP = view(128 * KB, [2, KD, NH, HD], F16)
        XTC = view(136 * KB, [2, 2, KD, CHUNK], F16)
        Q_ABS = view(112 * KB, [KD, NH, HD], F32)
        V_ABS = view(112 * KB, [BATCH, NH, D], F32)
        VW = view(72 * KB, [BATCH, NH, D], F32)
        SC = view(160 * KB, [2, NH, CTX], F32)
        EX = view(164 * KB, [2, NH, CTX], F32)
        PT = view(168 * KB, [2, 2, NH, P], F16)
        QW = view(172 * KB, [KD, NH, HD], F32)
        KT1 = view(180 * KB, [BATCH, CTX], F32)
        KT2 = view(181 * KB, [BATCH, CTX], F32)
        KVW = view(182 * KB, [2, KD, HD], F32)
        OW = view(186 * KB, [NH, D], F32)
        TAB = view(186 * KB, [2, 2, CHUNK], F32)
        CX = view(194 * KB, [BATCH, D], F32)
        CXT = view(198 * KB, [KD, CTX], F32)
        VT = view(200 * KB, [BATCH, CTX], F32)
        KN = view(201 * KB, [BATCH, CTX], F32)
        KR = view(202 * KB, [BATCH, HD], F32)
        KR2 = view(198 * KB, [BATCH, HD], F32)
        KM = view(199 * KB, [2, BATCH, HD // 2], F32)
        MB = view(203 * KB, [BATCH, CTX], F32)
        a0 = STATS + 1536 + 2560 + 64
        MU8 = view(a0, [BATCH, CTX], U8)
        RMS = view(a0 + 256, [KD], F32)
        st_c = [view(a0 + 288 + 8 * i, [BATCH], F32) for i in range(6)]
        NMX = view(a0 + 352, [2, NH], F32)
        RSUM = view(a0 + 384, [2, NH], F32)
        RINV = view(a0 + 416, [2, NH], F32)
        v_row, v_all = view(a0 + 448, [2], F32), view(a0 + 456, [2], F32)
        v_pow, v_scale, v_undo = (view(a0 + 464 + 8 * i, [2], F32) for i in range(3))
        v_sum = view(a0 + 500, [BATCH], F32)
        q_undo, o_gate = view(a0 + 488, [1], F32), view(a0 + 492, [1], F32)
        XT = view(72 * KB, [CHUNKS, 2, KD, CHUNK], F16)
        G = view(0, [UNITS, PAIR], I16)
        W = view(136 * KB, [OT, 2, KD, P], F16)
        STG = view(160 * KB, [3, 2, CHUNK], F32)
        XI = view(172 * KB, [TPC, D], I16)
        XH = view(176 * KB, [TPC, D], F16)
        XL = view(180 * KB, [TPC, D], F16)
        GB = view(172 * KB, [4, PAIR], F32)
        SQ = view(196 * KB, [4, PAIR], U16)
        SJ = view(196 * KB, [4, PAIR], BF16)
        GQ = view(188 * KB, [4, PAIR], I16)
        LU = view(96 * KB, [UPC, PAIR], F32)
        UR = view(172 * KB, [6, PAIR], F32)
        U0 = view(132 * KB, [UPC, PAIR], I16)
        UA = view(196 * KB, [3, PAIR], I16)
        AB = view(120 * KB, [3, PAIR], I16)
        OH = view(96 * KB, [2, OT, CHUNK], F16)
        OL = view(120 * KB, [2, OT, CHUNK], F16)
        WD = view(144 * KB, [3, KD, 2, KD, P], F16)
        UB = view(168 * KB, [3, PAIR], F32)
        HB = view(180 * KB, [2, TPC, D], F32)
        UI = view(196 * KB, [2, PAIR], I16)
        OI = view(200 * KB, [2, PAIR], I16)

        def col(v, n):
            return v[:, bass.ds(n, 1)]

        bank16 = [b[:, :].bitcast(F16).rearrange("p (a k c) -> p a k c", a=2, k=KD) for b in banks]
        bank4 = [b[:, :].rearrange("p (a c) -> p a c", a=4) for b in banks]
        TB, QB, LB, PB, OB = (0, 1), (2, 3), (4, 5), 6, 7
        XB, WB = 6, 7
        MM = 6

        ld_ctx, ld_qw, ld_ow, ld_wd, ld_wg, ld_peak, ld_v = (
            sem(n) for n in ("ld_ctx", "ld_qw", "ld_ow", "ld_wd", "ld_wg", "ld_peak", "ld_v"))
        ld_w = [sem(f"ld_w{g}") for g in range(4)]
        ld_x = [sem(f"ld_x{c}") for c in range(CHUNKS)]
        ld_tab = [sem(f"ld_tab{i}") for i in range(2)]
        ld_wu = [sem(f"ld_wu{i}") for i in range(3)]
        ld_gb = [sem(f"ld_gb{i}") for i in range(4)]
        ld_ur = [sem(f"ld_ur{i}") for i in range(6)]
        ld_ub = [sem(f"ld_ub{i}") for i in range(3)]
        ld_hb = [sem(f"ld_hb{i}") for i in range(2)]
        st_wg = [sem(f"st_wg{i}") for i in range(4)]
        st_v = [sem(f"st_v{i}") for i in range(3)]
        st_h, st_lu = sem("st_h"), sem("st_lu")
        st_stg = [sem(f"st_stg{i}") for i in range(3)]
        st_out = [sem(f"st_out{i}") for i in range(2)]
        idents = sem("idents")
        steps = sem("vector_steps")
        asteps = sem("scalar_steps")
        psteps = sem("tensor_steps")
        gsteps = sem("gpsimd_steps")
        peaks = sem("peaks_over_partitions")
        counted = {}

        def event(name):
            counted[name] = sem(name)
            return counted[name]

        wq_ready, ws_ready, whi_ready, wlo_ready, wtrans, wt_ready = (event(n) for n in (
            "wq_ready", "ws_ready", "whi_ready", "wlo_ready", "w_transposed", "wt_ready"))
        w_summed, wb_ready = event("w_summed"), event("wb_ready")
        xn_ready, xn_trans, xtc_hi, xtc_lo, q_ready, roped = (event(n) for n in (
            "xn_ready", "xn_transposed", "xtc_hi", "xtc_lo", "q_ready", "roped"))
        scores_ready, masked, max_ready, exp_ready, inv_ready, probs_ready = (event(n) for n in (
            "scores_ready", "masked", "max_ready", "exp_ready", "inv_ready", "probs_ready"))
        probs_trans, pt_hi, pt_lo, attn_ready, h_ready, h_stats = (event(n) for n in (
            "probs_transposed", "pt_hi", "pt_lo", "attn_ready", "h_ready", "h_stats"))
        xi_ready, xh_ready, xl_ready, x_trans, xt_ready = (event(n) for n in (
            "xi_ready", "xh_ready", "xl_ready", "x_transposed", "xt_ready"))
        mm_ready, stg_ready, stg_peaked, up_peaked = (event(n) for n in (
            "mm_ready", "stg_ready", "stg_peaked", "up_peaked"))
        gi_ready, sig_ready, sq_ready, g_kept, gg_peaked, gg_folded = (event(n) for n in (
            "gi_ready", "sig_ready", "sq_ready", "g_kept", "gg_peaked", "gg_folded"))
        sig2_ready, sq2_ready, gg_ready = (event(n) for n in ("sig2_ready", "sq2_ready", "gg_ready"))
        ua_ready, ga_ready, ga2_ready, p_peaked = (event(n) for n in (
            "ua_ready", "ga_ready", "ga2_ready", "p_peaked"))
        ui_ready, oi_ready, oh_ready, ol_ready, down_ready, y_ready = (event(n) for n in (
            "ui_ready", "oi_ready", "oh_ready", "ol_ready", "down_ready", "y_ready"))

        block = es.enter_context(nc.Block())
        marks = {}

        up_src = w_up.rearrange("(g s p) d -> g p s d", p=P, s=3)
        down_src = w_down.rearrange("(j p) (s d) -> j p s d", p=P, d=D)
        flat_src = [w_up.rearrange("(p q) d -> p (q d)", p=P), w_down.rearrange("(p q) f -> p (q f)", p=P)]
        x_src = x.rearrange("b (c t p) d -> (b c) p t d", p=P, t=TPC)
        out_dst = out.rearrange("b (c t p) d -> (b c) p t d", p=P, t=TPC)

        def ahead(j, i, d):
            if isinstance(j, int) and j * 2 * TPC + i + d >= TILES:
                return None
            e, tt = divmod(i + d, TPC)
            return j * 2 + e, e % 2, tt, (j + e // 2) // 2

        @block.vector
        def _(dve):
            for name, s in counted.items():
                if name in DVE_EVENTS:
                    dve.sem_inc(s, LEAD)
            n_steps = [0]

            def step(ins, mark=None):
                n_steps[0] += 1
                ins.then_inc(steps, 1)
                dve.wait_ge(steps, n_steps[0])
                if mark:
                    marks[mark] = n_steps[0]

            def rsqrt(y, a, root, t, mark, act_step):
                marks[mark] = n_steps[0]
                dve.wait_ge(asteps, act_step)
                step(nc.vector.reciprocal(y, root))
                step(nc.vector.tensor_tensor(t, y, y, ALU.mult))
                step(nc.vector.tensor_tensor(t, t, a, ALU.mult))
                step(nc.vector.tensor_scalar(t, t, -0.5, 1.5, ALU.mult, ALU.add))
                step(nc.vector.tensor_tensor(y, y, t, ALU.mult))

            def moments(bn, mean, var, a, b):
                step(nc.vector.tensor_tensor(a, bn[:, :, 1], bn[:, :, 4], ALU.add))
                step(nc.vector.tensor_scalar(mean, a, 0.5, None, ALU.mult))
                step(nc.vector.tensor_tensor(a, bn[:, :, 1], bn[:, :, 4], ALU.subtract))
                step(nc.vector.tensor_tensor(a, a, a, ALU.mult))
                step(nc.vector.tensor_tensor(b, bn[:, :, 2], bn[:, :, 5], ALU.add))
                step(nc.vector.tensor_scalar(b, b, 1.0 / D, None, ALU.mult))
                step(nc.vector.scalar_tensor_tensor(var, a, 0.25, b, ALU.mult, ALU.add))

            def scale_of(s, inv, peak, qmax):
                step(nc.vector.tensor_scalar(s, peak, 1.0 / qmax, TINY, ALU.mult, ALU.max))
                step(nc.vector.reciprocal(inv, s))

            def power_scale(peak, power, scale, undo):
                step(nc.vector.tensor_scalar(power, peak, 1e-30, None, ALU.max))
                step(nc.vector.tensor_scalar(power.bitcast(I32), power.bitcast(I32), 0x7F800000, None,
                                             ALU.bitwise_and))
                step(nc.vector.reciprocal(scale, power))
                step(nc.vector.tensor_scalar(scale, scale, 16384.0, None, ALU.mult))
                step(nc.vector.tensor_scalar(undo, power, 1.0 / 16384.0, None, ALU.mult))

            def by_block(v):
                return v.rearrange("p s (b e) -> p (s b) e", e=BLOCK)

            def over_block(v):
                return v.rearrange("p s b -> p (s b)").unsqueeze(2).broadcast_to([P, 3 * D // BLOCK, BLOCK])

            def quantise_weights(g, raw, ints, recip, scale, used=None):
                if used is not None:
                    dve.wait_ge(wtrans, at(used))
                nc.vector.tensor_tensor(by_block(ints), by_block(raw), over_block(recip), ALU.mult).then_inc(wq_ready, 1)
                dve.wait_ge(wq_ready, at(g))
                nc.vector.tensor_tensor(by_block(raw), by_block(ints), over_block(scale), ALU.mult).then_inc(ws_ready, 1)

            def weights_low(g, raw, low, high):
                dve.wait_ge(ws_ready, at(g))
                dve.wait_ge(whi_ready, at(g))
                nc.vector.tensor_tensor(low, raw, high, ALU.subtract).then_inc(wlo_ready, 1)

            def quantise_gate(g):
                w = slice(3 * g, 3 * g + 3)
                quantise_weights(g, W_RAW[:, w], W_QI[:, g], W_RECIP[:, w], W_BSCALE[:, w])

            def gate_low(g):
                weights_low(g, W_RAW[:, 3 * g:3 * g + 3], W_LO[:, g], W_HI[:, g])

            dve.wait_ge(ld_ctx, 16 * N_CTX)
            step(nc.vector.tensor_scalar(RMS, RMS, 1.0, None, ALU.add), "rms")
            for b in range(BATCH):
                step(nc.vector.bn_stats(bn_c[:, b, :], CX[:, b, :]))
            mc, vc, cc, ca, cb, cd = st_c
            moments(bn_c, mc, vc, ca, cb)
            step(nc.vector.tensor_tensor(ca, mc, mc, ALU.mult))
            step(nc.vector.tensor_tensor(ca, ca, vc, ALU.add))
            step(nc.vector.tensor_scalar(ca, ca, 1e-6, None, ALU.add))
            rsqrt(cc, ca, cb, cd, "ms_c", AS["root_c"])
            for b in range(BATCH):
                step(nc.vector.tensor_scalar(CX[:, b, :], CX[:, b, :], cc[:, b:b + 1], None, ALU.mult))
            marks["cx"] = n_steps[0]
            step(nc.vector.tensor_copy(MB, MU8))
            step(nc.vector.tensor_scalar(MB, MB, 1.0, -MASK_FILL, ALU.subtract, ALU.mult))
            for g in range(4):
                dve.wait_ge(ld_w[g], 16)
                step(nc.vector.tensor_reduce(
                    W_BMAX[:, 3 * g:3 * g + 3, :].rearrange("p t b -> p (t b)"),
                    by_block(W_RAW[:, 3 * g:3 * g + 3]), axis=AX.X, op=ALU.max, apply_absolute_value=True))
            step(nc.vector.tensor_reduce(w_row[:, 0:1], W_BMAX, axis=AX.XY, op=ALU.max), "w_row")
            step(nc.vector.tensor_scalar(W_BSCALE, W_BMAX, 1.0 / QMAX4, TINY, ALU.mult, ALU.max))
            step(nc.vector.reciprocal(W_RECIP, W_BSCALE))
            dve.wait_ge(peaks, PK["qw"])
            power_scale(v_all[:, 0:1], v_pow[:, 0:1], v_scale[:, 0:1], v_undo[:, 0:1])
            marks["qw_scale"] = n_steps[0]
            step(nc.vector.tensor_scalar(q_undo, v_undo[:, 0:1], 1.0 / XN_SCALE, None, ALU.mult))
            HH = HD // 2
            kcos, ksin = (RK[:, i].unsqueeze(1).broadcast_to([P, BATCH, HH]) for i in range(2))
            k1, k2 = KN[:, :, 0:HH], KN[:, :, HH:]
            r1, r2 = KR[:, :, 0:HH], KR[:, :, HH:]
            dve.wait_ge(asteps, AS["knvt1"])
            step(nc.vector.tensor_tensor(r1, k1, kcos, ALU.mult))
            step(nc.vector.tensor_tensor(KM[:, 0], k2, ksin, ALU.mult))
            step(nc.vector.tensor_tensor(r1, r1, KM[:, 0], ALU.subtract))
            step(nc.vector.tensor_tensor(r2, k2, kcos, ALU.mult))
            step(nc.vector.tensor_tensor(KM[:, 1], k1, ksin, ALU.mult))
            step(nc.vector.tensor_tensor(r2, r2, KM[:, 1], ALU.add))
            step(nc.vector.tensor_copy(KR2[:, :, 0:HH], r2))
            step(nc.vector.tensor_scalar(KR2[:, :, HH:], r1, -1.0, None, ALU.mult), "kr")

            def x_moments(first, end):
                for n in range(first, end):
                    if n % TPC == 0:
                        dve.wait_ge(ld_x[n // TPC], 16)
                    n_steps[0] += 1
                    nc.vector.bn_stats(BN_X[:, n, :], H[:, n, :]).then_inc(steps, 1)

            dve.wait_ge(peaks, PK["w_gate"])
            power_scale(w_all[:, 0:1], w_pow[:, 0:1], w_scale[:, 0:1], w_undo[:, 0:1])
            step(nc.vector.tensor_scalar(W_BSCALE, W_BSCALE, w_scale[:, 0:1], None, ALU.mult))
            quantise_gate(0)
            quantise_gate(1)
            gate_low(0)
            x_moments(0, 4)
            dve.wait_ge(asteps, AS["vsum1"])
            step(nc.vector.tensor_reduce(v_row[:, 1:2], v_sum, axis=AX.X, op=ALU.max), "vw_row")
            gate_low(1)
            dve.wait_ge(peaks, PK["vw"])
            power_scale(v_all[:, 1:2], v_pow[:, 1:2], v_scale[:, 1:2], v_undo[:, 1:2])
            marks["vw_scale"] = n_steps[0]
            dve.wait_ge(asteps, AS["tanh"])
            step(nc.vector.tensor_scalar(o_gate, v_undo[:, 1:2], gates[:, 0:1], 1.0 / PROB_SCALE, ALU.mult,
                                         ALU.mult))
            quantise_gate(2)
            x_moments(4, 10)
            quantise_gate(3)
            gate_low(2)
            x_moments(10, X_FIRST)
            gate_low(3)

            def x_norms(part, first, end):
                t = slice(first, end)
                a, root, z, mean, var, fac = (v[:, t] for v in (ra, rb, rd, mean_x, var_x, r_x))
                dve.wait_ge(steps, n_steps[0])
                moments(BN_X[:, t], mean, var, a, root)
                step(nc.vector.tensor_scalar(a, var, 1e-5, 1e-6, ALU.add, ALU.mult))
                step(nc.vector.tensor_tensor(a, a, var, ALU.add))
                rsqrt(fac, a, root, z, f"var_x{part}", AS[f"root_x{part}"])
                step(nc.vector.scalar_tensor_tensor(nmr_x[:, t], mean, -1.0, fac, ALU.mult, ALU.mult), f"r_x{part}")

            x_norms(0, 0, X_FIRST)

            def xt_low(c, par, tt):
                n = c * TPC + tt
                dve.wait_ge(xtc_hi, at(n))
                part = XTC[:, par, :, :, tt * P:(tt + 1) * P]
                nc.vector.scalar_tensor_tensor(part[:, 1], bank4[TB[tt % 2]], XN_SCALE, part[:, 0], ALU.mult,
                                               ALU.subtract).then_inc(xtc_lo, 1)

            def mask_and_max(c, tt, b):
                m, s = c * TPC + tt, tt % 2
                dve.wait_ge(scores_ready, at(m))
                dve.wait_ge(exp_ready, at(m - 2))
                nc.vector.tensor_tensor(SC[:, s], bank4[LB[s]],
                                        MB[:, b, :].unsqueeze(1).broadcast_to([P, NH, CTX]),
                                        ALU.add).then_inc(masked, 1)
                dve.wait_ge(masked, at(m))
                nc.vector.tensor_reduce(NMX[:, s, :], SC[:, s], axis=AX.X, op=ALU.max,
                                        negate=True).then_inc(max_ready, 1)

            def normalise(c, tt):
                m, s = c * TPC + tt, tt % 2
                dve.wait_ge(exp_ready, at(m))
                nc.vector.reciprocal(RINV[:, s, :], RSUM[:, s, :]).then_inc(inv_ready, 1)
                dve.wait_ge(inv_ready, at(m))
                nc.vector.tensor_tensor(EX[:, s], EX[:, s], RINV[:, s, :].unsqueeze(2).broadcast_to([P, NH, CTX]),
                                        ALU.mult).then_inc(probs_ready, 1)

            def probs_low(c, tt):
                m, s = c * TPC + tt, tt % 2
                dve.wait_ge(pt_hi, at(m))
                nc.vector.scalar_tensor_tensor(PT[:, s, 1], bank4[PB], PROB_SCALE, PT[:, s, 0], ALU.mult,
                                               ALU.subtract).then_inc(pt_lo, 1)

            def rope(c, par, n, turn):
                q = c * NH + n
                dve.wait_ge(q_ready, at(q))
                if n == 0:
                    dve.wait_ge(ld_tab[par], (turn + 1) * 16)
                    dve.wait_ge(scores_ready, at(c * TPC - TPC - 1))
                for buf, k in ((QC, 0), (QS, 1)):
                    last = nc.vector.scalar_tensor_tensor(buf[:, par, n, :], banks[QB[n % 2]][:, :], q_undo,
                                                          TAB[:, par, k, :], ALU.mult, ALU.mult)
                last.then_inc(roped, 1)

            def residual(c, tt):
                m = c * TPC + tt
                dve.wait_ge(attn_ready, at(m))
                nc.vector.scalar_tensor_tensor(H[:, m, :], banks[OB][:, :], o_gate, H[:, m, :],
                                               ALU.mult, ALU.add).then_inc(h_ready, 1)

            def statistics(c, tt):
                m = c * TPC + tt
                dve.wait_ge(h_ready, at(m))
                nc.vector.bn_stats(BN_H[:, m, :], H[:, m, :])
                nc.vector.tensor_reduce(col(hmax, m), H[:, m, :], axis=AX.X, op=ALU.max)
                nc.vector.tensor_reduce(col(hmin, m), H[:, m, :], axis=AX.X, op=ALU.min).then_inc(h_stats, 1)

            def slot(j, i):
                c, par, tt, b = ahead(j, i, 0)
                nxt, row, head = ahead(j, i, 1), ahead(j, i, ROW_AHEAD), ahead(j, i, HEAD_AHEAD)
                if not head:
                    probs_low(c, tt)
                    if nxt:
                        mask_and_max(nxt[0], nxt[2], nxt[3])
                    statistics(*ahead(j, i, -1)[0:3:2])
                    if nxt:
                        normalise(nxt[0], nxt[2])
                    residual(c, tt)
                    return
                if nxt:
                    mask_and_max(nxt[0], nxt[2], nxt[3])
                probs_low(c, tt)
                if row:
                    xt_low(*row[:3])
                if nxt:
                    normalise(nxt[0], nxt[2])
                rope(*head[:3], j + (i + HEAD_AHEAD) // (2 * NH))
                residual(c, tt)
                if ahead(j, i, HEAD_AHEAD + 1):
                    statistics(c, tt)

            for tt in range(TPC):
                xt_low(0, 0, tt)
            x_moments(X_FIRST, X_FIRST + 6)
            dve.wait_ge(wtrans, at(OT - 1))
            dve.wait_ge(gsteps, 3)
            for n in range(NH):
                rope(0, 0, n, 0)
                x_moments(X_FIRST + 6 + 2 * n, X_FIRST + 8 + 2 * n)
                xt_low(1, 1, n)
            x_moments(X_FIRST + 14, TILES)
            xt_low(2, 0, 0)
            rope(1, 1, 0, 0)
            mask_and_max(0, 0, 0)
            normalise(0, 0)
            x_norms(1, X_FIRST, TILES)
            with dve.Fori(0, CHUNKS // 2 - 2) as j:
                for i in range(2 * TPC):
                    slot(j, i)
            for j in (CHUNKS // 2 - 2, CHUNKS // 2 - 1):
                for i in range(2 * TPC):
                    slot(j, i)
                    if (j, i) == (CHUNKS // 2 - 1, 0):
                        dve.wait_ge(peaks, PK["w_up_down"])
                        power_scale(w_all[:, 1:3], w_pow[:, 1:3], w_scale[:, 1:3], w_undo[:, 1:3])
                if j == CHUNKS // 2 - 2:
                    dve.wait_ge(w_summed, at(4 * M_GROUPS - 1))
                    for m in range(2):
                        step(nc.vector.tensor_reduce(w_row[:, m + 1:m + 2], M_SUM[:, m], axis=AX.X, op=ALU.max),
                             "w_rows")
            statistics(CHUNKS - 1, TPC - 1)

            dve.wait_ge(h_stats, at(TILES - 1))
            moments(BN_H, mean_h, var_h, ra, rb)
            step(nc.vector.tensor_scalar(ra, var_h, 1e-5, None, ALU.add))
            rsqrt(r_h, ra, rb, rd, "var_h", AS["root_var_h"])
            step(nc.vector.tensor_tensor(ra, hmax, mean_h, ALU.subtract))
            step(nc.vector.tensor_tensor(rb, mean_h, hmin, ALU.subtract))
            step(nc.vector.tensor_tensor(ra, ra, rb, ALU.max))
            step(nc.vector.tensor_tensor(ra, ra, r_h, ALU.mult))
            step(nc.vector.tensor_reduce(x_row, ra, axis=AX.X, op=ALU.max), "x_row")
            dve.wait_ge(peaks, PK["x"])
            scale_of(s_x, i_x, x_all, QMAX)
            step(nc.vector.tensor_scalar(c_h, r_h, i_x, None, ALU.mult))

            def quantise_row(n, s):
                dve.wait_ge(x_trans, at(n - TPC))
                nc.vector.tensor_scalar(XI[:, s, :], H[:, n, :], col(mean_h, n), col(c_h, n),
                                        ALU.subtract, ALU.mult).then_inc(xi_ready, 1)
                dve.wait_ge(xi_ready, at(n))
                nc.vector.tensor_copy(XH[:, s, :], XI[:, s, :]).then_inc(xh_ready, 1)
                dve.wait_ge(xh_ready, at(n))
                nc.vector.tensor_tensor(XL[:, s, :], XI[:, s, :], XH[:, s, :], ALU.subtract).then_inc(xl_ready, 1)

            def peak_of_gate(r, k):
                dve.wait_ge(stg_ready, at(r * 2 + 1))
                unit = STG[:, k % 3].rearrange("p a b -> p (a b)")
                nc.vector.tensor_reduce(col(g_top, r), unit, axis=AX.X, op=ALU.max)
                nc.vector.tensor_reduce(col(g_peak, r), unit, axis=AX.X, op=ALU.max,
                                        apply_absolute_value=True).then_inc(stg_peaked, 1)

            def peak_of_up(c, o, late=False):
                dve.wait_ge(stg_ready, at((c + CHUNKS) * OT + o))
                product = LU[:, o // 2, bass.ts(o % 2, CHUNK)] if late else STG[:, o // 2 % 3, o % 2, :]
                nc.vector.tensor_reduce(col(u_peak, c * OT + o), product, axis=AX.X, op=ALU.max,
                                        apply_absolute_value=True).then_inc(up_peaked, 1)

            for tt in range(TPC):
                quantise_row(tt, tt)
            for tt in range(TPC):
                quantise_row(TPC + tt, tt)
            step(nc.vector.tensor_scalar(d_g, w_undo[:, 0:1], s_x, None, ALU.mult))
            step(nc.vector.tensor_scalar(d_u, w_undo[:, 1:2], s_x, None, ALU.mult))
            step(nc.vector.memset(gg_run, 0.0))
            step(nc.vector.memset(p_acc, 0.0))
            step(nc.vector.memset(p_run, 0.0))

            def block_scales(c, m):
                dve.wait_ge(ld_v, (c + 1) * 16)
                bmax, recip, scale = W_BMAX[:, 0:3], W_RECIP[:, 0:3], W_BSCALE[:, 0:3]
                nc.vector.tensor_reduce(bmax.rearrange("p t b -> p (t b)"), by_block(V_RAW), axis=AX.X, op=ALU.max,
                                        apply_absolute_value=True).then_inc(wb_ready, 1)
                dve.wait_ge(wb_ready, at(c * 4))
                nc.vector.tensor_scalar(scale, bmax, 1.0 / QMAX4, TINY, ALU.mult, ALU.max).then_inc(wb_ready, 1)
                dve.wait_ge(wb_ready, at(c * 4 + 1))
                nc.vector.reciprocal(recip, scale).then_inc(wb_ready, 1)
                dve.wait_ge(wb_ready, at(c * 4 + 2))
                nc.vector.tensor_scalar(scale, scale, w_scale[:, m:m + 1], None, ALU.mult).then_inc(wb_ready, 1)
                dve.wait_ge(wb_ready, at(c * 4 + 3))

            def gate_chunk(c, m, rows):
                for k in range(UPC):
                    r = c * UPC + k
                    peak_of_gate(r, k)
                    if k == 0:
                        block_scales(c, m)
                        quantise_weights(c + 4, V_RAW, V_QI, W_RECIP[:, 0:3], W_BSCALE[:, 0:3], (c + 4) * 3 - 1)
                    if k == 3:
                        weights_low(c + 4, V_RAW, V_LO, V_HI)
                    if rows and k >= 2:
                        quantise_row((c + 2) * TPC + k - 2, k - 2)

            with dve.Fori(0, 4) as c:
                gate_chunk(c, 1, True)
            with dve.Fori(4, CHUNKS - 2) as c:
                gate_chunk(c, 2, True)
            for c in (CHUNKS - 2, CHUNKS - 1):
                gate_chunk(c, 2, False)
            dve.wait_ge(stg_peaked, at(UNITS - 1))
            step(nc.vector.tensor_reduce(g_row[:, 0:1], g_peak, axis=AX.X, op=ALU.max))
            step(nc.vector.tensor_reduce(g_row[:, 1:2], g_top, axis=AX.X, op=ALU.max), "g_row")
            dve.wait_ge(peaks, PK["gate"])
            step(nc.vector.tensor_scalar(tmp[:, 0:1], g_all[:, 0:1], d_g, None, ALU.mult))
            scale_of(s_g, i_g, tmp[:, 0:1], QMAX)
            step(nc.vector.tensor_scalar(c_g, i_g, d_g, None, ALU.mult), "c_g")
            dve.wait_ge(asteps, AS["top_sig"])
            step(nc.vector.tensor_scalar(top_sq, top_sig, 65536.0, 65535.0, ALU.mult, ALU.min))
            step(nc.vector.tensor_tensor(top_g, top_i, top_sq, ALU.mult))

            with dve.Fori(0, CHUNKS // 2) as c:
                for k in range(2 * UPC):
                    q = c * (2 * UPC) + k
                    if k % 2 == 0:
                        peak_of_up(c, k)
                    dve.wait_ge(sig_ready, at(q))
                    nc.vector.tensor_scalar(SQ[:, k % 4, :], GB[:, k % 4, :], 65536.0, 65535.0, ALU.mult,
                                            ALU.min).then_inc(sq_ready, 1)
                    if k == 0:
                        dve.wait_ge(gg_folded, at(c - 1))
                    dve.wait_ge(sq_ready, at(q))
                    if k % 2:
                        peak_of_up(c, k)
                    else:
                        nc.vector.tensor_copy(G[:, q, :], GQ[:, k % 4, :])
                    nc.vector.tensor_tensor_reduce(SJ[:, k % 4, :], GQ[:, k % 4, :], SQ[:, k % 4, :], -1.0, 0.0,
                                                   op0=ALU.mult, op1=ALU.max,
                                                   accum_out=gg_acc[:, k:k + 1]).then_inc(gg_peaked, 1)
                dve.wait_ge(gg_peaked, at(c * (2 * UPC) + 2 * UPC - 1))
                nc.vector.tensor_tensor(gg_run, gg_run, gg_acc, ALU.max).then_inc(gg_folded, 1)
            dve.wait_ge(gg_folded, at(CHUNKS // 2 - 1))
            step(nc.vector.tensor_reduce(gg_row, gg_run, axis=AX.X, op=ALU.max))
            step(nc.vector.tensor_tensor(gg_row, gg_row, top_g, ALU.max), "gg_row")
            dve.wait_ge(peaks, PK["product"])
            step(nc.vector.tensor_scalar(tmp[:, 1:2], s_g, 1.0 / 65536.0, None, ALU.mult))
            step(nc.vector.tensor_scalar(tmp[:, 2:3], gg_all, tmp[:, 1:2], None, ALU.mult))
            scale_of(s_gg, i_gg, tmp[:, 2:3], QMAX)
            step(nc.vector.tensor_scalar(c_gg, i_gg, tmp[:, 1:2], None, ALU.mult))

            def second_half(c, late=False):
                for k in range(2 * UPC):
                    q = c * (2 * UPC) + k
                    dve.wait_ge(sig2_ready, at(q))
                    nc.vector.tensor_scalar(SQ[:, k % 4, :], GB[:, k % 3, :], 65536.0, 65535.0, ALU.mult,
                                            ALU.min).then_inc(sq2_ready, 1)
                    peak_of_up(c + CHUNKS // 2, k, late)
                    dve.wait_ge(sq2_ready, at(q))
                    nc.vector.scalar_tensor_tensor(G[:, q, :], SQ[:, k % 4, :], c_gg, G[:, q, :], ALU.mult,
                                                   ALU.mult).then_inc(gg_ready, 1)

            with dve.Fori(0, CHUNKS // 2 - 1) as c:
                second_half(c)
            second_half(CHUNKS // 2 - 1, late=True)
            dve.wait_ge(up_peaked, at(2 * UNITS - 1))
            step(nc.vector.tensor_reduce(u_row, u_peak, axis=AX.X, op=ALU.max), "u_row")
            dve.wait_ge(peaks, PK["up"])
            step(nc.vector.tensor_scalar(tmp[:, 0:1], u_all, d_u, None, ALU.mult))
            scale_of(s_u, i_u, tmp[:, 0:1], QMAX)
            step(nc.vector.tensor_scalar(c_u, i_u, d_u, None, ALU.mult), "c_u")

            dve.wait_ge(gg_ready, at(UNITS - 1))

            def product_peaks(i, unused):
                for k in range(UPC):
                    n = i * UPC + k
                    s, old = k % 3, (k + 3) % UPC
                    dve.wait_ge(p_peaked, at(n - 2))
                    if k + 1 in DVE_ABS:
                        q = peak_chunk(i) * UPC + k + 1
                        nc.vector.scalar_tensor_tensor(AB[:, (k + 1) % 3, :], G[:, q, :], -1.0, G[:, q, :], ALU.mult,
                                                       ALU.max).then_inc(ga2_ready, 1)
                    if k in DVE_ABS:
                        dve.wait_ge(ga2_ready, at(i * len(DVE_ABS) + DVE_ABS.index(k)))
                    else:
                        dve.wait_ge(ga_ready, at(i * len(ACT_ABS) + ACT_ABS.index(k)))
                    dve.wait_ge(ua_ready, at(n))
                    nc.vector.tensor_tensor(p_run[:, old:old + 1], p_run[:, old:old + 1], p_acc[:, old:old + 1],
                                            ALU.max)
                    nc.vector.tensor_tensor_reduce(unused[:, k], AB[:, s, :], UA[:, s, :], 1.0, 0.0, op0=ALU.mult,
                                                   op1=ALU.max, accum_out=p_acc[:, k:k + 1]).then_inc(p_peaked, 1)

            product_peaks(0, LU)
            with dve.Fori(1, CHUNKS - 1) as i:
                product_peaks(i, UR)
            product_peaks(CHUNKS - 1, LU)
            step(nc.vector.tensor_tensor(tmp[:, 0:1], s_gg, s_u, ALU.mult))
            dve.wait_ge(p_peaked, at(UNITS - 1))
            step(nc.vector.tensor_tensor(p_run, p_run, p_acc, ALU.max))
            step(nc.vector.tensor_reduce(p_row, p_run, axis=AX.X, op=ALU.max), "p_row")
            dve.wait_ge(peaks, PK["output"])
            step(nc.vector.tensor_scalar(tmp[:, 1:2], p_all, tmp[:, 0:1], None, ALU.mult))
            scale_of(s_p, i_p, tmp[:, 1:2], QMAX)
            step(nc.vector.tensor_scalar(c_p, tmp[:, 0:1], i_p, None, ALU.mult))

            def product_units(c, par, ups=None):
                for k in range(UPC):
                    q, s = c * UPC + k, k % 2
                    up = UI[:, s, :] if ups is None else ups[:, k]
                    dve.wait_ge(ui_ready, at(q))
                    nc.vector.scalar_tensor_tensor(OI[:, s, :], G[:, q, :], c_p, up, ALU.mult,
                                                   ALU.mult).then_inc(oi_ready, 1)
                    oi = OI[:, s, :]
                    hi = OH[:, par, 2 * k:2 * k + 2, :].rearrange("p a b -> p (a b)")
                    lo = OL[:, par, 2 * k:2 * k + 2, :].rearrange("p a b -> p (a b)")
                    dve.wait_ge(oi_ready, at(q))
                    dve.wait_ge(down_ready, at(c * TPC - TPC - 1))
                    nc.vector.tensor_copy(hi, oi).then_inc(oh_ready, 1)
                    dve.wait_ge(oh_ready, at(q))
                    nc.vector.tensor_tensor(lo, oi, hi, ALU.subtract).then_inc(ol_ready, 1)

            def output_tiles(j, par):
                for tt in range(TPC):
                    m = (j * 2 + par) * TPC + tt
                    if tt == 0:
                        dve.wait_ge(ld_hb[par], (j + 1) * 16)
                    dve.wait_ge(down_ready, at(m))
                    nc.vector.scalar_tensor_tensor(HB[:, par, tt, :], banks[par * TPC + tt][:, :], c_out,
                                                   HB[:, par, tt, :], ALU.mult, ALU.add).then_inc(y_ready, 1)

            product_units(0, 0, U0)
            step(nc.vector.tensor_scalar(c_out, s_p, w_undo[:, 2:3], None, ALU.mult))
            step(nc.vector.tensor_scalar(c_out, c_out, gates[:, 1:2], None, ALU.mult))
            with dve.Fori(0, CHUNKS // 2 - 1) as j:
                product_units(j * 2 + 1, 1)
                output_tiles(j, 0)
                product_units(j * 2 + 2, 0)
                output_tiles(j, 1)
            product_units(CHUNKS - 1, 1)
            output_tiles(CHUNKS // 2 - 1, 0)
            output_tiles(CHUNKS // 2 - 1, 1)

        @block.scalar
        def _(act):
            for name, s in counted.items():
                if name in ACT_EVENTS:
                    act.sem_inc(s, LEAD)
            n_steps = [0]

            def step(ins, name):
                n_steps[0] += 1
                assert AS[name] == n_steps[0], name
                ins.then_inc(asteps, 1)

            def root_of(mark, name, out_, in_):
                act.wait_ge(steps, marks[mark])
                step(nc.scalar.activation(out_, in_, ACT.Sqrt), name)

            def weights_high(g, raw, high, used=None):
                act.wait_ge(ws_ready, at(g))
                if used is not None:
                    act.wait_ge(wtrans, at(used))
                nc.scalar.activation(high, raw, ACT.Copy).then_inc(whi_ready, 1)

            act.wait_ge(ld_ctx, 16 * N_CTX)
            step(nc.scalar.activation(gates, gates, ACT.Tanh), "tanh")
            root_of("ms_c", "root_c", st_c[4], st_c[3])
            act.wait_ge(steps, marks["rms"])
            for k in range(KD):
                last = nc.scalar.activation(KVW[:, :, k], KVW[:, :, k], ACT.Copy, scale=RMS[:, k:k + 1])
            step(last, "kvw")

            def take_cxt(b):
                act.wait_ge(psteps, PS[f"cxt{b}"] if b == 0 else max(PS["cxt1"], PS["kv0"]))
                step(nc.scalar.activation(CXT, bank4[b], ACT.Copy), f"cxt{b}")

            def take_kv(b):
                act.wait_ge(psteps, PS[f"kv{b}"])
                nc.scalar.activation(KN[:, b], banks[CTX_KB[b]][:, 0:CTX], ACT.Copy)
                step(nc.scalar.activation(VT[:, b], banks[CTX_VB[b]][:, 0:CTX], ACT.Copy), f"knvt{b}")

            take_cxt(0)
            act.wait_ge(ld_qw, 16 * NH)
            for k in range(KD):
                last = nc.scalar.activation(QW[:, k], QW[:, k], ACT.Copy, scale=RMS[:, k:k + 1])
            step(last, "qw")
            take_kv(0)
            take_cxt(1)
            act.wait_ge(asteps, AS["qw"])
            step(nc.scalar.activation(Q_ABS, QW, ACT.Abs, accum_out=v_row[:, 0:1]), "qsum")
            take_kv(1)
            act.wait_ge(steps, marks["qw_scale"])
            step(nc.scalar.activation(QW, QW, ACT.Copy, scale=v_scale[:, 0:1]), "qws")
            act.wait_ge(asteps, AS["qws"])
            step(nc.scalar.activation(QWP[:, 0], QW, ACT.Copy), "qwh")
            for b in range(BATCH):
                act.wait_ge(psteps, PS[f"kt{b}"])
                nc.scalar.activation(KT1[:, b], bank4[4 + b][:, 0, :], ACT.Copy)
                step(nc.scalar.activation(KT2[:, b], bank4[4 + b][:, 1, :], ACT.Copy), f"kt{b}")
            for b in range(BATCH):
                for n in range(NH):
                    act.wait_ge(psteps, PS[f"vw{b}{n}"])
                    step(nc.scalar.activation(VW[:, b, n, :], banks[VWB[b][n]][:, :], ACT.Copy), f"vw{b}{n}")
                weights_high(b, W_RAW[:, 3 * b:3 * b + 3], W_HI[:, b])
            for b in range(BATCH):
                act.wait_ge(asteps, AS[f"vw{b}{NH - 1}"])
                step(nc.scalar.activation(V_ABS[:, b], VW[:, b], ACT.Abs, accum_out=v_sum[:, b:b + 1]), f"vsum{b}")
            x_parts = (slice(0, X_FIRST), slice(X_FIRST, TILES))
            for g in range(4):
                if g == 3:
                    root_of("var_x0", "root_x0", rb[:, x_parts[0]], ra[:, x_parts[0]])
                for n in range(3 * g, 3 * g + 3):
                    act.wait_ge(wtrans, at(n))
                    if n >= 4:
                        act.wait_ge(st_wg[n % 4], 16 * (n // 4))
                    nc.scalar.activation(W_T[:, n % 4], bank16[4 + n % 2], ACT.Copy).then_inc(wt_ready, 1)
                if g < 2:
                    weights_high(g + 2, W_RAW[:, 3 * g + 6:3 * g + 9], W_HI[:, g + 2])
                    act.wait_ge(steps, marks["vw_scale"])
                    step(nc.scalar.activation(VW[:, g], VW[:, g], ACT.Copy, scale=v_scale[:, 1:2]), f"vws{g}")
                    act.wait_ge(asteps, AS[f"vws{g}"])
                    step(nc.scalar.activation(VWP[:, g, 0], VW[:, g], ACT.Copy), f"vwh{g}")

            def norm_tile(c, tt):
                n = c * TPC + tt
                act.wait_ge(xn_trans, at(n - TPC))
                nc.scalar.activation(XN[:, tt, :], H[:, n, :], ACT.Identity, bias=col(nmr_x, n),
                                     scale=col(r_x, n)).then_inc(xn_ready, 1)

            def take_xt(c, par, tt):
                n = c * TPC + tt
                act.wait_ge(xn_trans, at(n))
                act.wait_ge(q_ready, at(c * NH - NH - 1))
                nc.scalar.activation(XTC[:, par, 0, :, tt * P:(tt + 1) * P], bank4[TB[tt % 2]], ACT.Copy,
                                     scale=XN_SCALE).then_inc(xtc_hi, 1)

            def exps(c, tt):
                m, s = c * TPC + tt, tt % 2
                act.wait_ge(max_ready, at(m))
                act.wait_ge(probs_trans, at(m - 2))
                for n in range(NH):
                    last = nc.scalar.activation(EX[:, s, n, :], SC[:, s, n, :], ACT.Exp, bias=NMX[:, s, n:n + 1],
                                                accum_out=RSUM[:, s, n:n + 1])
                last.then_inc(exp_ready, 1)

            def take_pt(c, tt):
                m, s = c * TPC + tt, tt % 2
                act.wait_ge(probs_trans, at(m))
                act.wait_ge(attn_ready, at(m - 2))
                nc.scalar.activation(PT[:, s, 0], bank4[PB], ACT.Copy, scale=PROB_SCALE).then_inc(pt_hi, 1)

            act.wait_ge(steps, marks["r_x0"])
            act.wait_ge(wtrans, at(OT - 1))
            for tt in range(TPC):
                norm_tile(0, tt)
            for i in range(4):
                act.wait_ge(st_wg[i], 16 * OT // 4)
            for tt in range(TPC):
                take_xt(0, 0, tt)
                norm_tile(1, tt)
            for tt in range(TPC):
                take_xt(1, 1, tt)
            norm_tile(2, 0)
            take_xt(2, 0, 0)
            norm_tile(2, 1)
            exps(0, 0)
            root_of("var_x1", "root_x1", rb[:, x_parts[1]], ra[:, x_parts[1]])
            act.wait_ge(steps, marks["r_x1"])
            nc.scalar.activation(st_c[4], ident[:, 0:BATCH], ACT.Exp)

            def slot(j, i):
                c, par, tt, b = ahead(j, i, 0)
                nxt, row, norm = ahead(j, i, 1), ahead(j, i, ROW_AHEAD), ahead(j, i, ROW_AHEAD + 1)
                take_pt(c, tt)
                if row:
                    take_xt(*row[:3])
                if nxt:
                    exps(nxt[0], nxt[2])
                if norm:
                    norm_tile(norm[0], norm[2])
                if not isinstance(j, int) or j < M_GROUPS // 2:
                    g, (m, half) = j * 2 + i // 4, divmod(i % 4, 2)
                    if i % 4 == 0:
                        act.wait_ge(ld_peak, (g + 1) * 32)
                    piece = M_RAW[:, m, half]
                    nc.scalar.activation(piece, piece, ACT.Abs,
                                         accum_out=col(M_SUM[:, m], g * 2 + half)).then_inc(w_summed, 1)

            with act.Fori(0, CHUNKS // 2 - 2) as j:
                for i in range(2 * TPC):
                    slot(j, i)
            for j in (CHUNKS // 2 - 2, CHUNKS // 2 - 1):
                for i in range(2 * TPC):
                    slot(j, i)
            nc.scalar.activation(st_c[4], ident[:, 0:BATCH], ACT.Sqrt)
            root_of("var_h", "root_var_h", rb, ra)

            def take_x(n, c, tt, bank=XB):
                act.wait_ge(x_trans, at(n))
                nc.scalar.activation(XT[:, c, :, :, tt * P:(tt + 1) * P], bank16[bank],
                                     ACT.Copy).then_inc(xt_ready, 1)

            def take_v(c, s):
                act.wait_ge(wtrans, at((c + 4) * 3 + s))
                act.wait_ge(st_v[s], (c + 1) * 16)
                nc.scalar.activation(V_T[:, s], bank16[WB], ACT.Copy).then_inc(wt_ready, 1)

            def take_mm(c, o, up=False, late=False):
                n, k = c * OT + o, o // 2
                act.wait_ge(mm_ready, at(n))
                if late:
                    nc.scalar.activation(LU[:, k, bass.ts(o % 2, CHUNK)], banks[o % MM][:, :],
                                         ACT.Copy).then_inc(stg_ready, 1)
                    return
                if o % 2 == 0:
                    if up:
                        act.wait_ge(up_peaked, at((c - CHUNKS) * OT + o - 5))
                    else:
                        act.wait_ge(stg_peaked, at(c * UPC + k - 3))
                    act.wait_ge(st_stg[k % 3], (c * (UPC // 3) + k // 3 + 1) * 16)
                nc.scalar.activation(STG[:, k % 3, o % 2, :], banks[o % MM][:, :], ACT.Copy).then_inc(stg_ready, 1)

            for tt in range(TPC):
                take_x(tt, 0, tt, FIRST_XB[tt % 2])

            def gate_chunk(c, rows=True):
                for o in range(OT):
                    take_mm(c, o)
                    if o == 5:
                        weights_high(c + 4, V_RAW, V_HI, (c + 4) * 3 - 1)
                    if o in V_AT:
                        take_v(c, V_AT.index(o))
                    if rows and o % 3 == 1:
                        take_x((c + 1) * TPC + o // 3, c + 1, o // 3)

            with act.Fori(0, CHUNKS - 1) as c:
                gate_chunk(c)
            gate_chunk(CHUNKS - 1, rows=False)

            act.wait_ge(steps, marks["c_g"])
            step(nc.scalar.activation(top_i, g_all[:, 1:2], ACT.Copy, scale=c_g), "top_i")
            act.wait_ge(asteps, AS["top_i"])
            step(nc.scalar.activation(top_sig, top_i, ACT.Sigmoid, scale=s_g), "top_sig")
            for s in range(3):
                act.wait_ge(st_v[s], (CHUNKS + 1) * 16)
            with act.Fori(0, CHUNKS // 2) as c:
                for k in range(2 * UPC):
                    q = c * (2 * UPC) + k
                    act.wait_ge(ld_gb[k % 4], (c * 3 + k // 4 + 1) * 16)
                    act.wait_ge(gg_peaked, at(q - 4))
                    if k % 2:
                        act.wait_ge(g_kept, at(c * UPC + k // 2 - 2))
                    nc.scalar.activation(GQ[:, k % 4, :], GB[:, k % 4, :], ACT.Copy, scale=c_g).then_inc(gi_ready, 1)
                    take_mm(c + CHUNKS, k, up=True)
                    act.wait_ge(gi_ready, at(q))
                    nc.scalar.activation(GB[:, k % 4, :], GQ[:, k % 4, :], ACT.Sigmoid, scale=s_g).then_inc(sig_ready, 1)
            def second_half(c, late=False):
                for k in range(2 * UPC):
                    q = c * (2 * UPC) + k
                    take_mm(c + CHUNKS + CHUNKS // 2, k, up=True, late=late)
                    if k == 0:
                        act.wait_ge(g_kept, at(UNITS // 2 - 1))
                        act.wait_ge(gg_peaked, at(UNITS - 1))
                    act.wait_ge(sq2_ready, at(q - 3))
                    nc.scalar.activation(GB[:, k % 3, :], G[:, q, :], ACT.Sigmoid, scale=s_g).then_inc(sig2_ready, 1)

            with act.Fori(0, CHUNKS // 2 - 1) as c:
                second_half(c)
            second_half(CHUNKS // 2 - 1, late=True)

            act.wait_ge(steps, marks["c_u"])
            def absolutes(i):
                for k in range(UPC):
                    n = i * UPC + k
                    q = peak_chunk(i) * UPC + k
                    late = isinstance(i, int) and i == 0
                    act.wait_ge(p_peaked, at(n - 3))
                    if k in ACT_ABS:
                        nc.scalar.activation(AB[:, k % 3, :], G[:, q, :], ACT.Abs).then_inc(ga_ready, 1)
                    if not late:
                        act.wait_ge(ld_ur[k], i * 16)
                    nc.scalar.activation(UA[:, k % 3, :], (LU if late else UR)[:, k], ACT.Abs,
                                         scale=c_u).then_inc(ua_ready, 1)

            act.wait_ge(gg_ready, at(UNITS - 1))
            act.wait_ge(st_lu, 16 * UPC)
            absolutes(0)
            with act.Fori(1, CHUNKS - 1) as i:
                absolutes(i)
            absolutes(CHUNKS - 1)

            for k in range(UPC):
                nc.scalar.activation(U0[:, k], UR[:, k], ACT.Copy, scale=c_u).then_inc(ui_ready, 1)
            act.wait_ge(p_peaked, at(UNITS - 1))
            with act.Fori(1, CHUNKS) as c:
                for k in range(UPC):
                    q = c * UPC + k
                    act.wait_ge(ld_ub[k % 3], ((c - 1) * 2 + k // 3 + 1) * 16)
                    act.wait_ge(oi_ready, at(q - 2))
                    nc.scalar.activation(UI[:, k % 2, :], UB[:, k % 3, :], ACT.Copy, scale=c_u).then_inc(ui_ready, 1)

        @block.tensor
        def _(pe):
            for name, s in counted.items():
                if name in PE_EVENTS:
                    pe.sem_inc(s, LEAD)
            pe.wait_ge(idents, 4)
            n_steps = [0]

            def step(ins, name):
                n_steps[0] += 1
                assert PS[name] == n_steps[0], name
                ins.then_inc(psteps, 1)

            def transpose_weights(g, n, high, low, bank, freed):
                pe.wait_ge(wlo_ready, at(g))
                pe.wait_ge(wt_ready, at(freed))
                for a, part in enumerate((high, low)):
                    for k in range(KD):
                        last = nc.tensor.transpose(bank16[bank][:, a, k, :], part[:, k * P:(k + 1) * P], ident16)
                last.then_inc(wtrans, 1)

            for b in range(BATCH):
                pe.wait_ge(steps, marks["cx"])
                for k in range(KD):
                    last = nc.tensor.transpose(bank4[b][:, k, :], CX[:, b, k * P:(k + 1) * P], ident)
                step(last, f"cxt{b}")
                pe.wait_ge(asteps, AS[f"cxt{b}"])
                pe.wait_ge(asteps, AS["kvw"])
                for k in range(KD):
                    nc.tensor.matmul(banks[CTX_KB[b]][:, 0:CTX], CXT[:, k, :], KVW[:, 0, k, :], start=k == 0,
                                     stop=k == KD - 1)
                for k in range(KD):
                    last = nc.tensor.matmul(banks[CTX_VB[b]][:, 0:CTX], KVW[:, 1, k, :], CXT[:, k, :], start=k == 0,
                                            stop=k == KD - 1)
                step(last, f"kv{b}")
            for b in range(BATCH):
                pe.wait_ge(steps, marks["kr"])
                nc.tensor.transpose(bank4[4 + b][:, 0, :], KR[:, b], ident)
                step(nc.tensor.transpose(bank4[4 + b][:, 1, :], KR2[:, b], ident), f"kt{b}")
            pe.wait_ge(ld_ow, 16)
            for b in range(BATCH):
                for n in range(NH):
                    pe.wait_ge(asteps, AS["knvt1"] if (b, n) < (1, 2) else AS[f"vw0{n - 2}"])
                    step(nc.tensor.matmul(banks[VWB[b][n]][:, :], VT[:, b], OW[:, n, :], start=True, stop=True),
                         f"vw{b}{n}")
            pe.wait_ge(asteps, AS["kt1"])
            for n in range(OT):
                g, s = n // 3, n % 3
                transpose_weights(g, n, W_HI[:, g, s], W_LO[:, g, s], 4 + n % 2, n - 2)
            pe.wait_ge(wt_ready, at(OT - 1))
            pe.wait_ge(asteps, AS["vw13"])

            def transposes(c, tt):
                n = c * TPC + tt
                pe.wait_ge(xn_ready, at(n))
                pe.wait_ge(xtc_lo, at(n - 2))
                for k in range(KD):
                    last = nc.tensor.transpose(bank4[TB[tt % 2]][:, k, :], XN[:, tt, k * P:(k + 1) * P], ident)
                last.then_inc(xn_trans, 1)

            def query(c, par, n):
                pe.wait_ge(xtc_lo, at(c * TPC + TPC - 1))
                pe.wait_ge(roped, at(c * NH + n - 2))
                i = 0
                for a, x_part in ((0, 0), (0, 1), (1, 0)):
                    for k in range(KD):
                        last = nc.tensor.matmul(banks[QB[n % 2]][:, :], QWP[:, a, k, n, :], XTC[:, par, x_part, k, :],
                                                start=i == 0, stop=i == 3 * KD - 1)
                        i += 1
                last.then_inc(q_ready, 1)

            def scores(c, par, tt, b):
                m, s = c * TPC + tt, tt % 2
                pe.wait_ge(roped, at(c * NH + NH - 1))
                pe.wait_ge(masked, at(m - 2))
                for n in range(NH):
                    nc.tensor.matmul(bank4[LB[s]][:, n, :], QC[:, par, n, tt * P:(tt + 1) * P], KT1[:, b, :],
                                     start=True, stop=False)
                    last = nc.tensor.matmul(bank4[LB[s]][:, n, :], QS[:, par, n, tt * P:(tt + 1) * P], KT2[:, b, :],
                                            start=False, stop=True)
                last.then_inc(scores_ready, 1)

            def probs(c, tt):
                m, s = c * TPC + tt, tt % 2
                pe.wait_ge(probs_ready, at(m))
                pe.wait_ge(pt_lo, at(m - 1))
                for n in range(NH):
                    last = nc.tensor.transpose(bank4[PB][:, n, :], EX[:, s, n, :], ident)
                last.then_inc(probs_trans, 1)

            def output(c, tt, b):
                m, s = c * TPC + tt, tt % 2
                pe.wait_ge(pt_lo, at(m))
                pe.wait_ge(h_ready, at(m - 1))
                i = 0
                for a, v_part in ((0, 0), (0, 1), (1, 0)):
                    for n in range(NH):
                        last = nc.tensor.matmul(banks[OB][:, :], PT[:, s, a, n, :], VWP[:, b, v_part, n, :],
                                                start=i == 0, stop=i == 3 * NH - 1)
                        i += 1
                last.then_inc(attn_ready, 1)

            def slot(j, i):
                c, par, tt, b = ahead(j, i, 0)
                row, head, score = ahead(j, i, ROW_AHEAD), ahead(j, i, HEAD_AHEAD), ahead(j, i, 2)
                probs(c, tt)
                if row:
                    transposes(row[0], row[2])
                if head:
                    query(*head[:3])
                output(c, tt, b)
                if score:
                    scores(*score)

            for tt in range(TPC):
                transposes(0, tt)
            pe.wait_ge(gsteps, 1)
            for n in range(NH):
                query(0, 0, n)
                transposes(1, n)
            transposes(2, 0)
            scores(0, 0, 0, 0)
            query(1, 1, 0)
            scores(0, 0, 1, 0)
            pe.wait_ge(gsteps, 3)
            with pe.Fori(0, CHUNKS // 2 - 2) as j:
                for i in range(2 * TPC):
                    slot(j, i)
            for j in (CHUNKS // 2 - 2, CHUNKS // 2 - 1):
                for i in range(2 * TPC):
                    slot(j, i)

            def transpose_x(n, tt, bank=XB, freed=1):
                pe.wait_ge(xl_ready, at(n))
                pe.wait_ge(xt_ready, at(n - freed))
                for a, part in enumerate((XH, XL)):
                    for k in range(KD):
                        last = nc.tensor.transpose(bank16[bank][:, a, k, :], part[:, tt, k * P:(k + 1) * P], ident16)
                last.then_inc(x_trans, 1)

            def product(c, cx, o):
                n = c * OT + o
                pe.wait_ge(stg_ready, at(n - MM))
                i = 0
                for a, x_part in ((0, 0), (0, 1), (1, 0)):
                    for k in range(KD):
                        last = nc.tensor.matmul(banks[o % MM][:, :], W[:, o, a, k, :], XT[:, cx, x_part, k, :],
                                                start=i == 0, stop=i == 3 * KD - 1)
                        i += 1
                last.then_inc(mm_ready, 1)

            for tt in range(TPC):
                transpose_x(tt, tt, FIRST_XB[tt % 2], 2)

            def gate_chunk(c, rows=True):
                pe.wait_ge(xt_ready, at(c * TPC + TPC - 1))
                for o in range(OT):
                    product(c, c, o)
                    if o in V_AT:
                        s = V_AT.index(o)
                        n = (c + 4) * 3 + s
                        transpose_weights(c + 4, n, V_HI[:, s], V_LO[:, s], WB, n - 1)
                    if rows and o % 3 == 1:
                        transpose_x((c + 1) * TPC + o // 3, o // 3)

            pe.wait_ge(ld_wg, 16)
            with pe.Fori(0, CHUNKS - 1) as c:
                gate_chunk(c)
            gate_chunk(CHUNKS - 1, rows=False)
            with pe.Fori(0, CHUNKS) as c:
                for o in range(OT):
                    if o % 4 == 0:
                        pe.wait_ge(ld_wu[o // 4], 16)
                    product(c + CHUNKS, c, o)

            def down(c, par):
                for tt in range(TPC):
                    m = c * TPC + tt
                    pe.wait_ge(y_ready, at(m - 2 * TPC))
                    i = 0
                    for o in range(OT):
                        if tt == 0 and o % 2 == 0:
                            pe.wait_ge(ol_ready, at(c * UPC + o // 2))
                        for part, a in ((OH, 0), (OH, 1), (OL, 0)):
                            last = nc.tensor.matmul(banks[par * TPC + tt][:, :],
                                                    part[:, par, o, tt * P:(tt + 1) * P],
                                                    WD[:, o // KD, :, a, o % KD, :],
                                                    start=i == 0, stop=i == 3 * OT - 1)
                            i += 1
                    last.then_inc(down_ready, 1)

            pe.wait_ge(ld_wd, 48)
            pe.wait_ge(stg_ready, at(2 * CHUNKS * OT - 1))
            for o in range(OT):
                pe.wait_ge(ol_ready, at(o // 2))
                for tt in range(TPC):
                    for i, (part, a) in enumerate(((OH, 0), (OH, 1), (OL, 0))):
                        last = nc.tensor.matmul(banks[tt][:, :], part[:, 0, o, tt * P:(tt + 1) * P],
                                                WD[:, o // KD, :, a, o % KD, :], start=(o, i) == (0, 0),
                                                stop=(o, i) == (OT - 1, 2))
                    if o == OT - 1:
                        last.then_inc(down_ready, 1)
            down(1, 1)
            with pe.Fori(1, CHUNKS // 2) as j:
                down(j * 2, 0)
                down(j * 2 + 1, 1)

        @block.gpsimd
        def _(pool):
            pool.sem_inc(g_kept, LEAD)
            pool.memset(ident, 0.0).then_inc(idents, 1)
            pool.memset(ident16, 0.0).then_inc(idents, 1)
            pool.wait_ge(idents, 2)
            for m in (ident, ident16):
                pool.affine_select(out=m, in_=m, compare_op=ALU.not_equal, fill=1.0, base=0,
                                   pattern=[[-1, P]], channel_multiplier=1).then_inc(idents, 1)
            RMAX = bass.bass_isa.ReduceOp.max
            def over_partitions(mark, row, all_):
                pool.wait_ge(steps, marks[mark])
                pool.partition_all_reduce(all_, row, P, RMAX).then_inc(peaks, 1)

            pool.wait_ge(asteps, AS["qsum"])
            pool.partition_all_reduce(v_all[:, 0:1], v_row[:, 0:1], P, RMAX).then_inc(peaks, 1)
            over_partitions("w_row", w_row[:, 0:1], w_all[:, 0:1])
            pool.wait_ge(asteps, AS["qwh"])
            nc.gpsimd.tensor_tensor(QWP[:, 1], QW, QWP[:, 0], ALU.subtract).then_inc(gsteps, 1)
            over_partitions("vw_row", v_row[:, 1:2], v_all[:, 1:2])
            for b in range(BATCH):
                pool.wait_ge(asteps, AS[f"vwh{b}"])
                nc.gpsimd.tensor_tensor(VWP[:, b, 1], VW[:, b], VWP[:, b, 0], ALU.subtract).then_inc(gsteps, 1)
            over_partitions("w_rows", w_row[:, 1:3], w_all[:, 1:3])
            over_partitions("x_row", x_row, x_all)
            over_partitions("g_row", g_row, g_all)
            with pool.Fori(0, CHUNKS // 2) as c:
                for k in range(1, 2 * UPC, 2):
                    q = c * (2 * UPC) + k
                    pool.wait_ge(gi_ready, at(q))
                    nc.gpsimd.tensor_copy(G[:, q, :], GQ[:, k % 4, :]).then_inc(g_kept, 1)
            over_partitions("gg_row", gg_row, gg_all)
            over_partitions("u_row", u_row, u_all)
            over_partitions("p_row", p_row, p_all)

        @block.sync
        def _(sp):
            for s in st_v + st_stg + st_out:
                sp.sem_inc(s, 16)
            for dst, src in ((CX, ctx_in.rearrange("b s d -> s b d")),
                             (KVW[:, 0], kv_w[0, 0].rearrange("(k p) h -> p k h", p=P)),
                             (KVW[:, 1], kv_w[1, 0].rearrange("(k p) h -> p k h", p=P)),
                             (MU8, mask.partition_broadcast(P)),
                             (RK, rope_k),
                             (gates[:, 0:1], g_xattn.partition_broadcast(P)),
                             (gates[:, 1:2], g_ffn.partition_broadcast(P))):
                sp.dma_start(dst, src).then_inc(ld_ctx, 16)
            sp.dma_start(RMS, rms_scale.rearrange("(k p) -> p k", p=P),
                         allow_slow_non_contiguous=True).then_inc(ld_ctx, 16)
            for n in range(NH):
                sp.dma_start(QW[:, :, n, :], q_w[n].rearrange("(k p) h -> p k h", p=P)).then_inc(ld_qw, 16)
            gate_src = w_gate.rearrange("(g s p) d -> g p s d", p=P, s=3)
            for g in range(4):
                sp.dma_start(W_RAW[:, 3 * g:3 * g + 3], gate_src[g]).then_inc(ld_w[g], 16)
            sp.dma_start(OW, out_w.rearrange("n h d -> h n d")).then_inc(ld_ow, 16)
            for c in range(CHUNKS):
                sp.dma_start(H[:, c * TPC:(c + 1) * TPC, :], x_src[c]).then_inc(ld_x[c], 16)
            for n in range(OT):
                sp.wait_ge(wt_ready, at(n))
                sp.dma_start(wg_dram[n], W_T[:, n % 4]).then_inc(st_wg[n % 4], 16)
            sp.wait_ge(psteps, PS["vw13"])
            for par in range(2):
                sp.dma_start(TAB[:, par], rope_q[par]).then_inc(ld_tab[par], 16)
            with sp.Fori(0, CHUNKS // 2 - 1) as j:
                for par in range(2):
                    c = j * 2 + par
                    sp.wait_ge(w_summed, at(c * 4 - 1))
                    for m in range(2):
                        sp.dma_start(M_RAW[:, m].rearrange("p a b -> p (a b)"),
                                     flat_src[m][:, bass.ts(c, 2 * D)]).then_inc(ld_peak, 16)
                    sp.wait_ge(roped, at(c * NH + NH - 1))
                    sp.dma_start(TAB[:, par], rope_q[c + 2]).then_inc(ld_tab[par], 16)
                    sp.wait_ge(h_ready, at(c * TPC + TPC - 1))
                    sp.dma_start(h_dram[c], H[:, bass.ds(c * TPC, TPC), :]).then_inc(st_h, 16)
            sp.wait_ge(roped, at(CHUNKS * NH - 1))
            sp.dma_start(V_RAW, up_src[0]).then_inc(ld_v, 16)
            sp.wait_ge(q_ready, at(CHUNKS * NH - 1))
            sp.wait_ge(w_summed, at(4 * M_GROUPS - 1))
            for i in range(4):
                sp.wait_ge(st_wg[i], 16 * OT // 4)
            sp.dma_start(W, wg_dram.rearrange("o p a k c -> p o a k c")).then_inc(ld_wg, 16)
            for c in (CHUNKS - 2, CHUNKS - 1):
                sp.wait_ge(h_ready, at(c * TPC + TPC - 1))
                sp.dma_start(h_dram[c], H[:, c * TPC:(c + 1) * TPC, :]).then_inc(st_h, 16)

            def store(c, k, dst, q):
                sp.wait_ge(stg_ready, at(c * OT + 2 * k + 1))
                sp.dma_start(dst[q], STG[:, k % 3].rearrange("p a b -> p (a b)")).then_inc(st_stg[k % 3], 16)

            def gate_chunk(c, parts, nxt, last=False):
                for k in range(UPC):
                    if last and k % 2:
                        i = k // 2
                        sp.wait_ge(mm_ready, at(c * OT + 4 * i + 3))
                        sp.dma_start(W[:, 4 * i:4 * i + 4],
                                     wu_dram[4 * i:4 * i + 4].rearrange("o p a k c -> p o a k c")).then_inc(ld_wu[i], 16)
                    store(c, k, g_dram, c * UPC + k)
                    if k == 3 and nxt is not None:
                        sp.wait_ge(wlo_ready, at(c + 4))
                        sp.dma_start(V_RAW, nxt).then_inc(ld_v, 16)
                    for s in range(3):
                        if V_AT[s] // 2 == k:
                            sp.wait_ge(wt_ready, at((c + 4) * 3 + s))
                            sp.dma_start(parts[s], V_T[:, s]).then_inc(st_v[s], 16)

            def up_parts(c):
                return [wu_dram[c * 3 + s] for s in range(3)]

            def down_parts(c):
                return [wd_dram[s, c - 4] for s in range(3)]

            with sp.Fori(0, 3) as c:
                gate_chunk(c, up_parts(c), up_src[c + 1])
            gate_chunk(3, up_parts(3), down_src[0])
            with sp.Fori(4, CHUNKS - 1) as c:
                gate_chunk(c, down_parts(c), down_src[c - 3])
            sp.wait_ge(x_trans, at(TILES - 1))
            for s in range(3):
                sp.wait_ge(st_stg[s], 3 * 16)
            for k in range(3):
                sp.dma_start(GB[:, k, :], g_dram[k]).then_inc(ld_gb[k], 16)
            for s in range(3):
                sp.wait_ge(st_v[s], (CHUNKS // 2 + 1) * 16)
            gate_chunk(CHUNKS - 1, down_parts(CHUNKS - 1), None, last=True)
            sp.dma_start(GB[:, 3, :], g_dram[3]).then_inc(ld_gb[3], 16)
            for s in range(3):
                sp.wait_ge(st_stg[s], (UNITS // 3 + 1) * 16)

            def first_half(c, units):
                for k in range(2 * UPC):
                    if k in units:
                        q = c * (2 * UPC) + k + 4
                        sp.wait_ge(sq_ready, at(q - 4))
                        sp.dma_start(GB[:, k % 4, :], g_dram[q]).then_inc(ld_gb[k % 4], 16)
                    if k % 2:
                        store(c + CHUNKS, k // 2, u_dram, c * UPC + k // 2)

            with sp.Fori(0, CHUNKS // 2 - 1) as c:
                first_half(c, range(12))
            first_half(CHUNKS // 2 - 1, range(8))
            with sp.Fori(CHUNKS // 2, CHUNKS - 1) as c:
                for k in range(UPC):
                    store(c + CHUNKS, k, u_dram, c * UPC + k)
            for s in range(3):
                sp.wait_ge(st_stg[s], (UNITS // 3 + 5) * 16)

            def load_up(q, k):
                sp.dma_start(UR[:, k, :], u_dram[q]).then_inc(ld_ur[k], 16)

            for k in (3, 4, 5):
                load_up(UPC + k, k)
            for k in range(UPC):
                sp.wait_ge(stg_ready, at((2 * CHUNKS - 1) * OT + 2 * k + 1))
                sp.dma_start(u_dram[UNITS - UPC + k], LU[:, k, :]).then_inc(st_lu, 16)
            sp.wait_ge(sq2_ready, at(UNITS - 1))
            for k in range(3):
                load_up(UPC + k, k)
            sp.wait_ge(mm_ready, at(2 * CHUNKS * OT - 1))
            sp.wait_ge(up_peaked, at(2 * UNITS - 1))
            for s in range(3):
                sp.wait_ge(st_stg[s], (4 * CHUNKS - 1) * 16)
            for s in range(3):
                sp.dma_start(WD[:, s], wd_dram[s].rearrange("j p a k c -> p j a k c")).then_inc(ld_wd, 16)
            with sp.Fori(1, CHUNKS - 2) as i:
                for k in range(UPC):
                    sp.wait_ge(p_peaked, at(i * UPC + k))
                    load_up((i + 1) * UPC + k, k)
            for k in range(UPC):
                sp.wait_ge(p_peaked, at((CHUNKS - 2) * UPC + k))
                load_up(k, k)
            sp.wait_ge(st_lu, 16 * UPC)
            sp.wait_ge(st_h, 16 * CHUNKS)
            sp.wait_ge(ui_ready, at(UPC - 1))
            for par in range(2):
                sp.dma_start(HB[:, par], h_dram[par]).then_inc(ld_hb[par], 16)

            def up_units(c):
                for k in range(UPC):
                    sp.wait_ge(ui_ready, at(c * UPC + k - 3))
                    sp.dma_start(UB[:, k % 3, :], u_dram[c * UPC + k]).then_inc(ld_ub[k % 3], 16)

            def out_chunk(j, par, more):
                sp.wait_ge(y_ready, at((j * 2 + par) * TPC + TPC - 1))
                sp.dma_start(out_dst[j * 2 + par], HB[:, par]).then_inc(st_out[par], 16)
                if more:
                    sp.wait_ge(st_out[par], (j + 2) * 16)
                    sp.dma_start(HB[:, par], h_dram[j * 2 + par + 2]).then_inc(ld_hb[par], 16)

            with sp.Fori(0, CHUNKS // 2 - 1) as j:
                up_units(j * 2 + 1)
                out_chunk(j, 0, True)
                up_units(j * 2 + 2)
                out_chunk(j, 1, True)
            up_units(CHUNKS - 1)
            out_chunk(CHUNKS // 2 - 1, 0, False)
            for tt in range(TPC):
                sp.wait_ge(y_ready, at(TILES - TPC + tt))
                sp.dma_start(out_dst[CHUNKS - 1][:, tt], HB[:, 1, tt]).then_inc(st_out[1], 16)
            sp.wait_ge(st_out[0], (CHUNKS // 2 + 1) * 16)
            sp.wait_ge(st_out[1], (CHUNKS // 2 + TPC) * 16)


N_CTX = 8
M_GROUPS = 6


def _numbered(names):
    return {name: i + 1 for i, name in enumerate(names)}


PS = _numbered(["cxt0", "kv0", "cxt1", "kv1", "kt0", "kt1"] + [f"vw{b}{n}" for b in range(BATCH) for n in range(NH)])
AS = _numbered(["tanh", "root_c", "kvw", "cxt0", "qw", "knvt0", "cxt1", "qsum", "knvt1", "qws", "qwh", "kt0", "kt1"]
               + [f"vw{b}{n}" for b in range(BATCH) for n in range(NH)]
               + ["vsum0", "vsum1", "vws0", "vwh0", "vws1", "vwh1", "root_x0", "root_x1",
                  "root_var_h", "top_i", "top_sig"])
PK = _numbered(["qw", "w_gate", "vw", "w_up_down", "x", "gate", "product", "up", "output"])
CTX_KB, CTX_VB = (2, 6), (3, 7)
VWB = ((0, 1, 2, 3), (6, 7, 0, 1))
FIRST_XB = (5, 6)
X_FIRST = 12
V_AT = (9, 10, 11)
ROW_AHEAD, HEAD_AHEAD = 9, 5
XN_SCALE = 1024.0
PROB_SCALE = 4096.0
DVE_ABS, ACT_ABS = (2, 5), (0, 1, 3, 4)


def peak_chunk(i):
    return {0: CHUNKS - 1, CHUNKS - 1: 0}[i] if isinstance(i, int) and i in (0, CHUNKS - 1) else i


ACT_EVENTS = {"w_summed", "whi_ready", "wt_ready", "xn_ready", "xtc_hi", "exp_ready", "pt_hi", "xt_ready", "stg_ready", "gi_ready",
              "sig_ready", "sig2_ready", "ua_ready", "ga_ready", "ui_ready"}
PE_EVENTS = {"w_transposed", "xn_transposed", "q_ready", "scores_ready", "probs_transposed", "attn_ready",
             "x_transposed", "mm_ready", "down_ready"}
DVE_EVENTS = {"wb_ready", "wq_ready", "ws_ready", "wlo_ready", "xtc_lo", "pt_lo", "roped", "masked", "max_ready", "inv_ready",
              "probs_ready", "h_ready", "h_stats", "xi_ready", "xh_ready", "xl_ready", "stg_peaked", "up_peaked",
              "sq_ready", "gg_peaked", "gg_folded", "sq2_ready", "gg_ready", "ga2_ready", "p_peaked",
              "oi_ready", "oh_ready", "ol_ready", "y_ready"}

_INS = ["x", "ctx_1024", "mask_BxS2_bk0", "g_xattn", "g_ffn", "L0_xattn_rms_scale", "L0_xattn_q_w", "L0_xattn_kv_w",
        "L0_xattn_out_w", "L0_ffn_w_gate", "L0_ffn_w_up", "L0_ffn_w_down"]


def _rope_tables():
    import numpy as np
    half = HD // 2
    exponent = np.float32(2.0 / HD) * np.arange(half, dtype=np.float32)
    timescale = np.power(np.float32(10000.0), exponent).astype(np.float32)

    def table(first, count):
        radians = np.arange(first, first + count, dtype=np.float32)[:, None] / timescale
        r = radians.astype(np.float64)
        return np.cos(r), np.sin(r)

    c, s = table(CTX, SEQ)
    q = np.stack([np.concatenate([c, c], 1), np.concatenate([s, s], 1)], 0) * HD ** -0.5
    q = q.reshape(2, SEQ // CHUNK, CHUNK, HD).transpose(1, 3, 0, 2)
    q = np.concatenate([q] * BATCH, 0)
    c, s = table(0, CTX)
    return np.ascontiguousarray(q, np.float32), np.ascontiguousarray(np.stack([c, s], 1), np.float32)


def kernel(**inputs):
    import numpy as np
    import concourse.bacc as bacc
    from concourse.bass_utils import run_bass_kernel_spmd

    nc = bacc.Bacc("TRN2", target_bir_lowering=False, num_devices=1)
    arrays, args = {}, []
    rope_q, rope_k = _rope_tables()
    given = [(n, np.ascontiguousarray(inputs[n])) for n in _INS] + [("rope_q", rope_q), ("rope_k", rope_k)]
    for name, a in given:
        arrays[f"in_{name}"] = a
        args.append(nc.dram_tensor(f"in_{name}", a.shape, mybir.dt.from_np(a.dtype), kind="ExternalInput").ap())
    args.append(nc.dram_tensor("out_0", (BATCH, SEQ, D), mybir.dt.float32, kind="ExternalOutput").ap())
    flamingo_kernel(nc, *args)
    r = run_bass_kernel_spmd(nc, [arrays], core_ids=[0])
    return r.results[0]["out_0"]
```
